# Optimizing a Trainium2 kernel written in Bass

```python
import numpy as np
import jax
import jax.numpy as jnp

def _softmax(x, axis=-1):
    return jax.nn.softmax(x, axis=axis)

def _gelu(x):
    return jax.nn.gelu(x, approximate=True)

def _silu(x):
    return jax.nn.silu(x)

def _sigmoid(x):
    return jax.nn.sigmoid(x)

def _layernorm(x, axis=-1, eps=1e-05):
    m = jnp.mean(x, axis=axis, keepdims=True)
    v = jnp.var(x, axis=axis, keepdims=True)
    return (x - m) / jnp.sqrt(v + eps)

def _scatter_add(tgt, idx, src, axis=0):
    return tgt.at[idx].add(src)

def _segment_sum(src, seg, n):
    return jax.ops.segment_sum(src, seg, n)
kernel_name = 'mk_gnn_resnorm_d4_gnn_r32_e3b3e5'

def setup_inputs(seed: int=0):
    np.random.seed(seed)
    _w = jnp.asarray

    def _rec_inputs():
        import jax
        import jax.numpy as jnp
        _gk = jax.random.key(seed)
        x = -0.000202 + 1 * jax.random.normal(jax.random.fold_in(_gk, 1), (3125, 64), jnp.float32)
        _s = jax.random.randint(jax.random.fold_in(_gk, 2), (50000,), 0, 3125, jnp.int32)
        _d = jax.random.randint(jax.random.fold_in(_gk, 3), (50000,), 0, 3125, jnp.int32)
        _loop = jnp.arange(3125, dtype=jnp.int32)
        src = jnp.concatenate([_s, _d, _loop])
        dst = jnp.concatenate([_d, _s, _loop])
        _o = jnp.argsort(dst, stable=True)
        src = src[_o]
        dst = dst[_o]
        edge_type_8 = jax.random.randint(jax.random.fold_in(_gk, 14), (103125,), 0, 8, jnp.int32)
        node_vec1 = jax.random.uniform(jax.random.fold_in(_gk, 15), (3125, 1), jnp.float32, 0.0, 0.999993)
        return (x, src, dst, edge_type_8, node_vec1)
    x, src, dst, edge_type_8, node_vec1 = _rec_inputs()

    def _L0_gnn_setup():
        import jax, jax.numpy as jnp
        import numpy as np
        EPS = 1e-05

        def _bn(x):
            mu = jnp.mean(x, axis=0, keepdims=True)
            var = jnp.var(x, axis=0, keepdims=True)
            return (x - mu) * jax.lax.rsqrt(var + EPS)

        def _conv(x, src, tgt, norm, W):
            n = x.shape[0]
            agg = x + jax.ops.segment_sum(x[src], tgt, num_segments=n)
            return norm * agg @ W

        def _biconv(x, src, tgt, norm, norm_t, W_out, W_back):
            return _conv(x, src, tgt, norm, W_out) + _conv(x, tgt, src, norm_t, W_back)
        key = jax.random.key(seed)
        ks = jax.random.split(key, 9)
        N, E, C = (3125, 1250000, 64)
        x = jax.random.normal(ks[0], (N, C), dtype=jnp.float32)
        sources = jax.random.randint(ks[1], (E,), 0, N)
        targets = jax.random.randint(ks[2], (E,), 0, N)
        norm = jax.random.uniform(ks[3], (N, 1), dtype=jnp.float32)
        norm_t = jax.random.uniform(ks[4], (N, 1), dtype=jnp.float32)
        std = float(np.sqrt(2.0 / (C + C)))
        W1_out = jax.random.normal(ks[5], (C, C), dtype=jnp.float32) * std
        W1_back = jax.random.normal(ks[6], (C, C), dtype=jnp.float32) * std
        W2_out = jax.random.normal(ks[7], (C, C), dtype=jnp.float32) * std
        W2_back = jax.random.normal(ks[8], (C, C), dtype=jnp.float32) * std
        return {'x': x, 'sources': sources, 'targets': targets, 'norm': norm, 'norm_t': norm_t, 'W1_out': W1_out, 'W1_back': W1_back, 'W2_out': W2_out, 'W2_back': W2_back}
    _L0_gnn_all = _L0_gnn_setup()
    _L0_gnn_in = {k: v for k, v in _L0_gnn_all.items() if k in ('W1_out', 'W1_back', 'W2_out', 'W2_back')}
    del _L0_gnn_all

    def _L1_gnn_setup():
        import jax, jax.numpy as jnp
        import numpy as np
        N_NODES = 50000
        N_EDGES = 25000
        D_IN = 64
        D_HID = 128
        D_OUT = 64
        key = jax.random.key(seed)
        k0, k1, k2, k3 = jax.random.split(key, 4)
        x = jax.random.normal(k0, (N_NODES, D_IN), dtype=jnp.float32)
        edge_index = jax.random.randint(k1, (2, N_EDGES), 0, N_NODES, dtype=jnp.int32)
        W1 = jax.random.normal(k2, (2 * D_IN, D_HID), dtype=jnp.float32) * 0.05
        b1 = jnp.zeros((D_HID,), dtype=jnp.float32)
        W2 = jax.random.normal(k3, (D_HID, D_OUT), dtype=jnp.float32) * 0.05
        b2 = jnp.zeros((D_OUT,), dtype=jnp.float32)
        return {'x': x, 'edge_index': edge_index, 'W1': W1, 'b1': b1, 'W2': W2, 'b2': b2}
    _L1_gnn_all = _L1_gnn_setup()
    _L1_gnn_in = {k: v for k, v in _L1_gnn_all.items() if k in ('W1', 'b1', 'W2', 'b2')}
    del _L1_gnn_all

    def _L2_gnn_setup():
        import jax, jax.numpy as jnp
        import numpy as np
        N, E, D, H, C = (50000, 25000, 64, 2, 64)

        def _transformer_conv(x, src, dst, wq, bq, wk, bk, wv, bv, ws, bs):
            n = x.shape[0]
            q = (x @ wq + bq).reshape(n, H, C)
            k = (x @ wk + bk).reshape(n, H, C)
            v = (x @ wv + bv).reshape(n, H, C)
            qi = q[dst]
            kj = k[src]
            vj = v[src]
            alpha = jnp.einsum('ehc,ehc->eh', qi, kj) / jnp.sqrt(jnp.asarray(C, x.dtype))
            amax = jax.ops.segment_max(alpha, dst, num_segments=n)
            amax = jnp.where(jnp.isfinite(amax), amax, 0.0)
            ex = jnp.exp(alpha - amax[dst])
            denom = jax.ops.segment_sum(ex, dst, num_segments=n)
            a = ex / (denom[dst] + 1e-16)
            out = jax.ops.segment_sum(a[:, :, None] * vj, dst, num_segments=n)
            out = out.mean(axis=1)
            return out + x @ ws + bs
        key = jax.random.key(seed)
        ks = jax.random.split(key, 20)
        x = jax.random.normal(ks[0], (N, D), dtype=jnp.float32)
        edge_index = jax.random.randint(ks[1], (2, E), 0, N, dtype=jnp.int64)
        s = 1.0 / np.sqrt(D)

        def lin(k, din, dout):
            return jax.random.uniform(k, (din, dout), jnp.float32, -s, s)
        inp = {'x': x, 'edge_index': edge_index}
        i = 2
        for l, din in ((1, D), (2, C)):
            for nm, dout in (('wq', H * C), ('wk', H * C), ('wv', H * C), ('ws', C)):
                inp[f'l{l}_{nm}'] = lin(ks[i], din, dout)
                i += 1
                inp[f"l{l}_{nm.replace('w', 'b')}"] = jnp.zeros((dout,), jnp.float32)
        return inp
    _L2_gnn_all = _L2_gnn_setup()
    _L2_gnn_in = {k: v for k, v in _L2_gnn_all.items() if k in ('l1_wq', 'l1_bq', 'l1_wk', 'l1_bk', 'l1_wv', 'l1_bv', 'l1_ws', 'l1_bs', 'l2_wq', 'l2_bq', 'l2_wk', 'l2_bk', 'l2_wv', 'l2_bv', 'l2_ws', 'l2_bs')}
    del _L2_gnn_all

    def _L3_gnn_setup():
        import jax, jax.numpy as jnp
        import numpy as np
        N_NODES = 3125
        N_EDGES = 50000
        DIM = 64
        N_REL = 8
        N_LAYERS = 2

        def _rgcn_layer(x, W, W_root, b, src, dst, edge_type, num_nodes, num_rel):
            h = jnp.einsum('nd,rdf->rnf', x, W)
            msg = h[edge_type, src]
            comb = dst * num_rel + edge_type
            cnt = jax.ops.segment_sum(jnp.ones(src.shape, dtype=x.dtype), comb, num_segments=num_nodes * num_rel)
            norm = 1.0 / jnp.clip(cnt[comb], 1.0)
            agg = jax.ops.segment_sum(msg * norm[:, None], dst, num_segments=num_nodes)
            return agg + x @ W_root + b
        key = jax.random.key(seed)
        ks = jax.random.split(key, 6)
        x = jax.random.normal(ks[0], (N_NODES, DIM), dtype=jnp.float32)
        weight = jax.random.normal(ks[1], (N_LAYERS, N_REL, DIM, DIM), dtype=jnp.float32) * (1.0 / np.sqrt(DIM))
        root = jax.random.normal(ks[2], (N_LAYERS, DIM, DIM), dtype=jnp.float32) * (1.0 / np.sqrt(DIM))
        bias = jnp.zeros((N_LAYERS, DIM), dtype=jnp.float32)
        edge_index = jax.random.randint(ks[3], (2, N_EDGES), 0, N_NODES, dtype=jnp.int32)
        edge_type = jax.random.randint(ks[4], (N_EDGES,), 0, N_REL, dtype=jnp.int32)
        return {'x': x, 'weight': weight, 'root': root, 'bias': bias, 'edge_index': edge_index, 'edge_type': edge_type}
    _L3_gnn_all = _L3_gnn_setup()
    _L3_gnn_in = {k: v for k, v in _L3_gnn_all.items() if k in ('weight', 'root', 'bias')}
    del _L3_gnn_all
    return {'x': x, 'src': src, 'dst': dst, 'edge_type_8': edge_type_8, 'node_vec1': node_vec1, 'L0_gnn_W1_out': _L0_gnn_in['W1_out'], 'L0_gnn_W1_back': _L0_gnn_in['W1_back'], 'L0_gnn_W2_out': _L0_gnn_in['W2_out'], 'L0_gnn_W2_back': _L0_gnn_in['W2_back'], 'L1_gnn_W1': _L1_gnn_in['W1'], 'L1_gnn_b1': _L1_gnn_in['b1'], 'L1_gnn_W2': _L1_gnn_in['W2'], 'L1_gnn_b2': _L1_gnn_in['b2'], 'L2_gnn_l1_wq': _L2_gnn_in['l1_wq'], 'L2_gnn_l1_bq': _L2_gnn_in['l1_bq'], 'L2_gnn_l1_wk': _L2_gnn_in['l1_wk'], 'L2_gnn_l1_bk': _L2_gnn_in['l1_bk'], 'L2_gnn_l1_wv': _L2_gnn_in['l1_wv'], 'L2_gnn_l1_bv': _L2_gnn_in['l1_bv'], 'L2_gnn_l1_ws': _L2_gnn_in['l1_ws'], 'L2_gnn_l1_bs': _L2_gnn_in['l1_bs'], 'L2_gnn_l2_wq': _L2_gnn_in['l2_wq'], 'L2_gnn_l2_bq': _L2_gnn_in['l2_bq'], 'L2_gnn_l2_wk': _L2_gnn_in['l2_wk'], 'L2_gnn_l2_bk': _L2_gnn_in['l2_bk'], 'L2_gnn_l2_wv': _L2_gnn_in['l2_wv'], 'L2_gnn_l2_bv': _L2_gnn_in['l2_bv'], 'L2_gnn_l2_ws': _L2_gnn_in['l2_ws'], 'L2_gnn_l2_bs': _L2_gnn_in['l2_bs'], 'L3_gnn_weight': _L3_gnn_in['weight'], 'L3_gnn_root': _L3_gnn_in['root'], 'L3_gnn_bias': _L3_gnn_in['bias']}

def reference(x, src, dst, edge_type_8, node_vec1, L0_gnn_W1_out, L0_gnn_W1_back, L0_gnn_W2_out, L0_gnn_W2_back, L1_gnn_W1, L1_gnn_b1, L1_gnn_W2, L1_gnn_b2, L2_gnn_l1_wq, L2_gnn_l1_bq, L2_gnn_l1_wk, L2_gnn_l1_bk, L2_gnn_l1_wv, L2_gnn_l1_bv, L2_gnn_l1_ws, L2_gnn_l1_bs, L2_gnn_l2_wq, L2_gnn_l2_bq, L2_gnn_l2_wk, L2_gnn_l2_bk, L2_gnn_l2_wv, L2_gnn_l2_bv, L2_gnn_l2_ws, L2_gnn_l2_bs, L3_gnn_weight, L3_gnn_root, L3_gnn_bias):
    import jax
    import jax.numpy as jnp

    def _L0_gnn_ref(x, sources, targets, norm, norm_t, W1_out, W1_back, W2_out, W2_back):
        import jax, jax.numpy as jnp
        import numpy as np
        EPS = 1e-05

        def _bn(x):
            mu = jnp.mean(x, axis=0, keepdims=True)
            var = jnp.var(x, axis=0, keepdims=True)
            return (x - mu) * jax.lax.rsqrt(var + EPS)

        def _conv(x, src, tgt, norm, W):
            n = x.shape[0]
            agg = x + jax.ops.segment_sum(x[src], tgt, num_segments=n)
            return norm * agg @ W

        def _biconv(x, src, tgt, norm, norm_t, W_out, W_back):
            return _conv(x, src, tgt, norm, W_out) + _conv(x, tgt, src, norm_t, W_back)
        save = x
        h = _bn(jax.nn.relu(x))
        h = _biconv(h, sources, targets, norm, norm_t, W1_out, W1_back)
        h = _bn(jax.nn.relu(h))
        h = _biconv(h, sources, targets, norm, norm_t, W2_out, W2_back)
        return save + h

    def _L1_gnn_ref(x, edge_index, W1, b1, W2, b2):
        import jax, jax.numpy as jnp
        import numpy as np
        N_NODES = 50000
        N_EDGES = 25000
        D_IN = 64
        D_HID = 128
        D_OUT = 64
        row, col = (edge_index[0], edge_index[1])
        x_row = x[row]
        x_col = x[col]
        h = jnp.concatenate([x_row, x_col - x_row], axis=1)
        h = jax.nn.relu(h @ W1 + b1)
        h = h @ W2 + b2
        out = jax.ops.segment_max(h, row, num_segments=x.shape[0])
        out = jnp.where(jnp.isfinite(out), out, jnp.zeros_like(out))
        return out

    def _L2_gnn_ref(x, edge_index, l1_wq, l1_bq, l1_wk, l1_bk, l1_wv, l1_bv, l1_ws, l1_bs, l2_wq, l2_bq, l2_wk, l2_bk, l2_wv, l2_bv, l2_ws, l2_bs):
        import jax, jax.numpy as jnp
        import numpy as np
        N, E, D, H, C = (50000, 25000, 64, 2, 64)

        def _transformer_conv(x, src, dst, wq, bq, wk, bk, wv, bv, ws, bs):
            n = x.shape[0]
            q = (x @ wq + bq).reshape(n, H, C)
            k = (x @ wk + bk).reshape(n, H, C)
            v = (x @ wv + bv).reshape(n, H, C)
            qi = q[dst]
            kj = k[src]
            vj = v[src]
            alpha = jnp.einsum('ehc,ehc->eh', qi, kj) / jnp.sqrt(jnp.asarray(C, x.dtype))
            amax = jax.ops.segment_max(alpha, dst, num_segments=n)
            amax = jnp.where(jnp.isfinite(amax), amax, 0.0)
            ex = jnp.exp(alpha - amax[dst])
            denom = jax.ops.segment_sum(ex, dst, num_segments=n)
            a = ex / (denom[dst] + 1e-16)
            out = jax.ops.segment_sum(a[:, :, None] * vj, dst, num_segments=n)
            out = out.mean(axis=1)
            return out + x @ ws + bs
        src, dst = (edge_index[0], edge_index[1])
        h = _transformer_conv(x, src, dst, l1_wq, l1_bq, l1_wk, l1_bk, l1_wv, l1_bv, l1_ws, l1_bs)
        h = _transformer_conv(h, src, dst, l2_wq, l2_bq, l2_wk, l2_bk, l2_wv, l2_bv, l2_ws, l2_bs)
        return h

    def _L3_gnn_ref(x, weight, root, bias, edge_index, edge_type):
        import jax, jax.numpy as jnp
        import numpy as np
        N_NODES = 3125
        N_EDGES = 50000
        DIM = 64
        N_REL = 8
        N_LAYERS = 2

        def _rgcn_layer(x, W, W_root, b, src, dst, edge_type, num_nodes, num_rel):
            h = jnp.einsum('nd,rdf->rnf', x, W)
            msg = h[edge_type, src]
            comb = dst * num_rel + edge_type
            cnt = jax.ops.segment_sum(jnp.ones(src.shape, dtype=x.dtype), comb, num_segments=num_nodes * num_rel)
            norm = 1.0 / jnp.clip(cnt[comb], 1.0)
            agg = jax.ops.segment_sum(msg * norm[:, None], dst, num_segments=num_nodes)
            return agg + x @ W_root + b
        src, dst = (edge_index[0], edge_index[1])
        num_nodes = x.shape[0]
        num_rel = weight.shape[1]
        for l in range(weight.shape[0]):
            x = _rgcn_layer(x, weight[l], root[l], bias[l], src, dst, edge_type, num_nodes, num_rel)
        return x
    edge_index = jnp.stack([src, dst])
    deg = jnp.maximum(jax.ops.segment_sum(jnp.ones(dst.shape, jnp.float32), dst, num_segments=3125), 1.0)
    deg_isqrt = deg ** (-0.5)
    x = _layernorm(x + _L0_gnn_ref(x, src, dst, deg_isqrt[:, None], node_vec1, L0_gnn_W1_out, L0_gnn_W1_back, L0_gnn_W2_out, L0_gnn_W2_back), axis=-1)
    x = _layernorm(x + _L1_gnn_ref(x, edge_index, L1_gnn_W1, L1_gnn_b1, L1_gnn_W2, L1_gnn_b2), axis=-1)
    x = _layernorm(x + _L2_gnn_ref(x, edge_index, L2_gnn_l1_wq, L2_gnn_l1_bq, L2_gnn_l1_wk, L2_gnn_l1_bk, L2_gnn_l1_wv, L2_gnn_l1_bv, L2_gnn_l1_ws, L2_gnn_l1_bs, L2_gnn_l2_wq, L2_gnn_l2_bq, L2_gnn_l2_wk, L2_gnn_l2_bk, L2_gnn_l2_wv, L2_gnn_l2_bv, L2_gnn_l2_ws, L2_gnn_l2_bs), axis=-1)
    x = _layernorm(x + _L3_gnn_ref(x, L3_gnn_weight, L3_gnn_root, L3_gnn_bias, edge_index, edge_type_8), axis=-1)
    return x

_drawn_inputs = setup_inputs


def setup_inputs(seed=0):
    import zlib

    import numpy as np

    out = dict(_drawn_inputs(seed))
    spreads = {'L1_gnn_b1': (0.0, 0.1),
     'L1_gnn_b2': (0.0, 0.1),
     'L2_gnn_l1_bq': (0.0, 0.8),
     'L2_gnn_l1_bk': (0.0, 0.8),
     'L2_gnn_l1_bv': (0.0, 0.1),
     'L2_gnn_l1_bs': (0.0, 0.1),
     'L2_gnn_l2_bq': (0.0, 0.8),
     'L2_gnn_l2_bk': (0.0, 0.8),
     'L2_gnn_l2_bv': (0.0, 0.1),
     'L2_gnn_l2_bs': (0.0, 0.1),
     'L3_gnn_bias': (0.0, 0.1)}
    factors = {'L2_gnn_l1_wq': 3.784, 'L2_gnn_l1_wk': 3.536, 'L2_gnn_l2_wq': 8.0, 'L2_gnn_l2_wk': 7.583}
    for name, (base, spread) in spreads.items():
        noise = np.random.default_rng([zlib.crc32(name.encode()), seed]).standard_normal(out[name].shape)
        drawn = base * np.exp(spread * noise) if base else spread * noise
        out[name] = jnp.asarray(drawn.astype(out[name].dtype))
    for name, factor in factors.items():
        out[name] = (out[name] * factor).astype(out[name].dtype)
    return out
```

```python
import concourse.bass as bass
from concourse import mybir
from concourse.alu_op_type import AluOpType as ALU
from contextlib import ExitStack

F32 = mybir.dt.float32
I32 = mybir.dt.int32
I16 = mybir.dt.int16
F16 = mybir.dt.float16
BF16 = mybir.dt.bfloat16
ACT = mybir.ActivationFunctionType
AX = mybir.AxisListType
ds = bass.ds

P = 128
N = 3125
E = 103125
D = 64
NREL = 8
W = -(-N // P)
NP = W * P
TAIL = N - (W - 1) * P
T = -(-E // P)
CH = -(-T // P)
NT = CH * P
FULL_T = E // P
LAST_T = E - FULL_T * P
G = 4
NO_NODE = 4000.0
CUT = 512
SLICES = [(c, min(CUT, NP - c)) for c in range(0, NP, CUT)]
EPS = 1e-5
NEG = -1e30


class Own:

    def __init__(self, eng, sem):
        self.eng, self.sem, self.base, self.n = eng, sem, 0, 0

    def at(self, base):
        self.base, self.n = base, 0

    def did(self, ins):
        ins.then_inc(self.sem, 1)
        self.n += 1

    def wait(self):
        self.eng.wait_ge(self.sem, self.base + self.n)

    def do(self, ins):
        self.did(ins)
        self.wait()


def wait_alone(eng, sem, value, passed):
    eng.wait_ge(sem, value)
    eng.sem_inc(passed, 1)


class Kept:

    def __init__(self, nc):
        self.nc, self.sems = nc, []

    def sem(self, name):
        self.sems.append(self.nc.alloc_semaphore(name))
        return self.sems[-1]

    def clear_semaphores(self):
        self.nc.all_engine_barrier()
        self.nc.clear_and_free_semaphores(self.sems)
        self.nc.all_engine_barrier()
        self.sems = []


def allocate(nc, ctx):
    k = Kept(nc)

    def sb(name, shape, dt):
        return ctx.enter_context(nc.sbuf_tensor(name, shape, dt))

    k.ident = sb("ident", [P, P], F32)
    k.identb = sb("identb", [P, P], BF16)
    k.iota_p = sb("iota_p", [P, P], F32)
    k.wbase = sb("wbase", [P, W], F32)
    k.src_t = sb("src_t", [P, NT], F32)
    k.dst_t = sb("dst_t", [P, NT], F32)
    k.msg_row = sb("msg_row", [P, NT], I32)
    k.type_hot = sb("type_hot", [P, NT, NREL], BF16)
    k.x = sb("x", [P, W, D], F32)
    k.vec = sb("vec", [P, W], F32)
    k.cnt8 = sb("cnt8", [P, W, NREL], F32)
    k.xt = sb("xt", [D + 1, NP], F32)
    k.z = sb("z", [P, W, D], F32)
    k.uniq = sb("uniq", [P, W], F32)
    k.table = nc.dram_tensor("window_table", [W, 4], I32).ap()
    k.rounds = nc.dram_tensor("neighbour_rounds", [1, 1], I32).ap()
    k.at = nc.dram_tensor("count_rows", [W, P, NP], BF16).ap()
    k.a = nc.dram_tensor("count_panels", [W, P, W, P], BF16).ap()
    k.q = nc.dram_tensor("edge_q", [NP, 2 * D], F32).ap()
    k.h = nc.dram_tensor("rel_h", [NREL * NP, D], F32).ap()
    return k


def allocate_convolution(nc, ctx, k):
    sb = lambda n, s, d: ctx.enter_context(nc.sbuf_tensor(n, s, d))
    k.y = sb("y", [P, W, 2, D], F32)
    k.agg = sb("agg", [P, W, 2, D], F32)
    k.parts = sb("parts", [P, W, 2, 3, D], BF16)


def allocate_edges(nc, ctx, k):
    sb = lambda n, s, d: ctx.enter_context(nc.sbuf_tensor(n, s, d))
    k.p = sb("p", [P, W, 2 * D], F32)


def allocate_attention(nc, ctx, k):
    sb = lambda n, s, d: ctx.enter_context(nc.sbuf_tensor(n, s, d))
    k.qa = sb("qa", [D, 2, NP], F32)
    k.ka = sb("ka", [D + 1, 2, NP], F32)
    k.va = sb("va", [P, W, 2, D + 1], F32)


def prepare(nc, k, x, src, dst, edge_type, node_vec1):
    with ExitStack() as ctx:
        sb = lambda n, s, d: ctx.enter_context(nc.sbuf_tensor(n, s, d))
        sem = lambda n: k.sem(n)
        raw = [sb(f"raw{j}", [P, CH, P], I32) for j in range(3)]
        rawf = [sb(f"rawf{j}", [P, CH, P], F32) for j in range(3)]
        tri = sb("tri", [W, W], F32)
        idt = sb("idt", [W, NT], F32)
        t_min = sb("t_min", [P, CH], F32)
        t_max = sb("t_max", [P, CH], F32)
        hit = sb("hit", [W, NT], F32)
        hit2 = sb("hit2", [W, NT], F32)
        wlo = sb("wlo", [W, 1], F32)
        whi = sb("whi", [W, 1], F32)
        bound = sb("bound", [W, 4], F32)
        back = sb("back", [W, 1], F32)
        ni = sb("ni", [W, 1], I32)
        nf = sb("nf", [W, 1], F32)
        row = sb("row", [W, 4], I32)
        typ = sb("typ", [P, NT], F32)
        rowf = sb("rowf", [P, NT], F32)
        tp = [ctx.enter_context(nc.psum_tensor(f"tp{j}", [P, 2 * CUT], F32)) for j in range(3)]
        bc = ctx.enter_context(nc.psum_tensor("bc", [W, CUT], F32))
        blank, loaded, consts, floats, turned, kept = map(
            sem, ("blank", "loaded", "consts", "floats", "turned", "kept"))
        own_v, mins, spread, taken, nits, before, tabled, stored = map(
            sem, ("prep_own", "mins", "spread", "taken", "nits", "before", "tabled", "stored"))
        pads, own_p = sem("pads"), sem("prep_own_p")
        block = ctx.enter_context(nc.Block())
        head = (CH - 1) * P * P
        full = FULL_T - (CH - 1) * P
        arrays = (src, dst, edge_type)

        @block.sync
        def _(sp):
            sp.wait_ge(blank, 5)
            for j, a in enumerate(arrays):
                sp.dma_start(raw[j][:, 0:CH - 1, :],
                             a[0:head].rearrange("(c p j) -> p c j", p=P, j=P)).then_inc(loaded, 16)
                sp.dma_start(raw[j][0:full, CH - 1, :],
                             a[head:head + full * P].rearrange("(p j) -> p j", j=P)).then_inc(loaded, 16)
                sp.dma_start(raw[j][full:full + 1, CH - 1, 0:LAST_T],
                             a[FULL_T * P:E].rearrange("(p j) -> p j", p=1)).then_inc(loaded, 16)
            sp.dma_start(k.x[:, 0:W - 1, :],
                         x[0:(W - 1) * P, :].rearrange("(w p) d -> p w d", p=P)).then_inc(loaded, 16)
            sp.dma_start(k.x[0:TAIL, W - 1, :], x[(W - 1) * P:N, :]).then_inc(loaded, 16)
            sp.dma_start(k.vec[:, 0:W - 1],
                         node_vec1[0:(W - 1) * P, :].rearrange("(w p) a -> p (w a)", p=P),
                         allow_slow_non_contiguous=True).then_inc(loaded, 16)
            sp.dma_start(k.vec[0:TAIL, W - 1:W], node_vec1[(W - 1) * P:N, :]).then_inc(loaded, 16)
            sp.wait_ge(tabled, 1)
            sp.dma_start(k.table[:, :], row[:, :]).then_inc(stored, 16)
            sp.wait_ge(stored, 16)

        @block.gpsimd
        def _(pool):
            own = Own(pool, own_p)
            pool.memset(raw[0][:, CH - 1, :], 0).then_inc(blank, 1)
            pool.memset(raw[1][:, CH - 1, :], int(NO_NODE)).then_inc(blank, 1)
            pool.memset(raw[2][:, CH - 1, :], 0).then_inc(blank, 1)
            pool.memset(k.x[:, W - 1, :], 0.0).then_inc(blank, 1)
            pool.memset(k.vec[:, W - 1:W], 0.0).then_inc(blank, 1)
            own.did(pool.memset(k.ident[:, :], 0.0))
            own.did(pool.memset(k.identb[:, :], 0.0))
            own.did(pool.memset(tri[:, :], 1.0))
            own.wait()
            for m in (k.ident, k.identb):
                pool.affine_select(out=m[:, :], in_=m[:, :], compare_op=ALU.not_equal, fill=1.0, base=0,
                                   pattern=[[-1, P]], channel_multiplier=1).then_inc(consts, 1)
            pool.affine_select(out=tri[:, :], in_=tri[:, :], compare_op=ALU.is_gt, fill=0.0, base=0,
                               pattern=[[1, W]], channel_multiplier=-1).then_inc(consts, 1)
            pool.iota(k.iota_p[:, :], pattern=[[1, P]], base=0, channel_multiplier=0,
                      allow_small_or_imprecise_dtypes=True).then_inc(consts, 1)
            pool.iota(k.wbase[:, :], pattern=[[P, W]], base=0, channel_multiplier=0,
                      allow_small_or_imprecise_dtypes=True).then_inc(consts, 1)
            pool.iota(wlo[:, :], pattern=[[0, 1]], base=0, channel_multiplier=P,
                      allow_small_or_imprecise_dtypes=True).then_inc(consts, 1)
            pool.iota(whi[:, :], pattern=[[0, 1]], base=P - 1, channel_multiplier=P,
                      allow_small_or_imprecise_dtypes=True).then_inc(consts, 1)
            pool.iota(idt[:, :], pattern=[[1, NT]], base=0, channel_multiplier=0,
                      allow_small_or_imprecise_dtypes=True).then_inc(consts, 1)

        @block.vector
        def _(v):
            own = Own(v, own_v)
            v.wait_ge(loaded, 16 * 13)
            for j in range(3):
                v.tensor_copy(rawf[j][:, :, :], raw[j][:, :, :]).then_inc(floats, 1)
            v.wait_ge(floats, 2)
            v.tensor_reduce(t_min[:, :], rawf[1][:, :, :], AX.X, ALU.min).then_inc(mins, 1)
            v.tensor_reduce(t_max[:, :], rawf[1][:, :, :], AX.X, ALU.max).then_inc(mins, 1)
            for j, out in enumerate((k.src_t, k.dst_t, typ)):
                v.wait_ge(turned, j + 1)
                v.tensor_copy(out[:, :], tp[j][:, 0:NT]).then_inc(kept, 1)
            v.wait_ge(kept, 3)
            own.do(v.scalar_tensor_tensor(rowf[:, :], typ[:, :], float(NP), k.src_t[:, :], ALU.mult, ALU.add))
            own.did(v.tensor_copy(k.msg_row[:, :], rowf[:, :]))
            for r in range(NREL):
                own.did(v.tensor_scalar(k.type_hot[:, :, r], typ[:, :], float(r), None, ALU.is_equal))
            v.wait_ge(consts, 8)
            for c in range(2):
                cols = slice(c * CUT, min((c + 1) * CUT, NT))
                wd = cols.stop - cols.start
                v.wait_ge(spread, 1 + c)
                own.do(v.tensor_scalar(hit[:, cols], bc[:, 0:wd], whi[:, 0:1], None, ALU.is_le))
                v.sem_inc(taken, 1)
            for c in range(2):
                cols = slice(c * CUT, min((c + 1) * CUT, NT))
                wd = cols.stop - cols.start
                v.wait_ge(spread, 3 + c)
                own.do(v.tensor_scalar(hit2[:, cols], bc[:, 0:wd], wlo[:, 0:1], None, ALU.is_ge))
                v.sem_inc(taken, 1)
            own.do(v.tensor_tensor(hit[:, :], hit[:, :], hit2[:, :], ALU.mult))
            own.do(v.scalar_tensor_tensor(hit2[:, :], idt[:, :], 1.0, hit[:, :], ALU.add, ALU.mult))
            own.did(v.tensor_reduce(bound[:, 1:2], hit2[:, :], AX.X, ALU.max))
            own.do(v.scalar_tensor_tensor(hit[:, :], idt[:, :], -float(NT), hit[:, :], ALU.add, ALU.mult))
            own.do(v.tensor_reduce(bound[:, 0:1], hit[:, :], AX.X, ALU.min))
            own.do(v.tensor_scalar(bound[:, 0:1], bound[:, 0:1], float(NT), None, ALU.add))
            own.do(v.tensor_tensor(bound[:, 0:1], bound[:, 0:1], bound[:, 1:2], ALU.min))
            own.do(v.tensor_tensor(bound[:, 2:3], bound[:, 1:2], bound[:, 0:1], ALU.subtract))
            own.do(v.tensor_scalar(bound[:, 2:3], bound[:, 2:3], float(G - 1), float(3 * G - 1), ALU.add, ALU.max))
            own.do(v.tensor_copy(ni[:, :], bound[:, 2:3]))
            own.do(v.tensor_scalar(ni[:, :], ni[:, :], G.bit_length() - 1, None, ALU.arith_shift_right))
            own.do(v.tensor_copy(nf[:, :], ni[:, :]))
            v.sem_inc(nits, 1)
            own.did(v.tensor_copy(row[:, 0:1], bound[:, 0:1]))
            own.did(v.memset(row[:, 3:4], 0))
            own.do(v.tensor_scalar(back[:, :], bound[:, 0:1], -float(NT), None, ALU.add))
            own.did(v.scalar_tensor_tensor(row[:, 1:2], nf[:, :], float(G), bound[:, 0:1], ALU.mult, ALU.add))
            v.wait_ge(before, 1)
            own.do(v.scalar_tensor_tensor(row[:, 2:3], bc[:, 0:1], float(G), back[:, :],
                                          ALU.mult, ALU.subtract))
            v.sem_inc(tabled, 1)

        @block.tensor
        def _(pe):
            pe.wait_ge(consts, 1)
            for j in range(3):
                pe.wait_ge(floats, j + 1)
                for c in range(CH):
                    last = pe.transpose(tp[j][:, c * P:(c + 1) * P], rawf[j][:, c, :], k.ident[:, :])
                last.then_inc(turned, 1)
            pe.wait_ge(mins, 2)
            n = 0
            for t in (t_min, t_max):
                for cs in (range(0, 4), range(4, CH)):
                    if n:
                        pe.wait_ge(taken, n)
                    for c in cs:
                        o = (c - cs.start) * P
                        last = pe.matmul(bc[:, o:o + P], t[:, c:c + 1].broadcast_to([P, W]), k.ident[:, :],
                                         start=True, stop=True)
                    last.then_inc(spread, 1)
                    n += 1
            pe.wait_ge(nits, 1)
            pe.wait_ge(consts, 8)
            pe.matmul(bc[:, 0:1], tri[:, :], nf[:, 0:1], start=True, stop=True).then_inc(before, 1)


def window_tiles(eng, k, w):
    first = eng.value_load(k.table[ds(w, 1), 0:1], min_val=0, max_val=T)
    end = eng.value_load(k.table[ds(w, 1), 1:2], min_val=2 * G, max_val=T + 2 * G)
    place = eng.value_load(k.table[ds(w, 1), 2:3], min_val=NT - T, max_val=NT + W * (T + 2 * G))
    return first, end, place


def count_edges(nc, k):
    with ExitStack() as ctx:
        sb = lambda n, s, d: ctx.enter_context(nc.sbuf_tensor(n, s, d))
        sem = lambda n: k.sem(n)
        iota_s = sb("iota_s", [P, NP], F16)
        srcm = sb("srcm", [P, NT], F32)
        hot_s = sb("hot_s", [P, G, NP], BF16)
        hot_d = sb("hot_d", [P, G, P], BF16)
        rows = sb("rows", [P, 2, NP], BF16)
        ps = ctx.enter_context(nc.psum_tensor("ps_count", [P, 8 * CUT], F32))
        passed = sem("passed")
        iota_ok, own_v, hots, used, copied, stored = map(
            sem, ("iota_ok", "cnt_own", "hots", "used", "copied", "cnt_stored"))
        block = ctx.enter_context(nc.Block())
        half = NP // 2


        @block.gpsimd
        def _(pool):
            pool.iota(iota_s[:, :], pattern=[[1, NP]], base=-half, channel_multiplier=0,
                      allow_small_or_imprecise_dtypes=True).then_inc(iota_ok, 1)

        @block.vector
        def _(v):
            own = Own(v, own_v)
            own.did(v.tensor_scalar(srcm[:, :], k.src_t[:, :], -float(half), None, ALU.add))
            own.wait()
            v.sem_inc(iota_ok, 1)
            v.sem_inc(hots, 2 * NT)
            v.wait_ge(iota_ok, 2)
            with v.Fori(0, W) as w:
                first, end, place = window_tiles(v, k, w)
                with v.Fori(first, end, G) as t0:
                    for j in range(G):
                        v.wait_ge(used, t0 + place + (j + 1))
                        t = t0 + j
                        v.tensor_scalar(hot_d[:, j, :], k.iota_p[:, :], k.wbase[:, ds(w, 1)],
                                        k.dst_t[:, ds(t, 1)], ALU.add, ALU.is_equal).then_inc(hots, 1)
                        v.tensor_scalar(hot_s[:, j, :], iota_s[:, :], srcm[:, ds(t, 1)], None,
                                        ALU.is_equal).then_inc(hots, 1)

        @block.tensor
        def _(pe):
            pe.sem_inc(used, NT + G)
            pe.wait_ge(iota_ok, 2)

            def tile(t, j, fresh, seq):
                pe.wait_ge(hots, seq)
                for n, (c, wd) in enumerate(SLICES):
                    pe.matmul(ps[:, c:c + wd], hot_d[:, j, :], hot_s[:, j, c:c + wd], start=fresh,
                              stop=True, skip_group_check=True)
                return pe.matmul(ps[:, NP:NP + NREL], hot_d[:, j, :], k.type_hot[:, ds(t, 1), :], start=False,
                                 stop=True, skip_group_check=True)

            with pe.Fori(0, W) as w:
                first, end, place = window_tiles(pe, k, w)
                pe.wait_ge(copied, w)
                for j in range(G):
                    last = tile(first + j, j, j == 0, (first + place + (j + 1)) * 2)
                    last.then_inc(used, 1)
                with pe.Fori(first + G, end, G) as t0:
                    for j in range(G):
                        tile(t0 + j, j, False, (t0 + place + (j + 1)) * 2).then_inc(used, 1)

        @block.scalar
        def _(act):
            with act.Fori(0, W) as w:
                first, end, place = window_tiles(act, k, w)
                act.wait_ge(used, end + place + G)
                act.wait_ge(stored, w * 16)
                act.activation(rows[:, ds(w % 2, 1), :], ps[:, 0:NP], ACT.Copy)
                act.activation(k.cnt8[:, ds(w, 1), :], ps[:, NP:NP + NREL], ACT.Copy).then_inc(copied, 1)

        @block.sync
        def _(sp):
            sp.sem_inc(stored, 16)
            with sp.Fori(0, W) as w:
                sp.wait_ge(copied, w + 1)
                sp.dma_start(k.at[ds(w, 1), :, :].rearrange("w p n -> p (w n)"),
                             rows[:, ds(w % 2, 1), :].rearrange("p a n -> p (a n)")).then_inc(stored, 16)
                wait_alone(sp, stored, w * 16 + 32, passed)


def turn_nodes(nc, k, source, func, name):
    with ExitStack() as ctx:
        sem = lambda n: k.sem(n)
        ps = ctx.enter_context(nc.psum_tensor(f"{name}_ps", [D, 7 * CUT], F32))
        turned, copied = sem(f"{name}_turned"), sem(f"{name}_copied")
        block = ctx.enter_context(nc.Block())

        @block.tensor
        def _(pe):
            for s, (c, wd) in enumerate(SLICES):
                for j in range(wd // P):
                    w = c // P + j
                    last = pe.transpose(ps[:, w * P:(w + 1) * P], source[:, w, :], k.ident[:, :])
                last.then_inc(turned, 1)

        @block.scalar
        def _(act):
            for s, (c, wd) in enumerate(SLICES):
                act.wait_ge(turned, s + 1)
                act.activation(k.xt[0:D, c:c + wd], ps[:, c:c + wd], func).then_inc(copied, 1)

        @block.vector
        def _(v):
            v.memset(k.xt[D:D + 1, :], 1.0)


def conv_features(nc, k, w_out, w_back, name):
    with ExitStack() as ctx:
        sb = lambda n, s, d: ctx.enter_context(nc.sbuf_tensor(f"{name}_{n}", s, d))
        sem = lambda n: k.sem(f"{name}_{n}")
        wt = sb("wt", [D, 2 * D], F32)
        stats = sb("stats", [D, len(SLICES), 6], F32)
        mv = sb("mv", [D, 2], F32)
        eps = sb("eps", [D, 1], F32)
        std = sb("std", [D, 1], F32)
        scale = sb("scale", [D, 2], F32)
        rest = sb("rest", [P, W * 2 * D], F32)
        ps = ctx.enter_context(nc.psum_tensor(f"{name}_ps", [P, 7 * CUT], F32))
        loaded, own_v, var_ok, std_ok, normed, products, copied = map(
            sem, ("loaded", "own", "var_ok", "std_ok", "normed", "products", "copied"))
        block = ctx.enter_context(nc.Block())

        @block.sync
        def _(sp):
            sp.dma_start(wt[:, 0:D], w_out[:, :]).then_inc(loaded, 16)
            sp.dma_start(wt[:, D:2 * D], w_back[:, :]).then_inc(loaded, 16)

        @block.vector
        def _(v):
            own = Own(v, own_v)
            for s, (c, wd) in enumerate(SLICES):
                own.did(v.bn_stats(stats[:, s, :], k.xt[0:D, c:min(c + wd, N)]))
            own.did(v.memset(eps[:, :], EPS))
            own.wait()
            own.do(v.bn_aggr(mv[:, :], stats[:, :, :].rearrange("p a b -> p (a b)")))
            v.sem_inc(var_ok, 1)
            v.wait_ge(std_ok, 1)
            own.do(v.reciprocal(scale[:, 0:1], std[:, :]))
            own.do(v.scalar_tensor_tensor(scale[:, 1:2], mv[:, 0:1], -1.0, scale[:, 0:1], ALU.mult, ALU.mult))
            v.tensor_scalar(k.xt[0:D, :], k.xt[0:D, :], scale[:, 0:1], scale[:, 1:2],
                            ALU.mult, ALU.add).then_inc(normed, 1)
            v.wait_ge(copied, len(SLICES))
            y = k.y[:, :, :, :].rearrange("p w c d -> p w (c d)")
            left = y
            r = rest[:, :].rearrange("p (w d) -> p w d", w=W)
            for part in range(3):
                for c in range(2):
                    own.did(v.tensor_copy(k.parts[:, :, c, part, :], left[:, :, c * D:(c + 1) * D]))
                own.wait()
                if part < 2:
                    for c in range(2):
                        own.did(v.tensor_tensor(r[:, :, c * D:(c + 1) * D], left[:, :, c * D:(c + 1) * D],
                                                k.parts[:, :, c, part, :], ALU.subtract))
                    own.wait()
                    left = r

        @block.scalar
        def _(act):
            act.wait_ge(var_ok, 1)
            act.activation(std[:, :], mv[:, 1:2], ACT.Sqrt, bias=eps[:, 0:1]).then_inc(std_ok, 1)
            for s, (c, wd) in enumerate(SLICES):
                act.wait_ge(products, s + 1)
                act.activation(k.y[:, c // P:(c + wd) // P, :, :].rearrange("p w c d -> p (w c d)"),
                               ps[:, c:c + wd], ACT.Copy).then_inc(copied, 1)

        @block.tensor
        def _(pe):
            pe.wait_ge(loaded, 32)
            pe.wait_ge(normed, 1)
            for s, (c, wd) in enumerate(SLICES):
                for j in range(wd // P):
                    o = c + j * P
                    last = pe.matmul(ps[:, o:o + P], k.xt[0:D, o:o + P], wt[:, :], start=True, stop=True)
                last.then_inc(products, 1)


def conv_sums(nc, k, first, name):
    with ExitStack() as ctx:
        sb = lambda n, s, d: ctx.enter_context(nc.sbuf_tensor(f"{name}_{n}", s, d))
        sem = lambda n: k.sem(f"{name}_{n}")
        rows = [sb(f"rows{u}", [P, NP], BF16) for u in range(2)]
        panel = [sb(f"panel{u}", [P, W, P], BF16) for u in range(2)]
        edge = sb("edge", [P, W, P], BF16)
        seen = sb("seen", [P, W], F32)
        zero = sb("zero", [P, CUT], BF16)
        by_src = ctx.enter_context(nc.psum_tensor(f"{name}_src", [P, 4 * CUT], F32))
        by_dst = [ctx.enter_context(nc.psum_tensor(f"{name}_dst{u}", [P, CUT], F32)) for u in range(2)]
        tps = [ctx.enter_context(nc.psum_tensor(f"{name}_t{u}", [P, 2 * CUT], BF16)) for u in range(2)]
        blank = sem("blank")
        rows_in = [sem(f"rows_in{u}") for u in range(2)]
        panel_in = [sem(f"panel_in{u}") for u in range(2)]
        panel_out = [sem(f"panel_out{u}") for u in range(2)]
        turned, copied, own_v, summed, read, panel_free = map(
            sem, ("turned", "copied", "own", "summed", "read", "panel_free"))
        block = ctx.enter_context(nc.Block())
        GRP = [(b, min(8, W - b)) for b in range(0, W, 8)]
        NG = len(GRP)

        def windows(eng, body):
            with eng.Fori(0, W - 1, 2) as w:
                body(w, 0)
                body(w + 1, 1)
            body(W - 1, 0)

        @block.sync
        def _(sp):
            def load(w, u):
                sp.wait_ge(summed, w + 1)
                sp.dma_start(rows[u][:, :], k.at[ds(w, 1), :, :].rearrange("w p n -> p (w n)")
                             ).then_inc(rows_in[u], 16)
                if not first:
                    sp.dma_start(panel[u][:, :, :], k.a[ds(w, 1), :, :, :].rearrange("w p k d -> p (w k) d")
                                 ).then_inc(panel_in[u], 16)
            windows(sp, load)

        @block.tensor
        def _(pe):
            pe.sem_inc(summed, 2)
            pe.wait_ge(blank, 1)
            for b in range(4):
                pe.matmul(by_src[:, b * CUT:(b + 1) * CUT], zero[:, 0:P], zero[:, :], start=True, stop=True,
                          skip_group_check=True)

            def window(w, u):
                pe.wait_ge(rows_in[u], (w - u) * 8 + 16)

                def turn(g):
                    b, n = GRP[g]
                    pe.wait_ge(copied, w * NG + g + 1)
                    for j in range(n):
                        last = pe.transpose(tps[g % 2][:, j * P:(j + 1) * P],
                                            rows[u][:, (b + j) * P:(b + j + 1) * P], k.identb[:, :])
                    last.then_inc(turned, 1)

                def back(blocks):
                    for b in blocks:
                        for part in range(3):
                            last = pe.matmul(by_src[:, b * D:(b + 1) * D], rows[u][:, b * P:(b + 1) * P],
                                             k.parts[:, ds(w, 1), 1, part, :], start=False, stop=True,
                                             skip_group_check=True)
                    return last

                cuts = [0, 7, 14, 20, W]
                for g in range(NG):
                    if first:
                        turn(g)
                    back(range(cuts[g], cuts[g + 1]))
                if first:
                    pe.wait_ge(copied, (w + 1) * NG + 2)
                else:
                    pe.wait_ge(panel_in[u], (w - u) * 8 + 16)
                pe.wait_ge(read, w + 1)
                for b in range(W):
                    last = pe.matmul(by_dst[u][:, 0:3 * D], panel[u][:, b, :],
                                     k.parts[:, b, 0, :, :].rearrange("p a d -> p (a d)"),
                                     start=(b == 0), stop=(b == W - 1))
                last.then_inc(summed, 1)
            windows(pe, window)

        @block.scalar
        def _(act):
            if not first:
                return
            act.sem_inc(copied, 2)
            for u in range(2):
                act.sem_inc(panel_out[u], 16)

            def window(w, u):
                act.wait_ge(panel_out[u], (w - u) * 8 + 16)
                act.wait_ge(summed, w + 1)
                act.wait_ge(panel_free, w + 1)
                for g, (b, n) in enumerate(GRP):
                    act.wait_ge(turned, w * NG + g + 1)
                    act.activation(panel[u][:, b:b + n, :].rearrange("p a d -> p (a d)"),
                                   tps[g % 2][:, 0:n * P], ACT.Copy).then_inc(copied, 1)
                act.wait_ge(copied, (w + 1) * NG + 2)
                act.dma_start(k.a[ds(w, 1), :, :, :].rearrange("w p k d -> p (w k) d"),
                              panel[u][:, :, :]).then_inc(panel_out[u], 16)
            windows(act, window)
            act.wait_ge(panel_out[0], 16 * (W // 2 + 2))
            act.wait_ge(panel_out[1], 16 * (W // 2 + 1))

        @block.vector
        def _(v):
            own = Own(v, own_v)
            if first:
                own.did(v.memset(k.uniq[:, :], 0.0))
            own.did(v.memset(zero[:, :], 0.0))
            own.wait()
            v.sem_inc(blank, 1)
            v.sem_inc(read, 2)
            v.sem_inc(panel_free, 2)
            begun = own.n
            steps = 4 if first else 1

            def window(w, u):
                own.at(w * steps + begun)
                if first:
                    v.wait_ge(copied, (w + 1) * NG + 2)
                    own.did(v.tensor_scalar(edge[:, :, :], panel[u][:, :, :], 1.0, None, ALU.min))
                    own.wait()
                    v.sem_inc(panel_free, 1)
                    own.do(v.tensor_reduce(seen[:, :], edge[:, :, :], AX.X, ALU.add))
                    own.do(v.tensor_tensor(k.uniq[:, :], k.uniq[:, :], seen[:, :], ALU.add))
                v.wait_ge(summed, w + 3)
                own.do(v.tensor_reduce(k.agg[:, ds(w, 1), 0, :],
                                       by_dst[u][:, 0:3 * D].rearrange("p (a d) -> p d a", a=3), AX.X, ALU.add))
                v.sem_inc(read, 1)
            windows(v, window)
            v.wait_ge(summed, W + 2)
            v.tensor_copy(k.agg[:, :, 1, :], by_src[:, 0:W * D].rearrange("p (w d) -> p w d", w=W)).then_inc(read, 1)


def conv_result(nc, k, name):
    with ExitStack() as ctx:
        sb = lambda n, s, d: ctx.enter_context(nc.sbuf_tensor(f"{name}_{n}", s, d))
        sem = lambda n: k.sem(f"{name}_{n}")
        deg = sb("deg", [P, W], F32)
        root = sb("root", [P, W], F32)
        norm = sb("norm", [P, W], F32)
        own_v, deg_ok, root_ok = map(sem, ("own", "deg_ok", "root_ok"))
        block = ctx.enter_context(nc.Block())

        @block.vector
        def _(v):
            own = Own(v, own_v)
            own.do(v.tensor_reduce(deg[:, :], k.cnt8[:, :, :], AX.X, ALU.add))
            own.do(v.tensor_scalar(deg[:, :], deg[:, :], 1.0, None, ALU.max))
            v.sem_inc(deg_ok, 1)
            own.do(v.tensor_tensor(k.agg[:, :, :, :], k.agg[:, :, :, :], k.y[:, :, :, :], ALU.add))
            v.wait_ge(root_ok, 1)
            own.do(v.reciprocal(norm[:, :], root[:, :]))
            for c, by in enumerate((norm, k.vec)):
                own.did(v.tensor_tensor(k.agg[:, :, c, :], k.agg[:, :, c, :],
                                        by[:, :].unsqueeze(2).broadcast_to([P, W, D]), ALU.mult))
            own.wait()
            own.do(v.tensor_tensor(k.z[:, :, :], k.agg[:, :, 0, :], k.agg[:, :, 1, :], ALU.add))

        @block.scalar
        def _(act):
            act.wait_ge(deg_ok, 1)
            act.activation(root[:, :], deg[:, :], ACT.Sqrt).then_inc(root_ok, 1)


def add_and_norm(nc, k, scale, name):
    with ExitStack() as ctx:
        sb = lambda n, s, d: ctx.enter_context(nc.sbuf_tensor(f"{name}_{n}", s, d))
        sem = lambda n: k.sem(f"{name}_{n}")
        mean = sb("mean", [P, W], F32)
        var = sb("var", [P, W], F32)
        sq = sb("sq", [P, W, D], F32)
        eps = sb("eps", [P, 1], F32)
        own_v, var_ok, std_ok = map(sem, ("own", "var_ok", "std_ok"))
        block = ctx.enter_context(nc.Block())
        wide = lambda t: t[:, :].unsqueeze(2).broadcast_to([P, W, D])

        @block.vector
        def _(v):
            own = Own(v, own_v)
            own.did(v.memset(eps[:, :], EPS))
            own.do(v.scalar_tensor_tensor(k.x[:, :, :], k.x[:, :, :], float(scale), k.z[:, :, :],
                                          ALU.mult, ALU.add))
            own.do(v.tensor_reduce(mean[:, :], k.x[:, :, :], AX.X, ALU.add))
            own.do(v.tensor_scalar(mean[:, :], mean[:, :], 1.0 / D, None, ALU.mult))
            own.do(v.tensor_tensor(k.x[:, :, :], k.x[:, :, :], wide(mean), ALU.subtract))
            own.do(v.tensor_tensor(sq[:, :, :], k.x[:, :, :], k.x[:, :, :], ALU.mult))
            own.do(v.tensor_reduce(var[:, :], sq[:, :, :], AX.X, ALU.add))
            v.sem_inc(var_ok, 1)
            v.wait_ge(std_ok, 1)
            own.do(v.reciprocal(var[:, :], var[:, :]))
            own.do(v.tensor_tensor(k.x[:, :, :], k.x[:, :, :], wide(var), ALU.mult))

        @block.scalar
        def _(act):
            act.wait_ge(var_ok, 1)
            act.activation(var[:, :], var[:, :], ACT.Sqrt, bias=eps[:, 0:1], scale=1.0 / D).then_inc(std_ok, 1)


def edge_features(nc, k, w1, b1):
    with ExitStack() as ctx:
        sb = lambda n, s, d: ctx.enter_context(nc.sbuf_tensor(f"ef_{n}", s, d))
        sem = lambda n: k.sem(f"ef_{n}")
        wt = sb("wt", [D + 1, 2, 2 * D], F32)
        qs = sb("qs", [P, W, 2 * D], F32)
        most = sb("most", [P, 1], F32)
        top = sb("top", [1, 2], F32)
        rnd = sb("rnd", [1, 1], I32)
        ps = [ctx.enter_context(nc.psum_tensor(f"ef_ps{u}", [P, CUT], F32)) for u in range(4)]
        pt = ctx.enter_context(nc.psum_tensor("ef_pt", [1, CUT], F32))
        loaded, own_v, wt_ok, most_ok, most_t, products, kept, rounds_ok, stored = map(
            sem, ("loaded", "own", "wt_ok", "most_ok", "most_t", "products", "kept", "rounds_ok", "stored"))
        block = ctx.enter_context(nc.Block())
        H = 2 * D
        PAIRS = [(w, min(2, W - w)) for w in range(0, W, 2)]

        @block.sync
        def _(sp):
            sp.dma_start(wt[0:D, 0, :], w1[0:D, :]).then_inc(loaded, 16)
            sp.dma_start(wt[0:D, 1, :], w1[D:2 * D, :]).then_inc(loaded, 16)
            sp.dma_start(wt[D:D + 1, 0, :], b1.rearrange("(a n) -> a n", a=1)).then_inc(loaded, 16)
            sp.wait_ge(rounds_ok, 1)
            sp.dma_start(k.rounds[:, :], rnd[:, :]).then_inc(stored, 16)
            sp.wait_ge(kept, len(PAIRS))
            sp.dma_start(k.q.rearrange("(w p) h -> p w h", p=P), qs[:, :, :]).then_inc(stored, 16)
            sp.wait_ge(stored, 32)

        @block.vector
        def _(v):
            own = Own(v, own_v)
            own.did(v.memset(wt[D:D + 1, 1, :], 0.0))
            own.do(v.tensor_reduce(most[:, :], k.uniq[:, :], AX.X, ALU.max))
            v.sem_inc(most_ok, 1)
            v.wait_ge(loaded, 48)
            own.do(v.tensor_tensor(wt[0:D, 0, :], wt[0:D, 0, :], wt[0:D, 1, :], ALU.subtract))
            v.sem_inc(wt_ok, 1)
            v.wait_ge(most_t, 1)
            own.do(v.tensor_reduce(top[:, 0:1], pt[:, 0:P], AX.X, ALU.max))
            own.do(v.tensor_scalar(top[:, 1:2], top[:, 0:1], 7.0, 8.0, ALU.add, ALU.max))
            own.do(v.tensor_copy(rnd[:, :], top[:, 1:2]))
            own.do(v.tensor_scalar(rnd[:, :], rnd[:, :], 3, None, ALU.arith_shift_right))
            v.sem_inc(rounds_ok, 1)

        @block.tensor
        def _(pe):
            pe.wait_ge(most_ok, 1)
            pe.transpose(pt[:, 0:P], most[:, :], k.ident[:, :]).then_inc(most_t, 1)
            pe.wait_ge(wt_ok, 1)
            for n, (w, m) in enumerate(PAIRS):
                if n >= 4:
                    pe.wait_ge(kept, n - 3)
                for j in range(m):
                    last = pe.matmul(ps[n % 4][:, j * 2 * H:(j + 1) * 2 * H],
                                     k.xt[:, (w + j) * P:(w + j + 1) * P],
                                     wt[:, :, :].rearrange("p a h -> p (a h)"), start=True, stop=True)
                last.then_inc(products, 1)

        @block.scalar
        def _(act):
            for n, (w, m) in enumerate(PAIRS):
                act.wait_ge(products, n + 1)
                both = ps[n % 4][:, 0:m * 2 * H].rearrange("p (j a h) -> p j a h", j=m, a=2)
                act.activation(k.p[:, w:w + m, :], both[:, :, 0, :], ACT.Copy)
                act.activation(qs[:, w:w + m, :], both[:, :, 1, :], ACT.Copy).then_inc(kept, 1)


def edge_maxima(nc, k, w2, b2):
    with ExitStack() as ctx:
        sb = lambda n, s, d: ctx.enter_context(nc.sbuf_tensor(f"em_{n}", s, d))
        sem = lambda n: k.sem(f"em_{n}")
        H = 2 * D
        Q = 4
        MAXR = -(-NP // 8)
        place = sb("place", [P, NP], I16)
        raw = sb("raw", [P, W, P], BF16)
        left = sb("left", [P, NP], I16)
        top = sb("top", [P, 8], F32)
        first = sb("first", [P, 1], F32)
        none = sb("none", [P, 8], F32)
        idx = sb("idx", [P, 2, MAXR * 8], I32)
        got = [sb(f"got{q}", [P, 2, H], F32) for q in range(Q)]
        now = [sb(f"now{q}", [P, 2], I32) for q in range(Q)]
        hid = [sb(f"hid{q}", [P, 2 * P], F32) for q in range(Q)]
        ident2 = sb("ident2", [P, 2, P], F32)
        pw = sb("pw", [P, H], F32)
        w2s = sb("w2s", [P, D], F32)
        b2s = sb("b2s", [P, D], F32)
        best = sb("best", [P, D], F32)
        red = sb("red", [P, 2, D], F32)
        has = sb("has", [P, W], F32)
        tps = [ctx.enter_context(nc.psum_tensor(f"em_t{q}", [P, CUT], F32)) for q in range(Q)]
        ops = [ctx.enter_context(nc.psum_tensor(f"em_o{u}", [P, CUT], F32)) for u in range(2)]
        consts, found, raw_in, raw_free, own_v, own_x = map(
            sem, ("consts", "found", "raw_in", "raw_free", "own", "own_x"))
        mid = sem("mid")
        gat = [sem(f"gat{q}") for q in range(Q)]
        taken = [sem(f"taken{q}") for q in range(Q)]
        now_ok = [sem(f"now_ok{q}") for q in range(Q)]
        lined = [sem(f"lined{q}") for q in range(Q)]
        outs = [sem(f"outs{u}") for u in range(2)]
        read = [sem(f"read{u}") for u in range(2)]
        p_ok = sem("p_ok")
        passed = [sem(f"passed{e}") for e in range(3)]
        block = ctx.enter_context(nc.Block())

        def number_of_rounds(eng):
            return eng.value_load(k.rounds[0:1, 0:1], min_val=1, max_val=MAXR)

        @block.sync
        def _(sp):
            sp.dma_start(w2s[:, :], w2[:, :]).then_inc(consts, 16)
            sp.dma_start(b2s[:, :], b2.rearrange("(a n) -> a n", a=1).broadcast_to([P, D])).then_inc(consts, 16)
            with sp.Fori(0, W) as w:
                sp.wait_ge(raw_free, w)
                sp.dma_start(raw[:, :, :], k.a[:, :, ds(w, 1), :].rearrange("a p k d -> p a (k d)")
                             ).then_inc(raw_in, 16)

        @block.gpsimd
        def _(pool):
            pool.iota(place[:, :], pattern=[[-1, NP]], base=NP, channel_multiplier=0,
                      allow_small_or_imprecise_dtypes=True).then_inc(consts, 1)
            rounds = number_of_rounds(pool)
            with pool.Fori(0, W) as w:
                with pool.Fori(0, rounds) as r:
                    g = pool.snap(w * rounds + r)
                    pool.wait_ge(found, g + 1)
                    for q in range(Q):
                        pool.wait_ge(taken[q], g + 1)
                        pool.tensor_copy(now[q][:, :], idx[:, ds(w % 2, 1), ds(r * 8 + 2 * q, 2)]
                                         .rearrange("p a b -> p (a b)")).then_inc(now_ok[q], 1)
                        wait_alone(pool, now_ok[q], g + 1, passed[0])
                        for j in range(2):
                            pool.indirect_dma_start(
                                out=got[q][:, j, :], out_offset=None, in_=k.q[:, :],
                                in_offset=bass.IndirectOffsetOnAxis(ap=now[q][:, j:j + 1], axis=0)
                            ).then_inc(gat[q], 16)

        @block.vector
        def _(v):
            own = Own(v, own_v)
            for j in range(2):
                own.did(v.tensor_copy(ident2[:, j, :], k.ident[:, :]))
            own.do(v.tensor_scalar(has[:, :], k.uniq[:, :], 0.0, None, ALU.is_gt))
            v.sem_inc(consts, 1)
            v.wait_ge(consts, 34)
            rounds = number_of_rounds(v)
            begun = own.n
            x = Own(v, own_x)

            def window_find(w, r, base):
                x.at(base)
                x.do(v.max(top[:, :], left[:, :]))
                x.did(v.scalar_tensor_tensor(left[:, :], left[:, :], top[:, 7:8], left[:, :],
                                             ALU.is_lt, ALU.mult))
                x.did(v.tensor_tensor(first[:, :], first[:, :], top[:, 0:1], ALU.max))
                x.do(v.tensor_scalar(none[:, :], top[:, :], 0.0, None, ALU.is_equal))
                x.do(v.scalar_tensor_tensor(none[:, :], none[:, :], first[:, :], top[:, :],
                                            ALU.mult, ALU.add))
                x.do(v.tensor_scalar(idx[:, ds(w % 2, 1), ds(r * 8, 8)].rearrange("p a b -> p (a b)"),
                                     none[:, :], -1.0, float(NP), ALU.mult, ALU.add))
                v.sem_inc(found, 1)
            STEPS = 6

            def window_begin(w, base):
                x.at(base)
                v.wait_ge(raw_in, (w + 1) * 16)
                x.did(v.scalar_tensor_tensor(left[:, :], raw[:, :, :].rearrange("p a d -> p (a d)"), 0.0,
                                             place[:, :], ALU.is_gt, ALU.mult))
                x.did(v.memset(first[:, :], 1.0))
                x.wait()
                v.sem_inc(raw_free, 1)
            BEGIN = 2

            def reduce(w, g, rbase):
                own.at(rbase)
                for u in range(2):
                    v.wait_ge(outs[u], g + 1)
                    own.did(v.tensor_reduce(red[:, u, :], ops[u][:, 0:4 * D].rearrange("p (k d) -> p d k", k=4),
                                            AX.X, ALU.max))
                own.wait()
                for u in range(2):
                    v.sem_inc(read[u], 1)
                    own.do(v.tensor_tensor(best[:, :], best[:, :], red[:, u, :], ALU.max))
            RED = 4

            for u in range(2):
                v.sem_inc(read[u], 1)
            window_begin(0, 0)
            with v.Fori(0, rounds) as r:
                window_find(0, r, r * STEPS + BEGIN)

            per = v.snap(rounds * STEPS + BEGIN)
            perr = v.snap(rounds * RED + 3)

            def close(w, base):
                own.at(base)
                own.do(v.tensor_tensor(best[:, :], best[:, :], b2s[:, :], ALU.add))
                own.do(v.tensor_scalar(k.z[:, ds(w, 1), :].rearrange("p a d -> p (a d)"), best[:, :],
                                       has[:, ds(w, 1)], None, ALU.mult))
                v.sem_inc(passed[2], 1)

            def open_(base):
                own.at(base)
                own.did(v.memset(best[:, :], -3.0e38))
                wait_alone(v, own_v, own.base + own.n, passed[2])

            with v.Fori(0, W - 1) as w:
                xb = v.snap((w + 1) * per)
                ob = v.snap(w * perr + begun)
                window_begin(w + 1, xb)
                open_(ob)
                with v.Fori(0, rounds) as r:
                    window_find(w + 1, r, xb + r * STEPS + BEGIN)
                    reduce(w, w * rounds + r, ob + r * RED + 1)
                close(w, ob + rounds * RED + 1)
            ob = v.snap((W - 1) * perr + begun)
            open_(ob)
            with v.Fori(0, rounds) as r:
                reduce(W - 1, (W - 1) * rounds + r, ob + r * RED + 1)
            close(W - 1, ob + rounds * RED + 1)

        @block.tensor
        def _(pe):
            for q in range(Q):
                pe.sem_inc(taken[q], 1)
            pe.wait_ge(consts, 34)
            rounds = number_of_rounds(pe)
            with pe.Fori(0, W) as w:
                wait_alone(pe, p_ok, w + 1, passed[1])
                with pe.Fori(0, rounds) as r:
                    g = pe.snap(w * rounds + r)

                    def turn(q):
                        pe.wait_ge(gat[q], (g + 1) * 32)
                        for j in range(2):
                            last = pe.matmul(tps[q][:, j * P:(j + 1) * P], got[q][:, j, :], k.ident[:, :],
                                             start=(j == 0), stop=False, skip_group_check=True)
                        pe.matmul(tps[q][:, 0:2 * P], pw[:, :], ident2[:, :, :].rearrange("p a b -> p (a b)"),
                                  start=False, stop=True, skip_group_check=True).then_inc(taken[q], 1)

                    def multiply(q):
                        pe.wait_ge(lined[q], g + 1)
                        u = q // 2
                        if q % 2 == 0:
                            pe.wait_ge(read[u], g + 1)
                        for j in range(2):
                            o = ((q % 2) * 2 + j) * D
                            last = pe.matmul(ops[u][:, o:o + D], hid[q][:, j * P:(j + 1) * P], w2s[:, :],
                                             start=True, stop=True, skip_group_check=True)
                        last.then_inc(outs[u] if q % 2 else mid, 1)
                    turn(0)
                    turn(1)
                    multiply(0)
                    turn(2)
                    multiply(1)
                    turn(3)
                    multiply(2)
                    multiply(3)

        @block.scalar
        def _(act):
            rounds = number_of_rounds(act)
            with act.Fori(0, W) as w:
                for q in range(Q):
                    act.wait_ge(taken[q], w * rounds + 1)
                act.activation(pw[:, :], k.p[:, ds(w, 1), :].rearrange("p a h -> p (a h)"),
                               ACT.Copy).then_inc(p_ok, 1)
                with act.Fori(0, rounds) as r:
                    g = act.snap(w * rounds + r)
                    for q in range(Q):
                        act.wait_ge(taken[q], g + 2)
                        if q % 2:
                            act.wait_ge(outs[q // 2], g)
                        else:
                            act.wait_ge(mid, 2 * g)
                        act.activation(hid[q][:, :], tps[q][:, 0:2 * P], ACT.Relu).then_inc(lined[q], 1)


def attention_features(nc, k, wq, bq, wk, bk, wv, bv, ws, bs, name):
    with ExitStack() as ctx:
        sb = lambda n, s, d: ctx.enter_context(nc.sbuf_tensor(f"{name}_{n}", s, d))
        sem = lambda n: k.sem(f"{name}_{n}")
        H = 2 * D
        wqk = sb("wqk", [D + 1, 2, H], F32)
        wvs = sb("wvs", [D + 1, H + D], F32)
        ps = [ctx.enter_context(nc.psum_tensor(f"{name}_ps{u}", [P, CUT], F32)) for u in range(8)]
        loaded, products, kept = map(sem, ("loaded", "products", "kept"))
        block = ctx.enter_context(nc.Block())
        row = lambda b: b.rearrange("(a n) -> a n", a=1)
        QK = [(t, h, c, wd) for t in range(2) for h in range(2) for c, wd in SLICES]
        VS = [(w, min(2, W - w)) for w in range(0, W, 2)]
        KV = H + D

        @block.sync
        def _(sp):
            for dst, src in ((wqk[0:D, 0, :], wq[:, :]), (wqk[0:D, 1, :], wk[:, :]),
                             (wqk[D:D + 1, 0, :], row(bq)), (wqk[D:D + 1, 1, :], row(bk)),
                             (wvs[0:D, 0:H], wv[:, :]), (wvs[D:D + 1, 0:H], row(bv)),
                             (wvs[0:D, H:KV], ws[:, :]), (wvs[D:D + 1, H:KV], row(bs))):
                sp.dma_start(dst, src).then_inc(loaded, 16)

        @block.tensor
        def _(pe):
            pe.wait_ge(loaded, 16 * 8)
            n = 0
            for t, h, c, wd in QK:
                if n >= 8:
                    pe.wait_ge(kept, n - 7)
                pe.matmul(ps[n % 8][0:D, 0:wd], wqk[:, t, h * D:(h + 1) * D], k.xt[:, c:c + wd],
                          start=True, stop=True).then_inc(products, 1)
                n += 1
            for w, m in VS:
                pe.wait_ge(kept, n - 7)
                for j in range(m):
                    last = pe.matmul(ps[n % 8][:, j * KV:(j + 1) * KV], k.xt[:, (w + j) * P:(w + j + 1) * P],
                                     wvs[:, :], start=True, stop=True)
                last.then_inc(products, 1)
                n += 1

        @block.scalar
        def _(act):
            n = 0
            for t, h, c, wd in QK:
                act.wait_ge(products, n + 1)
                act.activation((k.ka if t else k.qa)[0:D, h, c:c + wd], ps[n % 8][0:D, 0:wd], ACT.Copy,
                               scale=1.0 if t else D ** -0.5).then_inc(kept, 1)
                n += 1
            for w, m in VS:
                act.wait_ge(products, n + 1)
                both = ps[n % 8][:, 0:m * KV].rearrange("p (j c) -> p j c", j=m)
                for h in range(2):
                    act.activation(k.va[:, w:w + m, h, 0:D], both[:, :, h * D:(h + 1) * D], ACT.Copy)
                act.activation(k.z[:, w:w + m, :], both[:, :, H:KV], ACT.Copy).then_inc(kept, 1)
                n += 1

        @block.vector
        def _(v):
            v.memset(k.ka[D:D + 1, :, :], 1.0)
            v.memset(k.va[:, :, :, D:D + 1], 1.0)


def attention(nc, k, name):
    with ExitStack() as ctx:
        sb = lambda n, s, d: ctx.enter_context(nc.sbuf_tensor(f"{name}_{n}", s, d))
        sem = lambda n: k.sem(f"{name}_{n}")
        rows = sb("rows", [P, NP], BF16)
        no_row = [sb(f"no_row{u}", [P, NP], BF16) for u in range(2)]
        panel = [sb(f"panel{u}", [P, W * P], BF16) for u in range(2)]
        no_panel = [sb(f"no_panel{u}", [P, W * P], BF16) for u in range(2)]
        qw = [sb(f"qw{u}", [D + 1, 2, P], F32) for u in range(2)]
        WIDE = 2 * CUT
        PARTS = [(c, min(WIDE, NP - c)) for c in range(0, NP, WIDE)]
        most = sb("most", [P, 2, len(PARTS)], F32)
        top = sb("top", [P, 2], F32)
        some = sb("some", [P, 2], F32)
        GRP = [(b, min(4, W - b)) for b in range(0, W, 4)]
        ex = [sb(f"ex{u}", [P, 4 * P], F32) for u in range(2)]
        exc = [sb(f"exc{u}", [P, 4 * P], F32) for u in range(2)]
        den = sb("den", [P, 2], F32)
        res = sb("res", [P, 2, D], F32)
        sps = [ctx.enter_context(nc.psum_tensor(f"{name}_s{u}", [P, WIDE], F32)) for u in range(2)]
        tps = [ctx.enter_context(nc.psum_tensor(f"{name}_t{u}", [P, CUT], F32)) for u in range(2)]
        mps = ctx.enter_context(nc.psum_tensor(f"{name}_m", [P, CUT], F32))
        ops = ctx.enter_context(nc.psum_tensor(f"{name}_o", [P, CUT], F32))
        rows_in, rows_free, own_v, masked, q_ok, scored, maxed, top_ok, top_t, m_ok = map(
            sem, ("rows_in", "rows_free", "own", "masked", "q_ok", "scored", "maxed", "top_ok", "top_t", "m_ok"))
        panel_in = [sem(f"panel_in{u}") for u in range(2)]
        shifted, expd, weighed, summed, done = map(sem, ("shifted", "expd", "weighed", "summed", "done"))
        block = ctx.enter_context(nc.Block())
        NPT = 2 * len(PARTS)
        NGR = 2 * len(GRP)

        def windows(eng, body):
            with eng.Fori(0, W - 1, 2) as w:
                body(w, 0)
                body(w + 1, 1)
            body(W - 1, 0)

        @block.sync
        def _(sp):
            def load(w, u):
                sp.wait_ge(rows_free, w + 1)
                sp.dma_start(rows[:, :], k.at[ds(w, 1), :, :].rearrange("w p n -> p (w n)")).then_inc(rows_in, 16)
                sp.wait_ge(done, w + 1)
                sp.dma_start(panel[u][:, :], k.a[ds(w, 1), :, :, :].rearrange("w p k d -> p (w k d)")
                             ).then_inc(panel_in[u], 16)
            windows(sp, load)

        @block.scalar
        def _(act):
            def window(w, u):
                act.wait_ge(done, w + 1)
                act.activation(qw[u][0:D, :, :], k.qa[0:D, :, ds(w * P, P)], ACT.Copy).then_inc(q_ok, 1)
                act.wait_ge(top_t, w + 1)
                for h in range(2):
                    act.activation(qw[u][D:D + 1, h, :], mps[0:1, h * P:(h + 1) * P], ACT.Copy).then_inc(m_ok, 1)
                for h in range(2):
                    for g, (b, n) in enumerate(GRP):
                        i = h * len(GRP) + g
                        act.wait_ge(shifted, w * NGR + i + 1)
                        act.wait_ge(weighed, w * NGR + i + 1)
                        act.activation(ex[i % 2][:, 0:n * P], tps[i % 2][:, 0:n * P],
                                       ACT.Exp).then_inc(expd, 1)
            windows(act, window)

        @block.tensor
        def _(pe):
            def window(w, u):
                pe.wait_ge(masked, 2 * w + 2)
                pe.wait_ge(q_ok, w + 1)
                for h in range(2):
                    for n, (c, wd) in enumerate(PARTS):
                        i = h * len(PARTS) + n
                        pe.wait_ge(maxed, w * NPT + i + 1)
                        for o in range(0, wd, CUT):
                            m = min(CUT, wd - o)
                            s = sps[i % 2][:, o:o + m]
                            pe.matmul(s, qw[u][0:D, h, :], k.ka[0:D, h, c + o:c + o + m], start=True, stop=False)
                            last = pe.matmul(s, k.identb[:, :], no_row[u][:, c + o:c + o + m],
                                             start=False, stop=True)
                        last.then_inc(scored, 1)
                pe.wait_ge(top_ok, w + 1)
                for h in range(2):
                    last = pe.matmul(mps[0:1, h * P:(h + 1) * P], top[:, h:h + 1], k.ident[:, :],
                                     start=(h == 0), stop=True, skip_group_check=True)
                last.then_inc(top_t, 1)
                pe.wait_ge(m_ok, 2 * w + 2)
                units = [(h, g) for h in range(2) for g in range(len(GRP))]

                def shift(i):
                    h, g = units[i]
                    b, n = GRP[g]
                    pe.wait_ge(expd, w * NGR + i + 1)
                    t = tps[i % 2]
                    for j in range(n):
                        pe.matmul(t[:, j * P:(j + 1) * P], k.ka[:, h, (b + j) * P:(b + j + 1) * P],
                                  qw[u][:, h, :], start=(j == 0), stop=False, skip_group_check=True)
                    pe.matmul(t[:, 0:n * P], k.identb[:, :], no_panel[u][:, b * P:(b + n) * P],
                              start=False, stop=True, skip_group_check=True).then_inc(shifted, 1)

                def sum_up(i):
                    h, g = units[i]
                    b, n = GRP[g]
                    pe.wait_ge(weighed, w * NGR + i + 3)
                    if i == 0:
                        pe.wait_ge(done, w + 2)
                    for j in range(n):
                        last = pe.matmul(ops[:, h * 2 * D:h * 2 * D + D + 1], exc[i % 2][:, j * P:(j + 1) * P],
                                         k.va[:, b + j, h, :], start=(i == 0 and j == 0),
                                         stop=True, skip_group_check=True)
                    last.then_inc(summed, 1)
                for i in range(len(units)):
                    shift(i)
                    if i >= 2:
                        sum_up(i - 2)
                sum_up(len(units) - 2)
                sum_up(len(units) - 1)
            windows(pe, window)


        @block.vector
        def _(v):
            for s in (done, expd, weighed, summed, maxed):
                v.sem_inc(s, 2)
            v.sem_inc(rows_free, 1)
            own = Own(v, own_v)

            def mask(w, u):
                v.wait_ge(rows_in, (w + 1) * 16)
                v.tensor_scalar(no_row[u][:, :], rows[:, :], 0.0, NEG, ALU.is_equal, ALU.mult).then_inc(rows_free, 1)
                v.wait_ge(panel_in[u], (w - u) * 8 + 16)
                v.tensor_scalar(no_panel[u][:, :], panel[u][:, :], 0.0, NEG, ALU.is_equal,
                                ALU.mult).then_inc(masked, 1)
                v.wait_ge(rows_free, w + 2)
                v.sem_inc(masked, 1)

            def window(w, u, last=False):
                own.at(w * STEPS)
                for h in range(2):
                    for n, (c, wd) in enumerate(PARTS):
                        i = h * len(PARTS) + n
                        v.wait_ge(scored, w * NPT + i + 1)
                        v.tensor_reduce(most[:, h, n:n + 1], sps[i % 2][:, 0:wd], AX.X, ALU.max).then_inc(maxed, 1)
                v.wait_ge(maxed, (w + 1) * NPT + 2)
                own.do(v.tensor_reduce(top[:, :], most[:, :, :], AX.X, ALU.max))
                own.do(v.tensor_scalar(some[:, :], top[:, :], NEG / 2, None, ALU.is_gt))
                own.do(v.scalar_tensor_tensor(top[:, :], top[:, :], -1.0, some[:, :], ALU.mult, ALU.mult))
                v.sem_inc(top_ok, 1)
                if not last:
                    mask(w + 1, 1 - u)
                for i in range(NGR):
                    b, n = GRP[i % len(GRP)]
                    v.wait_ge(expd, w * NGR + i + 3)
                    v.wait_ge(summed, w * NGR + i + 1)
                    v.tensor_tensor(exc[i % 2][:, 0:n * P], ex[i % 2][:, 0:n * P],
                                    panel[u][:, b * P:(b + n) * P], ALU.mult).then_inc(weighed, 1)
                v.wait_ge(summed, (w + 1) * NGR + 2)
                own.do(v.tensor_scalar(den[:, :], ops[:, 0:4 * D].rearrange("p (h c) -> p h c", h=2)[:, :, D],
                                       1e-16, 2.0, ALU.add, ALU.mult))
                own.do(v.reciprocal(den[:, :], den[:, :]))
                for h in range(2):
                    z = k.z[:, ds(w, 1), :].rearrange("p a d -> p (a d)")
                    own.do(v.scalar_tensor_tensor(z, ops[:, h * 2 * D:h * 2 * D + D], den[:, h:h + 1], z,
                                                  ALU.mult, ALU.add))
                v.sem_inc(done, 1)
            STEPS = 7
            mask(0, 0)
            with v.Fori(0, W - 1, 2) as w:
                window(w, 0)
                window(w + 1, 1)
            window(W - 1, 0, last=True)


def relation_features(nc, k, weight, root, bias, name):
    with ExitStack() as ctx:
        sb = lambda n, s, d: ctx.enter_context(nc.sbuf_tensor(f"{name}_{n}", s, d))
        sem = lambda n: k.sem(f"{name}_{n}")
        wt = sb("wt", [D + 1, NREL + 1, D], F32)
        hs = [sb(f"hs{u}", [P, NREL, D], F32) for u in range(4)]
        ps = [ctx.enter_context(nc.psum_tensor(f"{name}_ps{u}", [P, CUT], F32)) for u in range(6)]
        rs = [ctx.enter_context(nc.psum_tensor(f"{name}_rs{u}", [P, CUT], F32)) for u in range(2)]
        loaded, blank, products, kept, rooted = map(sem, ("loaded", "blank", "products", "kept", "rooted"))
        stored = [sem(f"stored{u}") for u in range(4)]
        block = ctx.enter_context(nc.Block())

        @block.sync
        def _(sp):
            sp.dma_start(wt[0:D, 0:NREL, :], weight.rearrange("r d f -> d r f")).then_inc(loaded, 16)
            sp.dma_start(wt[0:D, NREL, :], root[:, :]).then_inc(loaded, 16)
            sp.dma_start(wt[D:D + 1, NREL, :], bias.rearrange("(a n) -> a n", a=1)).then_inc(loaded, 16)
            table = k.h.rearrange("(r w p) d -> w p r d", r=NREL, p=P)
            for w in range(W):
                sp.wait_ge(kept, w + 1)
                sp.dma_start(table[w], hs[w % 4][:, :, :]).then_inc(stored[w % 4], 16)
            for u in range(4):
                sp.wait_ge(stored[u], 16 * len(range(u, W, 4)))

        @block.vector
        def _(v):
            v.memset(wt[D:D + 1, 0:NREL, :], 0.0).then_inc(blank, 1)
            for w in range(W):
                v.wait_ge(rooted, w + 1)
                v.tensor_copy(k.z[:, w, :], rs[w % 2][:, 0:D]).then_inc(blank, 1)

        @block.tensor
        def _(pe):
            pe.wait_ge(loaded, 48)
            pe.wait_ge(blank, 1)
            for w in range(W):
                if w >= 6:
                    pe.wait_ge(kept, w - 5)
                if w >= 2:
                    pe.wait_ge(blank, w)
                at = k.xt[:, w * P:(w + 1) * P]
                pe.matmul(ps[w % 6][:, :], at, wt[:, 0:NREL, :].rearrange("p r d -> p (r d)"),
                          start=True, stop=True).then_inc(products, 1)
                pe.matmul(rs[w % 2][:, 0:D], at, wt[:, NREL, :], start=True, stop=True).then_inc(rooted, 1)

        @block.scalar
        def _(act):
            for w in range(W):
                act.wait_ge(products, w + 1)
                if w >= 4:
                    act.wait_ge(stored[w % 4], 16 * (w // 4))
                act.activation(hs[w % 4][:, :, :].rearrange("p r d -> p (r d)"), ps[w % 6][:, :],
                               ACT.Copy).then_inc(kept, 1)


def relation_sums(nc, k, name):
    with ExitStack() as ctx:
        sb = lambda n, s, d: ctx.enter_context(nc.sbuf_tensor(f"{name}_{n}", s, d))
        sem = lambda n: k.sem(f"{name}_{n}")
        now = [sb(f"now{j}", [P, 1], I32) for j in range(G)]
        got = [sb(f"got{j}", [P, D], F32) for j in range(G)]
        hot = [sb(f"hot{j}", [P, P], F32) for j in range(G)]
        typed = [sb(f"typed{j}", [P, NREL, D], F32) for j in range(G)]
        inv = sb("inv", [P, W, NREL], F32)
        mean = sb("mean", [P, NREL, D], F32)
        total = sb("total", [P, D], F32)
        ps = ctx.enter_context(nc.psum_tensor(f"{name}_ps", [P, CUT], F32))
        gat = [sem(f"gat{j}") for j in range(G)]
        passed = sem("passed")
        now_ok, spread, hots, multiplied, read, own_v = map(
            sem, ("now_ok", "spread", "hots", "multiplied", "read", "own"))
        block = ctx.enter_context(nc.Block())

        @block.gpsimd
        def _(pool):
            pool.sem_inc(now_ok, NT)
            with pool.Fori(0, W) as w:
                first, end, place = window_tiles(pool, k, w)
                with pool.Fori(first, end, G) as t0:
                    at = pool.snap(t0 + place)
                    for j in range(G):
                        pool.wait_ge(spread, at + j + 1)
                        pool.tensor_copy(now[j][:, :], k.msg_row[:, ds(t0 + j, 1)]).then_inc(now_ok, 1)
                        wait_alone(pool, now_ok, at + j + 1, passed)
                        pool.indirect_dma_start(
                            out=got[j][:, :], out_offset=None, in_=k.h[:, :],
                            in_offset=bass.IndirectOffsetOnAxis(ap=now[j][:, 0:1], axis=0)).then_inc(gat[j], 16)

        @block.vector
        def _(v):
            v.sem_inc(spread, NT + G)
            v.sem_inc(hots, NT)
            own = Own(v, own_v)
            own.do(v.tensor_scalar(inv[:, :, :], k.cnt8[:, :, :], 1.0, None, ALU.max))
            own.do(v.reciprocal(inv[:, :, :], inv[:, :, :]))
            begun = own.n
            gathered = v.alloc_register(f"{name}_gathered")
            v.reg_mov(gathered, 16)
            with v.Fori(0, W) as w:
                first, end, place = window_tiles(v, k, w)
                with v.Fori(first, end, G) as t0:
                    at = v.snap(t0 + place)
                    here = v.snap(gathered, min_val=16)
                    for j in range(G):
                        t = t0 + j
                        v.wait_ge(multiplied, at + j + 1)
                        v.tensor_scalar(hot[j][:, :], k.iota_p[:, :], k.wbase[:, ds(w, 1)],
                                        k.dst_t[:, ds(t, 1)], ALU.add, ALU.is_equal).then_inc(hots, 1)
                        v.wait_ge(gat[j], here)
                        v.tensor_tensor(typed[j][:, :, :], got[j][:, :].unsqueeze(1).broadcast_to([P, NREL, D]),
                                        k.type_hot[:, ds(t, 1), :].rearrange("p a r -> p (a r)")
                                        .unsqueeze(2).broadcast_to([P, NREL, D]), ALU.mult).then_inc(spread, 1)
                    v.reg_add(gathered, gathered, 16)
                v.wait_ge(multiplied, end + place + G)
                own.at(w * 3 + begun)
                own.do(v.tensor_tensor(mean[:, :, :], ps[:, :].rearrange("p (r d) -> p r d", r=NREL),
                                       inv[:, ds(w, 1), :].rearrange("p a r -> p (a r)")
                                       .unsqueeze(2).broadcast_to([P, NREL, D]), ALU.mult))
                v.sem_inc(read, 1)
                own.do(v.tensor_reduce(total[:, :], mean[:, :, :].rearrange("p r d -> p d r"), AX.X, ALU.add))
                z = k.z[:, ds(w, 1), :].rearrange("p a d -> p (a d)")
                own.do(v.tensor_tensor(z, z, total[:, :], ALU.add))

        @block.tensor
        def _(pe):
            pe.sem_inc(multiplied, NT + G)

            def tile(t, at, j, fresh):
                pe.wait_ge(hots, at + j + 1)
                pe.wait_ge(spread, at + j + 1 + G)
                pe.matmul(ps[:, :], hot[j][:, :], typed[j][:, :, :].rearrange("p r d -> p (r d)"),
                          start=fresh, stop=True, skip_group_check=True).then_inc(multiplied, 1)

            with pe.Fori(0, W) as w:
                first, end, place = window_tiles(pe, k, w)
                pe.wait_ge(read, w)
                at = pe.snap(first + place)
                for j in range(G):
                    tile(first + j, at, j, j == 0)
                with pe.Fori(first + G, end, G) as t0:
                    at2 = pe.snap(t0 + place)
                    for j in range(G):
                        tile(t0 + j, at2, j, False)


def store_nodes(nc, k, out):
    with ExitStack() as ctx:
        stored = k.sem("out_stored")
        block = ctx.enter_context(nc.Block())

        @block.sync
        def _(sp):
            sp.dma_start(out[0:(W - 1) * P, :].rearrange("(w p) d -> p w d", p=P),
                         k.x[:, 0:W - 1, :]).then_inc(stored, 16)
            sp.dma_start(out[(W - 1) * P:N, :], k.x[0:TAIL, W - 1, :]).then_inc(stored, 16)
            sp.wait_ge(stored, 32)


def build(nc, x, src, dst, edge_type_8, node_vec1, *rest, upto=99):
    weights, out = rest[:-1], rest[-1]
    with ExitStack() as ctx:
        k = allocate(nc, ctx)
        prepare(nc, k, x, src, dst, edge_type_8, node_vec1)
        count_edges(nc, k)
        if upto <= 2:
            return
        with ExitStack() as own:
            allocate_convolution(nc, own, k)
            for n, (a, b) in enumerate((weights[0:2], weights[2:4])):
                turn_nodes(nc, k, k.z if n else k.x, ACT.Relu, f"c{n}t")
                conv_features(nc, k, a, b, f"c{n}f")
                conv_sums(nc, k, n == 0, f"c{n}s")
                conv_result(nc, k, f"c{n}r")
            add_and_norm(nc, k, 2.0, "n0")
        if upto <= 3:
            return
        k.clear_semaphores()
        with ExitStack() as own:
            allocate_edges(nc, own, k)
            turn_nodes(nc, k, k.x, ACT.Copy, "et")
            edge_features(nc, k, weights[4], weights[5])
            edge_maxima(nc, k, weights[6], weights[7])
            add_and_norm(nc, k, 1.0, "n1")
        if upto <= 4:
            return
        k.clear_semaphores()
        with ExitStack() as own:
            allocate_attention(nc, own, k)
            for n in range(2):
                turn_nodes(nc, k, k.z if n else k.x, ACT.Copy, f"a{n}t")
                attention_features(nc, k, *weights[8 + 8 * n:16 + 8 * n], f"a{n}f")
                attention(nc, k, f"a{n}s")
                if upto <= 5:
                    return
            add_and_norm(nc, k, 1.0, "n2")
        if upto <= 6:
            return
        k.clear_semaphores()
        weight, root, bias = weights[24:27]
        for n in range(2):
            turn_nodes(nc, k, k.z if n else k.x, ACT.Copy, f"r{n}t")
            relation_features(nc, k, weight[n], root[n], bias[n], f"r{n}f")
            relation_sums(nc, k, f"r{n}s")
            if upto <= 7:
                return
        add_and_norm(nc, k, 1.0, "n3")
        store_nodes(nc, k, out)


UPTO = 99
_INS = ['x', 'src', 'dst', 'edge_type_8', 'node_vec1', 'L0_gnn_W1_out', 'L0_gnn_W1_back', 'L0_gnn_W2_out',
        'L0_gnn_W2_back', 'L1_gnn_W1', 'L1_gnn_b1', 'L1_gnn_W2', 'L1_gnn_b2', 'L2_gnn_l1_wq', 'L2_gnn_l1_bq',
        'L2_gnn_l1_wk', 'L2_gnn_l1_bk', 'L2_gnn_l1_wv', 'L2_gnn_l1_bv', 'L2_gnn_l1_ws', 'L2_gnn_l1_bs',
        'L2_gnn_l2_wq', 'L2_gnn_l2_bq', 'L2_gnn_l2_wk', 'L2_gnn_l2_bk', 'L2_gnn_l2_wv', 'L2_gnn_l2_bv',
        'L2_gnn_l2_ws', 'L2_gnn_l2_bs', 'L3_gnn_weight', 'L3_gnn_root', 'L3_gnn_bias']


def kernel(**inputs):
    import numpy as _np
    import concourse.bacc as _bacc
    from concourse import mybir as _mybir
    from concourse.bass_utils import run_bass_kernel_spmd as _run

    nc = _bacc.Bacc("TRN2", target_bir_lowering=False, num_devices=1)
    arrays, args = {}, []
    for name in _INS:
        a = _np.ascontiguousarray(inputs[name])
        arrays[f"in_{name}"] = a
        args.append(nc.dram_tensor(f"in_{name}", a.shape, _mybir.dt.from_np(a.dtype), kind="ExternalInput").ap())
    args.append(nc.dram_tensor("out_0", (N, D), _mybir.dt.float32, kind="ExternalOutput").ap())
    build(nc, *args, upto=UPTO)
    r = _run(nc, [arrays], core_ids=[0])
    return r.results[0]["out_0"]
```

```python
import concourse.bass as bass
from concourse import mybir
from concourse.alu_op_type import AluOpType as ALU
from contextlib import ExitStack

F32 = mybir.dt.float32
I32 = mybir.dt.int32
I16 = mybir.dt.int16
F16 = mybir.dt.float16
BF16 = mybir.dt.bfloat16
ACT = mybir.ActivationFunctionType
AX = mybir.AxisListType
ds = bass.ds

P = 128
N = 3125
E = 103125
D = 64
NREL = 8
W = -(-N // P)
NP = W * P
TAIL = N - (W - 1) * P
T = -(-E // P)
CH = -(-T // P)
NT = CH * P
FULL_T = E // P
LAST_T = E - FULL_T * P
G = 4
NO_NODE = 4000.0
CUT = 512
SLICES = [(c, min(CUT, NP - c)) for c in range(0, NP, CUT)]
EPS = 1e-5
NEG = -1e30


class Own:

    def __init__(self, eng, sem):
        self.eng, self.sem, self.base, self.n = eng, sem, 0, 0

    def at(self, base):
        self.base, self.n = base, 0

    def did(self, ins):
        ins.then_inc(self.sem, 1)
        self.n += 1

    def wait(self):
        self.eng.wait_ge(self.sem, self.base + self.n)

    def do(self, ins):
        self.did(ins)
        self.wait()


def wait_alone(eng, sem, value, passed):
    eng.wait_ge(sem, value)
    eng.sem_inc(passed, 1)


class Kept:

    def __init__(self, nc):
        self.nc, self.sems = nc, []

    def sem(self, name):
        self.sems.append(self.nc.alloc_semaphore(name))
        return self.sems[-1]

    def clear_semaphores(self):
        self.nc.all_engine_barrier()
        self.nc.clear_and_free_semaphores(self.sems)
        self.nc.all_engine_barrier()
        self.sems = []


def allocate(nc, ctx):
    k = Kept(nc)

    def sb(name, shape, dt):
        return ctx.enter_context(nc.sbuf_tensor(name, shape, dt))

    k.ident = sb("ident", [P, P], F32)
    k.identb = sb("identb", [P, P], BF16)
    k.iota_p = sb("iota_p", [P, P], F32)
    k.wbase = sb("wbase", [P, W], F32)
    k.src_t = sb("src_t", [P, NT], F32)
    k.dst_t = sb("dst_t", [P, NT], F32)
    k.msg_row = sb("msg_row", [P, NT], I32)
    k.type_hot = sb("type_hot", [P, NT, NREL], BF16)
    k.x = sb("x", [P, W, D], F32)
    k.vec = sb("vec", [P, W], F32)
    k.cnt8 = sb("cnt8", [P, W, NREL], F32)
    k.xt = sb("xt", [D + 1, NP], F32)
    k.z = sb("z", [P, W, D], F32)
    k.uniq = sb("uniq", [P, W], F32)
    k.table = nc.dram_tensor("window_table", [W, 4], I32).ap()
    k.rounds = nc.dram_tensor("neighbour_rounds", [1, 1], I32).ap()
    k.at = nc.dram_tensor("count_rows", [W, P, NP], BF16).ap()
    k.a = nc.dram_tensor("count_panels", [W, P, W, P], BF16).ap()
    k.q = nc.dram_tensor("edge_q", [NP, 2 * D], F32).ap()
    k.h = nc.dram_tensor("rel_h", [NREL * NP, D], F32).ap()
    return k


def allocate_convolution(nc, ctx, k):
    sb = lambda n, s, d: ctx.enter_context(nc.sbuf_tensor(n, s, d))
    k.y = sb("y", [P, W, 2, D], F32)
    k.agg = sb("agg", [P, W, 2, D], F32)
    k.parts = sb("parts", [P, W, 2, 3, D], BF16)


def allocate_edges(nc, ctx, k):
    sb = lambda n, s, d: ctx.enter_context(nc.sbuf_tensor(n, s, d))
    k.p = sb("p", [P, W, 2 * D], F32)


def allocate_attention(nc, ctx, k):
    sb = lambda n, s, d: ctx.enter_context(nc.sbuf_tensor(n, s, d))
    k.q_12 = sb("q_12", [P, 2, NP], BF16)
    k.q_13 = sb("q_13", [P, 2, NP], BF16)
    k.k_11 = sb("k_11", [P, 2, NP], BF16)
    k.k_22 = sb("k_22", [P, 2, NP], BF16)
    k.k_31 = sb("k_31", [P, 2, NP], BF16)
    k.va = sb("va", [P, W, 2, D + 1], F32)


def score_products(k):
    return (k.q_12, k.k_11), (k.q_12, k.k_22), (k.q_13, k.k_31)


def prepare(nc, k, x, src, dst, edge_type, node_vec1):
    with ExitStack() as ctx:
        sb = lambda n, s, d: ctx.enter_context(nc.sbuf_tensor(n, s, d))
        sem = lambda n: k.sem(n)
        raw = [sb(f"raw{j}", [P, CH, P], I32) for j in range(3)]
        rawf = [sb(f"rawf{j}", [P, CH, P], F32) for j in range(3)]
        tri = sb("tri", [W, W], F32)
        idt = sb("idt", [W, NT], F32)
        t_min = sb("t_min", [P, CH], F32)
        t_max = sb("t_max", [P, CH], F32)
        hit = sb("hit", [W, NT], F32)
        hit2 = sb("hit2", [W, NT], F32)
        wlo = sb("wlo", [W, 1], F32)
        whi = sb("whi", [W, 1], F32)
        bound = sb("bound", [W, 4], F32)
        back = sb("back", [W, 1], F32)
        ni = sb("ni", [W, 1], I32)
        nf = sb("nf", [W, 1], F32)
        row = sb("row", [W, 4], I32)
        typ = sb("typ", [P, NT], F32)
        rowf = sb("rowf", [P, NT], F32)
        tp = [ctx.enter_context(nc.psum_tensor(f"tp{j}", [P, 2 * CUT], F32)) for j in range(3)]
        bc = ctx.enter_context(nc.psum_tensor("bc", [W, CUT], F32))
        blank, loaded, consts, floats, turned, kept = map(
            sem, ("blank", "loaded", "consts", "floats", "turned", "kept"))
        own_v, mins, spread, taken, nits, before, tabled, stored = map(
            sem, ("prep_own", "mins", "spread", "taken", "nits", "before", "tabled", "stored"))
        pads, own_p = sem("pads"), sem("prep_own_p")
        block = ctx.enter_context(nc.Block())
        head = (CH - 1) * P * P
        full = FULL_T - (CH - 1) * P
        arrays = (src, dst, edge_type)

        @block.sync
        def _(sp):
            sp.wait_ge(blank, 5)
            for j, a in enumerate(arrays):
                sp.dma_start(raw[j][:, 0:CH - 1, :],
                             a[0:head].rearrange("(c p j) -> p c j", p=P, j=P)).then_inc(loaded, 16)
                sp.dma_start(raw[j][0:full, CH - 1, :],
                             a[head:head + full * P].rearrange("(p j) -> p j", j=P)).then_inc(loaded, 16)
                sp.dma_start(raw[j][full:full + 1, CH - 1, 0:LAST_T],
                             a[FULL_T * P:E].rearrange("(p j) -> p j", p=1)).then_inc(loaded, 16)
            sp.dma_start(k.x[:, 0:W - 1, :],
                         x[0:(W - 1) * P, :].rearrange("(w p) d -> p w d", p=P)).then_inc(loaded, 16)
            sp.dma_start(k.x[0:TAIL, W - 1, :], x[(W - 1) * P:N, :]).then_inc(loaded, 16)
            sp.dma_start(k.vec[:, 0:W - 1],
                         node_vec1[0:(W - 1) * P, :].rearrange("(w p) a -> p (w a)", p=P),
                         allow_slow_non_contiguous=True).then_inc(loaded, 16)
            sp.dma_start(k.vec[0:TAIL, W - 1:W], node_vec1[(W - 1) * P:N, :]).then_inc(loaded, 16)
            sp.wait_ge(tabled, 1)
            sp.dma_start(k.table[:, :], row[:, :]).then_inc(stored, 16)
            sp.wait_ge(stored, 16)

        @block.gpsimd
        def _(pool):
            own = Own(pool, own_p)
            pool.memset(raw[0][:, CH - 1, :], 0).then_inc(blank, 1)
            pool.memset(raw[1][:, CH - 1, :], int(NO_NODE)).then_inc(blank, 1)
            pool.memset(raw[2][:, CH - 1, :], 0).then_inc(blank, 1)
            pool.memset(k.x[:, W - 1, :], 0.0).then_inc(blank, 1)
            pool.memset(k.vec[:, W - 1:W], 0.0).then_inc(blank, 1)
            own.did(pool.memset(k.ident[:, :], 0.0))
            own.did(pool.memset(k.identb[:, :], 0.0))
            own.did(pool.memset(tri[:, :], 1.0))
            own.wait()
            for m in (k.ident, k.identb):
                pool.affine_select(out=m[:, :], in_=m[:, :], compare_op=ALU.not_equal, fill=1.0, base=0,
                                   pattern=[[-1, P]], channel_multiplier=1).then_inc(consts, 1)
            pool.affine_select(out=tri[:, :], in_=tri[:, :], compare_op=ALU.is_gt, fill=0.0, base=0,
                               pattern=[[1, W]], channel_multiplier=-1).then_inc(consts, 1)
            pool.iota(k.iota_p[:, :], pattern=[[1, P]], base=0, channel_multiplier=0,
                      allow_small_or_imprecise_dtypes=True).then_inc(consts, 1)
            pool.iota(k.wbase[:, :], pattern=[[P, W]], base=0, channel_multiplier=0,
                      allow_small_or_imprecise_dtypes=True).then_inc(consts, 1)
            pool.iota(wlo[:, :], pattern=[[0, 1]], base=0, channel_multiplier=P,
                      allow_small_or_imprecise_dtypes=True).then_inc(consts, 1)
            pool.iota(whi[:, :], pattern=[[0, 1]], base=P - 1, channel_multiplier=P,
                      allow_small_or_imprecise_dtypes=True).then_inc(consts, 1)
            pool.iota(idt[:, :], pattern=[[1, NT]], base=0, channel_multiplier=0,
                      allow_small_or_imprecise_dtypes=True).then_inc(consts, 1)

        @block.vector
        def _(v):
            own = Own(v, own_v)
            v.wait_ge(loaded, 16 * 13)
            for j in range(3):
                v.tensor_copy(rawf[j][:, :, :], raw[j][:, :, :]).then_inc(floats, 1)
            v.wait_ge(floats, 2)
            v.tensor_reduce(t_min[:, :], rawf[1][:, :, :], AX.X, ALU.min).then_inc(mins, 1)
            v.tensor_reduce(t_max[:, :], rawf[1][:, :, :], AX.X, ALU.max).then_inc(mins, 1)
            for j, out in enumerate((k.src_t, k.dst_t, typ)):
                v.wait_ge(turned, j + 1)
                v.tensor_copy(out[:, :], tp[j][:, 0:NT]).then_inc(kept, 1)
            v.wait_ge(kept, 3)
            own.do(v.scalar_tensor_tensor(rowf[:, :], typ[:, :], float(NP), k.src_t[:, :], ALU.mult, ALU.add))
            own.did(v.tensor_copy(k.msg_row[:, :], rowf[:, :]))
            for r in range(NREL):
                own.did(v.tensor_scalar(k.type_hot[:, :, r], typ[:, :], float(r), None, ALU.is_equal))
            v.wait_ge(consts, 8)
            for c in range(2):
                cols = slice(c * CUT, min((c + 1) * CUT, NT))
                wd = cols.stop - cols.start
                v.wait_ge(spread, 1 + c)
                own.do(v.tensor_scalar(hit[:, cols], bc[:, 0:wd], whi[:, 0:1], None, ALU.is_le))
                v.sem_inc(taken, 1)
            for c in range(2):
                cols = slice(c * CUT, min((c + 1) * CUT, NT))
                wd = cols.stop - cols.start
                v.wait_ge(spread, 3 + c)
                own.do(v.tensor_scalar(hit2[:, cols], bc[:, 0:wd], wlo[:, 0:1], None, ALU.is_ge))
                v.sem_inc(taken, 1)
            own.do(v.tensor_tensor(hit[:, :], hit[:, :], hit2[:, :], ALU.mult))
            own.do(v.scalar_tensor_tensor(hit2[:, :], idt[:, :], 1.0, hit[:, :], ALU.add, ALU.mult))
            own.did(v.tensor_reduce(bound[:, 1:2], hit2[:, :], AX.X, ALU.max))
            own.do(v.scalar_tensor_tensor(hit[:, :], idt[:, :], -float(NT), hit[:, :], ALU.add, ALU.mult))
            own.do(v.tensor_reduce(bound[:, 0:1], hit[:, :], AX.X, ALU.min))
            own.do(v.tensor_scalar(bound[:, 0:1], bound[:, 0:1], float(NT), None, ALU.add))
            own.do(v.tensor_tensor(bound[:, 0:1], bound[:, 0:1], bound[:, 1:2], ALU.min))
            own.do(v.tensor_tensor(bound[:, 2:3], bound[:, 1:2], bound[:, 0:1], ALU.subtract))
            own.do(v.tensor_scalar(bound[:, 2:3], bound[:, 2:3], float(G - 1), float(3 * G - 1), ALU.add, ALU.max))
            own.do(v.tensor_copy(ni[:, :], bound[:, 2:3]))
            own.do(v.tensor_scalar(ni[:, :], ni[:, :], G.bit_length() - 1, None, ALU.arith_shift_right))
            own.do(v.tensor_copy(nf[:, :], ni[:, :]))
            v.sem_inc(nits, 1)
            own.did(v.tensor_copy(row[:, 0:1], bound[:, 0:1]))
            own.did(v.memset(row[:, 3:4], 0))
            own.do(v.tensor_scalar(back[:, :], bound[:, 0:1], -float(NT), None, ALU.add))
            own.did(v.scalar_tensor_tensor(row[:, 1:2], nf[:, :], float(G), bound[:, 0:1], ALU.mult, ALU.add))
            v.wait_ge(before, 1)
            own.do(v.scalar_tensor_tensor(row[:, 2:3], bc[:, 0:1], float(G), back[:, :],
                                          ALU.mult, ALU.subtract))
            v.sem_inc(tabled, 1)

        @block.tensor
        def _(pe):
            pe.wait_ge(consts, 1)
            for j in range(3):
                pe.wait_ge(floats, j + 1)
                for c in range(CH):
                    last = pe.transpose(tp[j][:, c * P:(c + 1) * P], rawf[j][:, c, :], k.ident[:, :])
                last.then_inc(turned, 1)
            pe.wait_ge(mins, 2)
            n = 0
            for t in (t_min, t_max):
                for cs in (range(0, 4), range(4, CH)):
                    if n:
                        pe.wait_ge(taken, n)
                    for c in cs:
                        o = (c - cs.start) * P
                        last = pe.matmul(bc[:, o:o + P], t[:, c:c + 1].broadcast_to([P, W]), k.ident[:, :],
                                         start=True, stop=True)
                    last.then_inc(spread, 1)
                    n += 1
            pe.wait_ge(nits, 1)
            pe.wait_ge(consts, 8)
            pe.matmul(bc[:, 0:1], tri[:, :], nf[:, 0:1], start=True, stop=True).then_inc(before, 1)


def window_tiles(eng, k, w):
    first = eng.value_load(k.table[ds(w, 1), 0:1], min_val=0, max_val=T)
    end = eng.value_load(k.table[ds(w, 1), 1:2], min_val=2 * G, max_val=T + 2 * G)
    place = eng.value_load(k.table[ds(w, 1), 2:3], min_val=NT - T, max_val=NT + W * (T + 2 * G))
    return first, end, place


def count_edges(nc, k):
    with ExitStack() as ctx:
        sb = lambda n, s, d: ctx.enter_context(nc.sbuf_tensor(n, s, d))
        sem = lambda n: k.sem(n)
        iota_s = sb("iota_s", [P, NP], F16)
        srcm = sb("srcm", [P, NT], F32)
        hot_s = sb("hot_s", [P, G, NP], BF16)
        hot_d = sb("hot_d", [P, G, P], BF16)
        rows = sb("rows", [P, 2, NP], BF16)
        ps = ctx.enter_context(nc.psum_tensor("ps_count", [P, 8 * CUT], F32))
        passed = sem("passed")
        iota_ok, own_v, hots, used, copied, stored = map(
            sem, ("iota_ok", "cnt_own", "hots", "used", "copied", "cnt_stored"))
        block = ctx.enter_context(nc.Block())
        half = NP // 2


        @block.gpsimd
        def _(pool):
            pool.iota(iota_s[:, :], pattern=[[1, NP]], base=-half, channel_multiplier=0,
                      allow_small_or_imprecise_dtypes=True).then_inc(iota_ok, 1)

        @block.vector
        def _(v):
            own = Own(v, own_v)
            own.did(v.tensor_scalar(srcm[:, :], k.src_t[:, :], -float(half), None, ALU.add))
            own.wait()
            v.sem_inc(iota_ok, 1)
            v.sem_inc(hots, 2 * NT)
            v.wait_ge(iota_ok, 2)
            with v.Fori(0, W) as w:
                first, end, place = window_tiles(v, k, w)
                with v.Fori(first, end, G) as t0:
                    for j in range(G):
                        v.wait_ge(used, t0 + place + (j + 1))
                        t = t0 + j
                        v.tensor_scalar(hot_d[:, j, :], k.iota_p[:, :], k.wbase[:, ds(w, 1)],
                                        k.dst_t[:, ds(t, 1)], ALU.add, ALU.is_equal).then_inc(hots, 1)
                        v.tensor_scalar(hot_s[:, j, :], iota_s[:, :], srcm[:, ds(t, 1)], None,
                                        ALU.is_equal).then_inc(hots, 1)

        @block.tensor
        def _(pe):
            pe.sem_inc(used, NT + G)
            pe.wait_ge(iota_ok, 2)

            def tile(t, j, fresh, seq):
                pe.wait_ge(hots, seq)
                for n, (c, wd) in enumerate(SLICES):
                    pe.matmul(ps[:, c:c + wd], hot_d[:, j, :], hot_s[:, j, c:c + wd], start=fresh,
                              stop=True, skip_group_check=True)
                return pe.matmul(ps[:, NP:NP + NREL], hot_d[:, j, :], k.type_hot[:, ds(t, 1), :], start=False,
                                 stop=True, skip_group_check=True)

            with pe.Fori(0, W) as w:
                first, end, place = window_tiles(pe, k, w)
                pe.wait_ge(copied, w)
                for j in range(G):
                    last = tile(first + j, j, j == 0, (first + place + (j + 1)) * 2)
                    last.then_inc(used, 1)
                with pe.Fori(first + G, end, G) as t0:
                    for j in range(G):
                        tile(t0 + j, j, False, (t0 + place + (j + 1)) * 2).then_inc(used, 1)

        @block.scalar
        def _(act):
            with act.Fori(0, W) as w:
                first, end, place = window_tiles(act, k, w)
                act.wait_ge(used, end + place + G)
                act.wait_ge(stored, w * 16)
                act.activation(rows[:, ds(w % 2, 1), :], ps[:, 0:NP], ACT.Copy)
                act.activation(k.cnt8[:, ds(w, 1), :], ps[:, NP:NP + NREL], ACT.Copy).then_inc(copied, 1)

        @block.sync
        def _(sp):
            sp.sem_inc(stored, 16)
            with sp.Fori(0, W) as w:
                sp.wait_ge(copied, w + 1)
                sp.dma_start(k.at[ds(w, 1), :, :].rearrange("w p n -> p (w n)"),
                             rows[:, ds(w % 2, 1), :].rearrange("p a n -> p (a n)")).then_inc(stored, 16)
                wait_alone(sp, stored, w * 16 + 32, passed)


def turn_nodes(nc, k, source, func, name):
    with ExitStack() as ctx:
        sem = lambda n: k.sem(n)
        ps = ctx.enter_context(nc.psum_tensor(f"{name}_ps", [D, 7 * CUT], F32))
        turned, copied = sem(f"{name}_turned"), sem(f"{name}_copied")
        block = ctx.enter_context(nc.Block())

        @block.tensor
        def _(pe):
            for s, (c, wd) in enumerate(SLICES):
                for j in range(wd // P):
                    w = c // P + j
                    last = pe.transpose(ps[:, w * P:(w + 1) * P], source[:, w, :], k.ident[:, :])
                last.then_inc(turned, 1)

        @block.scalar
        def _(act):
            for s, (c, wd) in enumerate(SLICES):
                act.wait_ge(turned, s + 1)
                act.activation(k.xt[0:D, c:c + wd], ps[:, c:c + wd], func).then_inc(copied, 1)

        @block.vector
        def _(v):
            v.memset(k.xt[D:D + 1, :], 1.0)


def conv_features(nc, k, w_out, w_back, name):
    with ExitStack() as ctx:
        sb = lambda n, s, d: ctx.enter_context(nc.sbuf_tensor(f"{name}_{n}", s, d))
        sem = lambda n: k.sem(f"{name}_{n}")
        wt = sb("wt", [D, 2 * D], F32)
        stats = sb("stats", [D, len(SLICES), 6], F32)
        mv = sb("mv", [D, 2], F32)
        eps = sb("eps", [D, 1], F32)
        std = sb("std", [D, 1], F32)
        scale = sb("scale", [D, 2], F32)
        rest = sb("rest", [P, W * 2 * D], F32)
        ps = ctx.enter_context(nc.psum_tensor(f"{name}_ps", [P, 7 * CUT], F32))
        loaded, own_v, var_ok, std_ok, normed, products, copied = map(
            sem, ("loaded", "own", "var_ok", "std_ok", "normed", "products", "copied"))
        block = ctx.enter_context(nc.Block())

        @block.sync
        def _(sp):
            sp.dma_start(wt[:, 0:D], w_out[:, :]).then_inc(loaded, 16)
            sp.dma_start(wt[:, D:2 * D], w_back[:, :]).then_inc(loaded, 16)

        @block.vector
        def _(v):
            own = Own(v, own_v)
            for s, (c, wd) in enumerate(SLICES):
                own.did(v.bn_stats(stats[:, s, :], k.xt[0:D, c:min(c + wd, N)]))
            own.did(v.memset(eps[:, :], EPS))
            own.wait()
            own.do(v.bn_aggr(mv[:, :], stats[:, :, :].rearrange("p a b -> p (a b)")))
            v.sem_inc(var_ok, 1)
            v.wait_ge(std_ok, 1)
            own.do(v.reciprocal(scale[:, 0:1], std[:, :]))
            own.do(v.scalar_tensor_tensor(scale[:, 1:2], mv[:, 0:1], -1.0, scale[:, 0:1], ALU.mult, ALU.mult))
            v.tensor_scalar(k.xt[0:D, :], k.xt[0:D, :], scale[:, 0:1], scale[:, 1:2],
                            ALU.mult, ALU.add).then_inc(normed, 1)
            v.wait_ge(copied, len(SLICES))
            y = k.y[:, :, :, :].rearrange("p w c d -> p w (c d)")
            left = y
            r = rest[:, :].rearrange("p (w d) -> p w d", w=W)
            for part in range(3):
                for c in range(2):
                    own.did(v.tensor_copy(k.parts[:, :, c, part, :], left[:, :, c * D:(c + 1) * D]))
                own.wait()
                if part < 2:
                    for c in range(2):
                        own.did(v.tensor_tensor(r[:, :, c * D:(c + 1) * D], left[:, :, c * D:(c + 1) * D],
                                                k.parts[:, :, c, part, :], ALU.subtract))
                    own.wait()
                    left = r

        @block.scalar
        def _(act):
            act.wait_ge(var_ok, 1)
            act.activation(std[:, :], mv[:, 1:2], ACT.Sqrt, bias=eps[:, 0:1]).then_inc(std_ok, 1)
            for s, (c, wd) in enumerate(SLICES):
                act.wait_ge(products, s + 1)
                act.activation(k.y[:, c // P:(c + wd) // P, :, :].rearrange("p w c d -> p (w c d)"),
                               ps[:, c:c + wd], ACT.Copy).then_inc(copied, 1)

        @block.tensor
        def _(pe):
            pe.wait_ge(loaded, 32)
            pe.wait_ge(normed, 1)
            for s, (c, wd) in enumerate(SLICES):
                for j in range(wd // P):
                    o = c + j * P
                    last = pe.matmul(ps[:, o:o + P], k.xt[0:D, o:o + P], wt[:, :], start=True, stop=True)
                last.then_inc(products, 1)


def conv_sums(nc, k, first, name):
    with ExitStack() as ctx:
        sb = lambda n, s, d: ctx.enter_context(nc.sbuf_tensor(f"{name}_{n}", s, d))
        sem = lambda n: k.sem(f"{name}_{n}")
        rows = [sb(f"rows{u}", [P, NP], BF16) for u in range(2)]
        panel = [sb(f"panel{u}", [P, W, P], BF16) for u in range(2)]
        edge = sb("edge", [P, W, P], BF16)
        seen = sb("seen", [P, W], F32)
        zero = sb("zero", [P, CUT], BF16)
        by_src = ctx.enter_context(nc.psum_tensor(f"{name}_src", [P, 4 * CUT], F32))
        by_dst = [ctx.enter_context(nc.psum_tensor(f"{name}_dst{u}", [P, CUT], F32)) for u in range(2)]
        tps = [ctx.enter_context(nc.psum_tensor(f"{name}_t{u}", [P, 2 * CUT], BF16)) for u in range(2)]
        blank = sem("blank")
        rows_in = [sem(f"rows_in{u}") for u in range(2)]
        panel_in = [sem(f"panel_in{u}") for u in range(2)]
        panel_out = [sem(f"panel_out{u}") for u in range(2)]
        turned, copied, own_v, summed, read, panel_free = map(
            sem, ("turned", "copied", "own", "summed", "read", "panel_free"))
        block = ctx.enter_context(nc.Block())
        GRP = [(b, min(8, W - b)) for b in range(0, W, 8)]
        NG = len(GRP)

        def windows(eng, body):
            with eng.Fori(0, W - 1, 2) as w:
                body(w, 0)
                body(w + 1, 1)
            body(W - 1, 0)

        @block.sync
        def _(sp):
            def load(w, u):
                sp.wait_ge(summed, w + 1)
                sp.dma_start(rows[u][:, :], k.at[ds(w, 1), :, :].rearrange("w p n -> p (w n)")
                             ).then_inc(rows_in[u], 16)
                if not first:
                    sp.dma_start(panel[u][:, :, :], k.a[ds(w, 1), :, :, :].rearrange("w p k d -> p (w k) d")
                                 ).then_inc(panel_in[u], 16)
            windows(sp, load)

        @block.tensor
        def _(pe):
            pe.sem_inc(summed, 2)
            pe.wait_ge(blank, 1)
            for b in range(4):
                pe.matmul(by_src[:, b * CUT:(b + 1) * CUT], zero[:, 0:P], zero[:, :], start=True, stop=True,
                          skip_group_check=True)

            def window(w, u):
                pe.wait_ge(rows_in[u], (w - u) * 8 + 16)

                def turn(g):
                    b, n = GRP[g]
                    pe.wait_ge(copied, w * NG + g + 1)
                    for j in range(n):
                        last = pe.transpose(tps[g % 2][:, j * P:(j + 1) * P],
                                            rows[u][:, (b + j) * P:(b + j + 1) * P], k.identb[:, :])
                    last.then_inc(turned, 1)

                def back(blocks):
                    for b in blocks:
                        for part in range(3):
                            last = pe.matmul(by_src[:, b * D:(b + 1) * D], rows[u][:, b * P:(b + 1) * P],
                                             k.parts[:, ds(w, 1), 1, part, :], start=False, stop=True,
                                             skip_group_check=True)
                    return last

                cuts = [0, 7, 14, 20, W]
                for g in range(NG):
                    if first:
                        turn(g)
                    back(range(cuts[g], cuts[g + 1]))
                if first:
                    pe.wait_ge(copied, (w + 1) * NG + 2)
                else:
                    pe.wait_ge(panel_in[u], (w - u) * 8 + 16)
                pe.wait_ge(read, w + 1)
                for b in range(W):
                    last = pe.matmul(by_dst[u][:, 0:3 * D], panel[u][:, b, :],
                                     k.parts[:, b, 0, :, :].rearrange("p a d -> p (a d)"),
                                     start=(b == 0), stop=(b == W - 1))
                last.then_inc(summed, 1)
            windows(pe, window)

        @block.scalar
        def _(act):
            if not first:
                return
            act.sem_inc(copied, 2)
            for u in range(2):
                act.sem_inc(panel_out[u], 16)

            def window(w, u):
                act.wait_ge(panel_out[u], (w - u) * 8 + 16)
                act.wait_ge(summed, w + 1)
                act.wait_ge(panel_free, w + 1)
                for g, (b, n) in enumerate(GRP):
                    act.wait_ge(turned, w * NG + g + 1)
                    act.activation(panel[u][:, b:b + n, :].rearrange("p a d -> p (a d)"),
                                   tps[g % 2][:, 0:n * P], ACT.Copy).then_inc(copied, 1)
                act.wait_ge(copied, (w + 1) * NG + 2)
                act.dma_start(k.a[ds(w, 1), :, :, :].rearrange("w p k d -> p (w k) d"),
                              panel[u][:, :, :]).then_inc(panel_out[u], 16)
            windows(act, window)
            act.wait_ge(panel_out[0], 16 * (W // 2 + 2))
            act.wait_ge(panel_out[1], 16 * (W // 2 + 1))

        @block.vector
        def _(v):
            own = Own(v, own_v)
            if first:
                own.did(v.memset(k.uniq[:, :], 0.0))
            own.did(v.memset(zero[:, :], 0.0))
            own.wait()
            v.sem_inc(blank, 1)
            v.sem_inc(read, 2)
            v.sem_inc(panel_free, 2)
            begun = own.n
            steps = 4 if first else 1

            def window(w, u):
                own.at(w * steps + begun)
                if first:
                    v.wait_ge(copied, (w + 1) * NG + 2)
                    own.did(v.tensor_scalar(edge[:, :, :], panel[u][:, :, :], 1.0, None, ALU.min))
                    own.wait()
                    v.sem_inc(panel_free, 1)
                    own.do(v.tensor_reduce(seen[:, :], edge[:, :, :], AX.X, ALU.add))
                    own.do(v.tensor_tensor(k.uniq[:, :], k.uniq[:, :], seen[:, :], ALU.add))
                v.wait_ge(summed, w + 3)
                own.do(v.tensor_reduce(k.agg[:, ds(w, 1), 0, :],
                                       by_dst[u][:, 0:3 * D].rearrange("p (a d) -> p d a", a=3), AX.X, ALU.add))
                v.sem_inc(read, 1)
            windows(v, window)
            v.wait_ge(summed, W + 2)
            v.tensor_copy(k.agg[:, :, 1, :], by_src[:, 0:W * D].rearrange("p (w d) -> p w d", w=W)).then_inc(read, 1)


def conv_result(nc, k, name):
    with ExitStack() as ctx:
        sb = lambda n, s, d: ctx.enter_context(nc.sbuf_tensor(f"{name}_{n}", s, d))
        sem = lambda n: k.sem(f"{name}_{n}")
        deg = sb("deg", [P, W], F32)
        root = sb("root", [P, W], F32)
        norm = sb("norm", [P, W], F32)
        own_v, deg_ok, root_ok = map(sem, ("own", "deg_ok", "root_ok"))
        block = ctx.enter_context(nc.Block())

        @block.vector
        def _(v):
            own = Own(v, own_v)
            own.do(v.tensor_reduce(deg[:, :], k.cnt8[:, :, :], AX.X, ALU.add))
            own.do(v.tensor_scalar(deg[:, :], deg[:, :], 1.0, None, ALU.max))
            v.sem_inc(deg_ok, 1)
            own.do(v.tensor_tensor(k.agg[:, :, :, :], k.agg[:, :, :, :], k.y[:, :, :, :], ALU.add))
            v.wait_ge(root_ok, 1)
            own.do(v.reciprocal(norm[:, :], root[:, :]))
            for c, by in enumerate((norm, k.vec)):
                own.did(v.tensor_tensor(k.agg[:, :, c, :], k.agg[:, :, c, :],
                                        by[:, :].unsqueeze(2).broadcast_to([P, W, D]), ALU.mult))
            own.wait()
            own.do(v.tensor_tensor(k.z[:, :, :], k.agg[:, :, 0, :], k.agg[:, :, 1, :], ALU.add))

        @block.scalar
        def _(act):
            act.wait_ge(deg_ok, 1)
            act.activation(root[:, :], deg[:, :], ACT.Sqrt).then_inc(root_ok, 1)


def add_and_norm(nc, k, scale, name):
    with ExitStack() as ctx:
        sb = lambda n, s, d: ctx.enter_context(nc.sbuf_tensor(f"{name}_{n}", s, d))
        sem = lambda n: k.sem(f"{name}_{n}")
        mean = sb("mean", [P, W], F32)
        var = sb("var", [P, W], F32)
        sq = sb("sq", [P, W, D], F32)
        eps = sb("eps", [P, 1], F32)
        own_v, var_ok, std_ok = map(sem, ("own", "var_ok", "std_ok"))
        block = ctx.enter_context(nc.Block())
        wide = lambda t: t[:, :].unsqueeze(2).broadcast_to([P, W, D])

        @block.vector
        def _(v):
            own = Own(v, own_v)
            own.did(v.memset(eps[:, :], EPS))
            own.do(v.scalar_tensor_tensor(k.x[:, :, :], k.x[:, :, :], float(scale), k.z[:, :, :],
                                          ALU.mult, ALU.add))
            own.do(v.tensor_reduce(mean[:, :], k.x[:, :, :], AX.X, ALU.add))
            own.do(v.tensor_scalar(mean[:, :], mean[:, :], 1.0 / D, None, ALU.mult))
            own.do(v.tensor_tensor(k.x[:, :, :], k.x[:, :, :], wide(mean), ALU.subtract))
            own.do(v.tensor_tensor(sq[:, :, :], k.x[:, :, :], k.x[:, :, :], ALU.mult))
            own.do(v.tensor_reduce(var[:, :], sq[:, :, :], AX.X, ALU.add))
            v.sem_inc(var_ok, 1)
            v.wait_ge(std_ok, 1)
            own.do(v.reciprocal(var[:, :], var[:, :]))
            own.do(v.tensor_tensor(k.x[:, :, :], k.x[:, :, :], wide(var), ALU.mult))

        @block.scalar
        def _(act):
            act.wait_ge(var_ok, 1)
            act.activation(var[:, :], var[:, :], ACT.Sqrt, bias=eps[:, 0:1], scale=1.0 / D).then_inc(std_ok, 1)


def edge_features(nc, k, w1, b1):
    with ExitStack() as ctx:
        sb = lambda n, s, d: ctx.enter_context(nc.sbuf_tensor(f"ef_{n}", s, d))
        sem = lambda n: k.sem(f"ef_{n}")
        wt = sb("wt", [D + 1, 2, 2 * D], F32)
        qs = sb("qs", [P, W, 2 * D], F32)
        most = sb("most", [P, 1], F32)
        top = sb("top", [1, 2], F32)
        rnd = sb("rnd", [1, 1], I32)
        ps = [ctx.enter_context(nc.psum_tensor(f"ef_ps{u}", [P, CUT], F32)) for u in range(4)]
        pt = ctx.enter_context(nc.psum_tensor("ef_pt", [1, CUT], F32))
        loaded, own_v, wt_ok, most_ok, most_t, products, kept, rounds_ok, stored = map(
            sem, ("loaded", "own", "wt_ok", "most_ok", "most_t", "products", "kept", "rounds_ok", "stored"))
        block = ctx.enter_context(nc.Block())
        H = 2 * D
        PAIRS = [(w, min(2, W - w)) for w in range(0, W, 2)]

        @block.sync
        def _(sp):
            sp.dma_start(wt[0:D, 0, :], w1[0:D, :]).then_inc(loaded, 16)
            sp.dma_start(wt[0:D, 1, :], w1[D:2 * D, :]).then_inc(loaded, 16)
            sp.dma_start(wt[D:D + 1, 0, :], b1.rearrange("(a n) -> a n", a=1)).then_inc(loaded, 16)
            sp.wait_ge(rounds_ok, 1)
            sp.dma_start(k.rounds[:, :], rnd[:, :]).then_inc(stored, 16)
            sp.wait_ge(kept, len(PAIRS))
            sp.dma_start(k.q.rearrange("(w p) h -> p w h", p=P), qs[:, :, :]).then_inc(stored, 16)
            sp.wait_ge(stored, 32)

        @block.vector
        def _(v):
            own = Own(v, own_v)
            own.did(v.memset(wt[D:D + 1, 1, :], 0.0))
            own.do(v.tensor_reduce(most[:, :], k.uniq[:, :], AX.X, ALU.max))
            v.sem_inc(most_ok, 1)
            v.wait_ge(loaded, 48)
            own.do(v.tensor_tensor(wt[0:D, 0, :], wt[0:D, 0, :], wt[0:D, 1, :], ALU.subtract))
            v.sem_inc(wt_ok, 1)
            v.wait_ge(most_t, 1)
            own.do(v.tensor_reduce(top[:, 0:1], pt[:, 0:P], AX.X, ALU.max))
            own.do(v.tensor_scalar(top[:, 1:2], top[:, 0:1], 7.0, 8.0, ALU.add, ALU.max))
            own.do(v.tensor_copy(rnd[:, :], top[:, 1:2]))
            own.do(v.tensor_scalar(rnd[:, :], rnd[:, :], 3, None, ALU.arith_shift_right))
            v.sem_inc(rounds_ok, 1)

        @block.tensor
        def _(pe):
            pe.wait_ge(most_ok, 1)
            pe.transpose(pt[:, 0:P], most[:, :], k.ident[:, :]).then_inc(most_t, 1)
            pe.wait_ge(wt_ok, 1)
            for n, (w, m) in enumerate(PAIRS):
                if n >= 4:
                    pe.wait_ge(kept, n - 3)
                for j in range(m):
                    last = pe.matmul(ps[n % 4][:, j * 2 * H:(j + 1) * 2 * H],
                                     k.xt[:, (w + j) * P:(w + j + 1) * P],
                                     wt[:, :, :].rearrange("p a h -> p (a h)"), start=True, stop=True)
                last.then_inc(products, 1)

        @block.scalar
        def _(act):
            for n, (w, m) in enumerate(PAIRS):
                act.wait_ge(products, n + 1)
                both = ps[n % 4][:, 0:m * 2 * H].rearrange("p (j a h) -> p j a h", j=m, a=2)
                act.activation(k.p[:, w:w + m, :], both[:, :, 0, :], ACT.Copy)
                act.activation(qs[:, w:w + m, :], both[:, :, 1, :], ACT.Copy).then_inc(kept, 1)


def edge_maxima(nc, k, w2, b2):
    with ExitStack() as ctx:
        sb = lambda n, s, d: ctx.enter_context(nc.sbuf_tensor(f"em_{n}", s, d))
        sem = lambda n: k.sem(f"em_{n}")
        H = 2 * D
        Q = 4
        MAXR = -(-NP // 8)
        place = sb("place", [P, NP], I16)
        raw = sb("raw", [P, W, P], BF16)
        left = sb("left", [P, NP], I16)
        top = sb("top", [P, 8], F32)
        first = sb("first", [P, 1], F32)
        none = sb("none", [P, 8], F32)
        idx = sb("idx", [P, 2, MAXR * 8], I32)
        got = [sb(f"got{q}", [P, 2, H], F32) for q in range(Q)]
        now = [sb(f"now{q}", [P, 2], I32) for q in range(Q)]
        hid = [sb(f"hid{q}", [P, 2 * P], F32) for q in range(Q)]
        ident2 = sb("ident2", [P, 2, P], F32)
        pw = sb("pw", [P, H], F32)
        w2s = sb("w2s", [P, D], F32)
        b2s = sb("b2s", [P, D], F32)
        best = sb("best", [P, D], F32)
        red = sb("red", [P, 2, D], F32)
        has = sb("has", [P, W], F32)
        tps = [ctx.enter_context(nc.psum_tensor(f"em_t{q}", [P, CUT], F32)) for q in range(Q)]
        ops = [ctx.enter_context(nc.psum_tensor(f"em_o{u}", [P, CUT], F32)) for u in range(2)]
        consts, found, raw_in, raw_free, own_v, own_x = map(
            sem, ("consts", "found", "raw_in", "raw_free", "own", "own_x"))
        mid = sem("mid")
        gat = [sem(f"gat{q}") for q in range(Q)]
        taken = [sem(f"taken{q}") for q in range(Q)]
        now_ok = [sem(f"now_ok{q}") for q in range(Q)]
        lined = [sem(f"lined{q}") for q in range(Q)]
        outs = [sem(f"outs{u}") for u in range(2)]
        read = [sem(f"read{u}") for u in range(2)]
        p_ok = sem("p_ok")
        passed = [sem(f"passed{e}") for e in range(3)]
        block = ctx.enter_context(nc.Block())

        def number_of_rounds(eng):
            return eng.value_load(k.rounds[0:1, 0:1], min_val=1, max_val=MAXR)

        @block.sync
        def _(sp):
            sp.dma_start(w2s[:, :], w2[:, :]).then_inc(consts, 16)
            sp.dma_start(b2s[:, :], b2.rearrange("(a n) -> a n", a=1).broadcast_to([P, D])).then_inc(consts, 16)
            with sp.Fori(0, W) as w:
                sp.wait_ge(raw_free, w)
                sp.dma_start(raw[:, :, :], k.a[:, :, ds(w, 1), :].rearrange("a p k d -> p a (k d)")
                             ).then_inc(raw_in, 16)

        @block.gpsimd
        def _(pool):
            pool.iota(place[:, :], pattern=[[-1, NP]], base=NP, channel_multiplier=0,
                      allow_small_or_imprecise_dtypes=True).then_inc(consts, 1)
            rounds = number_of_rounds(pool)
            with pool.Fori(0, W) as w:
                with pool.Fori(0, rounds) as r:
                    g = pool.snap(w * rounds + r)
                    pool.wait_ge(found, g + 1)
                    for q in range(Q):
                        pool.wait_ge(taken[q], g + 1)
                        pool.tensor_copy(now[q][:, :], idx[:, ds(w % 2, 1), ds(r * 8 + 2 * q, 2)]
                                         .rearrange("p a b -> p (a b)")).then_inc(now_ok[q], 1)
                        wait_alone(pool, now_ok[q], g + 1, passed[0])
                        for j in range(2):
                            pool.indirect_dma_start(
                                out=got[q][:, j, :], out_offset=None, in_=k.q[:, :],
                                in_offset=bass.IndirectOffsetOnAxis(ap=now[q][:, j:j + 1], axis=0)
                            ).then_inc(gat[q], 16)

        @block.vector
        def _(v):
            own = Own(v, own_v)
            for j in range(2):
                own.did(v.tensor_copy(ident2[:, j, :], k.ident[:, :]))
            own.do(v.tensor_scalar(has[:, :], k.uniq[:, :], 0.0, None, ALU.is_gt))
            v.sem_inc(consts, 1)
            v.wait_ge(consts, 34)
            rounds = number_of_rounds(v)
            begun = own.n
            x = Own(v, own_x)

            def window_find(w, r, base):
                x.at(base)
                x.do(v.max(top[:, :], left[:, :]))
                x.did(v.scalar_tensor_tensor(left[:, :], left[:, :], top[:, 7:8], left[:, :],
                                             ALU.is_lt, ALU.mult))
                x.did(v.tensor_tensor(first[:, :], first[:, :], top[:, 0:1], ALU.max))
                x.do(v.tensor_scalar(none[:, :], top[:, :], 0.0, None, ALU.is_equal))
                x.do(v.scalar_tensor_tensor(none[:, :], none[:, :], first[:, :], top[:, :],
                                            ALU.mult, ALU.add))
                x.do(v.tensor_scalar(idx[:, ds(w % 2, 1), ds(r * 8, 8)].rearrange("p a b -> p (a b)"),
                                     none[:, :], -1.0, float(NP), ALU.mult, ALU.add))
                v.sem_inc(found, 1)
            STEPS = 6

            def window_begin(w, base):
                x.at(base)
                v.wait_ge(raw_in, (w + 1) * 16)
                x.did(v.scalar_tensor_tensor(left[:, :], raw[:, :, :].rearrange("p a d -> p (a d)"), 0.0,
                                             place[:, :], ALU.is_gt, ALU.mult))
                x.did(v.memset(first[:, :], 1.0))
                x.wait()
                v.sem_inc(raw_free, 1)
            BEGIN = 2

            def reduce(w, g, rbase):
                own.at(rbase)
                for u in range(2):
                    v.wait_ge(outs[u], g + 1)
                    own.did(v.tensor_reduce(red[:, u, :], ops[u][:, 0:4 * D].rearrange("p (k d) -> p d k", k=4),
                                            AX.X, ALU.max))
                own.wait()
                for u in range(2):
                    v.sem_inc(read[u], 1)
                    own.do(v.tensor_tensor(best[:, :], best[:, :], red[:, u, :], ALU.max))
            RED = 4

            for u in range(2):
                v.sem_inc(read[u], 1)
            window_begin(0, 0)
            with v.Fori(0, rounds) as r:
                window_find(0, r, r * STEPS + BEGIN)

            per = v.snap(rounds * STEPS + BEGIN)
            perr = v.snap(rounds * RED + 3)

            def close(w, base):
                own.at(base)
                own.do(v.tensor_tensor(best[:, :], best[:, :], b2s[:, :], ALU.add))
                own.do(v.tensor_scalar(k.z[:, ds(w, 1), :].rearrange("p a d -> p (a d)"), best[:, :],
                                       has[:, ds(w, 1)], None, ALU.mult))
                v.sem_inc(passed[2], 1)

            def open_(base):
                own.at(base)
                own.did(v.memset(best[:, :], -3.0e38))
                wait_alone(v, own_v, own.base + own.n, passed[2])

            with v.Fori(0, W - 1) as w:
                xb = v.snap((w + 1) * per)
                ob = v.snap(w * perr + begun)
                window_begin(w + 1, xb)
                open_(ob)
                with v.Fori(0, rounds) as r:
                    window_find(w + 1, r, xb + r * STEPS + BEGIN)
                    reduce(w, w * rounds + r, ob + r * RED + 1)
                close(w, ob + rounds * RED + 1)
            ob = v.snap((W - 1) * perr + begun)
            open_(ob)
            with v.Fori(0, rounds) as r:
                reduce(W - 1, (W - 1) * rounds + r, ob + r * RED + 1)
            close(W - 1, ob + rounds * RED + 1)

        @block.tensor
        def _(pe):
            for q in range(Q):
                pe.sem_inc(taken[q], 1)
            pe.wait_ge(consts, 34)
            rounds = number_of_rounds(pe)
            with pe.Fori(0, W) as w:
                wait_alone(pe, p_ok, w + 1, passed[1])
                with pe.Fori(0, rounds) as r:
                    g = pe.snap(w * rounds + r)

                    def turn(q):
                        pe.wait_ge(gat[q], (g + 1) * 32)
                        for j in range(2):
                            last = pe.matmul(tps[q][:, j * P:(j + 1) * P], got[q][:, j, :], k.ident[:, :],
                                             start=(j == 0), stop=False, skip_group_check=True)
                        pe.matmul(tps[q][:, 0:2 * P], pw[:, :], ident2[:, :, :].rearrange("p a b -> p (a b)"),
                                  start=False, stop=True, skip_group_check=True).then_inc(taken[q], 1)

                    def multiply(q):
                        pe.wait_ge(lined[q], g + 1)
                        u = q // 2
                        if q % 2 == 0:
                            pe.wait_ge(read[u], g + 1)
                        for j in range(2):
                            o = ((q % 2) * 2 + j) * D
                            last = pe.matmul(ops[u][:, o:o + D], hid[q][:, j * P:(j + 1) * P], w2s[:, :],
                                             start=True, stop=True, skip_group_check=True)
                        last.then_inc(outs[u] if q % 2 else mid, 1)
                    turn(0)
                    turn(1)
                    multiply(0)
                    turn(2)
                    multiply(1)
                    turn(3)
                    multiply(2)
                    multiply(3)

        @block.scalar
        def _(act):
            rounds = number_of_rounds(act)
            with act.Fori(0, W) as w:
                for q in range(Q):
                    act.wait_ge(taken[q], w * rounds + 1)
                act.activation(pw[:, :], k.p[:, ds(w, 1), :].rearrange("p a h -> p (a h)"),
                               ACT.Copy).then_inc(p_ok, 1)
                with act.Fori(0, rounds) as r:
                    g = act.snap(w * rounds + r)
                    for q in range(Q):
                        act.wait_ge(taken[q], g + 2)
                        if q % 2:
                            act.wait_ge(outs[q // 2], g)
                        else:
                            act.wait_ge(mid, 2 * g)
                        act.activation(hid[q][:, :], tps[q][:, 0:2 * P], ACT.Relu).then_inc(lined[q], 1)


def attention_features(nc, k, wq, bq, wk, bk, wv, bv, ws, bs, name):
    with ExitStack() as ctx:
        sb = lambda n, s, d: ctx.enter_context(nc.sbuf_tensor(f"{name}_{n}", s, d))
        sem = lambda n: k.sem(f"{name}_{n}")
        H = 2 * D
        wqk = sb("wqk", [D + 1, 2, 2, 2, D], F32)
        wvs = sb("wvs", [D + 1, H + D], F32)
        rest = [sb(f"rest{u}", [P, CUT], F32) for u in range(2)]
        ps = [ctx.enter_context(nc.psum_tensor(f"{name}_ps{u}", [P, CUT], F32)) for u in range(8)]
        loaded, products, copied, first, second, less, split = map(
            sem, ("loaded", "products", "copied", "first", "second", "less", "split"))
        block = ctx.enter_context(nc.Block())
        row = lambda b: b.rearrange("(a n) -> a n", a=1)
        heads = lambda m: m.rearrange("p (h d) -> p h d", h=2)
        QK = [(t, h, c, wd) for t in range(2) for h in range(2) for c, wd in SLICES]
        VS = [(w, min(2, W - w)) for w in range(0, W, 2)]
        KV = H + D
        NQK = len(QK)

        def free(eng, n):
            if n >= 8:
                if n - 8 < NQK:
                    eng.wait_ge(less, n - 7)
                else:
                    eng.wait_ge(copied, n - 8 - NQK + 1)

        @block.sync
        def _(sp):
            for u in range(2):
                for t, (m, b) in enumerate(((wq, bq), (wk, bk))):
                    sp.dma_start(wqk[0:D, t, :, u, :], heads(m[:, :])).then_inc(loaded, 16)
                    sp.dma_start(wqk[D:D + 1, t, :, u, :], heads(row(b))).then_inc(loaded, 16)
            for dst, src in ((wvs[0:D, 0:H], wv[:, :]), (wvs[D:D + 1, 0:H], row(bv)),
                             (wvs[0:D, H:KV], ws[:, :]), (wvs[D:D + 1, H:KV], row(bs))):
                sp.dma_start(dst, src).then_inc(loaded, 16)

        @block.tensor
        def _(pe):
            pe.wait_ge(loaded, 16 * 12)
            n = 0
            for t, h, c, wd in QK:
                free(pe, n)
                pe.matmul(ps[n % 8][:, 0:wd], wqk[:, t, h, :, :].rearrange("p u d -> p (u d)"), k.xt[:, c:c + wd],
                          start=True, stop=True).then_inc(products, 1)
                n += 1
            for w, m in VS:
                free(pe, n)
                for j in range(m):
                    last = pe.matmul(ps[n % 8][:, j * KV:(j + 1) * KV], k.xt[:, (w + j) * P:(w + j + 1) * P],
                                     wvs[:, :], start=True, stop=True)
                last.then_inc(products, 1)
                n += 1

        @block.scalar
        def _(act):
            def second_part(n):
                t, h, c, wd = QK[n]
                act.wait_ge(less, n + 1)
                lo = 0 if t else D
                out = k.k_22 if t else k.q_12
                act.activation(out[lo:P, h, c:c + wd], rest[n % 2][lo:P, 0:wd], ACT.Copy).then_inc(second, 1)

            for n, (t, h, c, wd) in enumerate(QK):
                act.wait_ge(products, n + 1)
                act.activation((k.k_11 if t else k.q_12)[:, h, c:c + wd], ps[n % 8][:, 0:wd], ACT.Copy,
                               scale=1.0 if t else D ** -0.5).then_inc(first, 1)
                if n >= 1:
                    second_part(n - 1)
            second_part(NQK - 1)
            for i, (w, m) in enumerate(VS):
                n = NQK + i
                act.wait_ge(products, n + 1)
                both = ps[n % 8][:, 0:m * KV].rearrange("p (j c) -> p j c", j=m)
                for h in range(2):
                    act.activation(k.va[:, w:w + m, h, 0:D], both[:, :, h * D:(h + 1) * D], ACT.Copy)
                act.activation(k.z[:, w:w + m, :], both[:, :, H:KV], ACT.Copy).then_inc(copied, 1)

        @block.vector
        def _(v):
            v.memset(k.va[:, :, :, D:D + 1], 1.0)

            def remainder(n):
                t, h, c, wd = QK[n]
                v.wait_ge(first, n + 1)
                if n >= 2:
                    v.wait_ge(split, n - 1)
                v.scalar_tensor_tensor(rest[n % 2][:, 0:wd], ps[n % 8][:, 0:wd], 1.0 if t else D ** -0.5,
                                       (k.k_11 if t else k.q_12)[:, h, c:c + wd],
                                       ALU.mult, ALU.subtract).then_inc(less, 1)

            def third_part(n):
                t, h, c, wd = QK[n]
                v.wait_ge(second, n + 1)
                own, other = (slice(0, D), slice(D, P)) if t else (slice(D, P), slice(0, D))
                third, one = (k.k_31, k.k_11) if t else (k.q_13, k.q_12)
                two = k.k_22 if t else k.q_12
                v.tensor_copy(third[other, h, c:c + wd], one[other, h, c:c + wd])
                v.tensor_tensor(third[own, h, c:c + wd], rest[n % 2][own, 0:wd], two[own, h, c:c + wd],
                                ALU.subtract).then_inc(split, 1)

            for n in range(NQK):
                remainder(n)
                if n >= 1:
                    third_part(n - 1)
            third_part(NQK - 1)


def attention(nc, k, name):
    with ExitStack() as ctx:
        sb = lambda n, s, d: ctx.enter_context(nc.sbuf_tensor(f"{name}_{n}", s, d))
        sem = lambda n: k.sem(f"{name}_{n}")
        rows = sb("rows", [P, NP], BF16)
        no_row = [sb(f"no_row{u}", [P, NP], BF16) for u in range(2)]
        panel = [sb(f"panel{u}", [P, W * P], BF16) for u in range(2)]
        ones = sb("ones", [3, P], BF16)
        parts = sb("parts", [P, 3, 2], BF16)
        rest = sb("rest", [P, 2], F32)
        mrow = [sb(f"mrow{u}", [3, 2, P], BF16) for u in range(2)]
        most = sb("most", [P, 2, len(SLICES)], F32)
        top = sb("top", [P, 2], F32)
        some = sb("some", [P, 2], F32)
        GRP = [(b, min(4, W - b)) for b in range(0, W, 4)]
        ex = [sb(f"ex{u}", [P, 4 * P], F32) for u in range(2)]
        exc = [sb(f"exc{u}", [P, 4 * P], F32) for u in range(2)]
        den = sb("den", [P, 2], F32)
        sps = [ctx.enter_context(nc.psum_tensor(f"{name}_s{u}", [P, CUT], F32)) for u in range(2)]
        tps = [ctx.enter_context(nc.psum_tensor(f"{name}_t{u}", [P, CUT], F32)) for u in range(2)]
        mps = ctx.enter_context(nc.psum_tensor(f"{name}_m", [P, CUT], F32))
        ops = [ctx.enter_context(nc.psum_tensor(f"{name}_o{u}", [P, CUT], F32)) for u in range(2)]
        rows_in, own_v, masked, scored, maxed, top_ok, top_t, m_ok = map(
            sem, ("rows_in", "own", "masked", "scored", "maxed", "top_ok", "top_t", "m_ok"))
        panel_in = [sem(f"panel_in{u}") for u in range(2)]
        shifted, expd, weighed, summed, done = map(sem, ("shifted", "expd", "weighed", "summed", "done"))
        block = ctx.enter_context(nc.Block())
        PART = [(h, c, wd) for h in range(2) for c, wd in SLICES]
        UNIT = [(h, b, n) for h in range(2) for b, n in GRP]
        NPT, NU = len(PART), len(UNIT)
        BESIDE = [[i for i in range(NPT) if i * (NU - 2) // NPT == g] for g in range(NU)]

        def windows(eng, body):
            with eng.Fori(0, W - 3, 2) as w:
                body(w, 0, True, True)
                body(w + 1, 1, True, True)
            body(W - 3, 0, True, True)
            body(W - 2, 1, True, False)
            body(W - 1, 0, False, False)

        @block.sync
        def _(sp):
            def load_rows(w):
                sp.dma_start(rows[:, :], k.at[ds(w, 1), :, :].rearrange("w p n -> p (w n)")).then_inc(rows_in, 16)

            def load_panel(w, u):
                sp.dma_start(panel[u][:, :], k.a[ds(w, 1), :, :, :].rearrange("w p k d -> p (w k d)")
                             ).then_inc(panel_in[u], 16)

            load_rows(0)
            load_panel(0, 0)
            load_panel(1, 1)
            sp.wait_ge(masked, 1)
            load_rows(1)

            def load(w, u, following, after):
                if after:
                    sp.wait_ge(masked, w + 2)
                    load_rows(w + 2)
                    sp.wait_ge(done, w + 3)
                    load_panel(w + 2, u)
            windows(sp, load)

        @block.scalar
        def _(act):
            def maxima(w, u):
                act.wait_ge(top_t, w + 1)
                act.activation(mrow[u][:, :, :], mps[0:3, 0:2 * P].rearrange("p (h d) -> p h d", h=2),
                               ACT.Copy).then_inc(m_ok, 1)

            maxima(0, 0)

            def window(w, u, following, after):
                for i, (h, b, n) in enumerate(UNIT):
                    act.wait_ge(shifted, w * NU + i + 1)
                    act.wait_ge(weighed, w * NU + i + 1)
                    act.activation(ex[i % 2][:, 0:n * P], tps[i % 2][:, 0:n * P], ACT.Exp).then_inc(expd, 1)
                    if i == NU - 2 and following:
                        maxima(w + 1, 1 - u)
            windows(act, window)

        @block.tensor
        def _(pe):
            def score(w, u, i):
                h, c, wd = PART[i]
                if i == 0:
                    pe.wait_ge(masked, w + 1)
                pe.wait_ge(maxed, w * NPT + i + 1)
                for n, (q, key) in enumerate(score_products(k)):
                    pe.matmul(sps[i % 2][:, 0:wd], q[:, h, ds(w * P, P)], key[:, h, c:c + wd],
                              start=(n == 0), stop=False)
                pe.matmul(sps[i % 2][:, 0:wd], k.identb[:, :], no_row[u][:, c:c + wd],
                          start=False, stop=True).then_inc(scored, 1)

            def turn_top(w):
                pe.wait_ge(top_ok, w + 1)
                for h in range(2):
                    last = pe.matmul(mps[0:3, h * P:(h + 1) * P], parts[:, :, h], k.identb[:, :],
                                     start=(h == 0), stop=True, skip_group_check=True)
                last.then_inc(top_t, 1)

            def shift(w, u, i):
                h, b, n = UNIT[i]
                if i == 0:
                    pe.wait_ge(m_ok, w + 1)
                pe.wait_ge(expd, w * NU + i + 1)
                pe.matmul(tps[i % 2][:, 0:n * P], ones[:, :], mrow[u][:, h, :].unsqueeze(1).broadcast_to([3, n, P]),
                          start=True, stop=True, skip_group_check=True)
                for j in range(n):
                    for q, key in score_products(k):
                        last = pe.matmul(tps[i % 2][:, j * P:(j + 1) * P], key[:, h, (b + j) * P:(b + j + 1) * P],
                                         q[:, h, ds(w * P, P)], start=False, stop=True, skip_group_check=True)
                last.then_inc(shifted, 1)

            def sum_up(w, u, i):
                h, b, n = UNIT[i]
                pe.wait_ge(weighed, w * NU + i + 3)
                if i == 0:
                    pe.wait_ge(done, w + 1)
                for j in range(n):
                    last = pe.matmul(ops[u][:, h * 2 * D:h * 2 * D + D + 1], exc[i % 2][:, j * P:(j + 1) * P],
                                     k.va[:, b + j, h, :], start=(i == 0 and j == 0),
                                     stop=True, skip_group_check=True)
                last.then_inc(summed, 1)

            for i in range(NPT):
                score(0, 0, i)
            turn_top(0)

            def window(w, u, following, after):
                for i in range(NU):
                    if following:
                        for part in BESIDE[i]:
                            score(w + 1, 1 - u, part)
                    shift(w, u, i)
                    if i >= 2:
                        sum_up(w, u, i - 2)
                    if i == NU - 2 and following:
                        turn_top(w + 1)
                sum_up(w, u, NU - 2)
                sum_up(w, u, NU - 1)
            windows(pe, window)

        @block.vector
        def _(v):
            for s in (done, expd, weighed, summed, maxed):
                v.sem_inc(s, 2)
            own = Own(v, own_v)

            def mask(w, u):
                v.wait_ge(rows_in, (w + 1) * 16)
                v.tensor_scalar(no_row[u][:, :], rows[:, :], 0.0, NEG, ALU.is_equal, ALU.mult).then_inc(masked, 1)

            def part_max(w, i):
                h, c, wd = PART[i]
                v.wait_ge(scored, w * NPT + i + 1)
                v.tensor_reduce(most[:, h, i % len(SLICES):i % len(SLICES) + 1], sps[i % 2][:, 0:wd],
                                AX.X, ALU.max).then_inc(maxed, 1)

            def find_top(w):
                v.wait_ge(maxed, (w + 1) * NPT + 2)
                own.do(v.tensor_reduce(top[:, :], most[:, :, :], AX.X, ALU.max))
                own.do(v.tensor_scalar(some[:, :], top[:, :], NEG / 2, None, ALU.is_gt))
                own.do(v.scalar_tensor_tensor(top[:, :], top[:, :], -1.0, some[:, :], ALU.mult, ALU.mult))
                own.do(v.tensor_copy(parts[:, 0, :], top[:, :]))
                own.do(v.tensor_tensor(rest[:, :], top[:, :], parts[:, 0, :], ALU.subtract))
                own.do(v.tensor_copy(parts[:, 1, :], rest[:, :]))
                own.do(v.tensor_tensor(parts[:, 2, :], rest[:, :], parts[:, 1, :], ALU.subtract))
                v.sem_inc(top_ok, 1)
            TOP = 7

            def weigh(w, u, i):
                h, b, n = UNIT[i]
                if i == 0:
                    v.wait_ge(panel_in[u], (w - u) * 8 + 16)
                v.wait_ge(expd, w * NU + i + 3)
                v.wait_ge(summed, w * NU + i + 1)
                v.scalar_tensor_tensor(exc[i % 2][:, 0:n * P], ex[i % 2][:, 0:n * P], 1.0,
                                       panel[u][:, b * P:(b + n) * P], ALU.min, ALU.mult).then_inc(weighed, 1)

            def finish(w, u):
                v.wait_ge(summed, (w + 1) * NU + 2)
                own.do(v.tensor_scalar(den[:, :], ops[u][:, 0:4 * D].rearrange("p (h c) -> p h c", h=2)[:, :, D],
                                       1e-16, 2.0, ALU.add, ALU.mult))
                own.do(v.reciprocal(den[:, :], den[:, :]))
                for h in range(2):
                    z = k.z[:, ds(w, 1), :].rearrange("p a d -> p (a d)")
                    own.do(v.scalar_tensor_tensor(z, ops[u][:, h * 2 * D:h * 2 * D + D], den[:, h:h + 1], z,
                                                  ALU.mult, ALU.add))
                v.sem_inc(done, 1)
            FINISH = 4

            v.memset(ones[:, :], 1.0)
            mask(0, 0)
            mask(1, 1)
            for i in range(NPT):
                part_max(0, i)
            find_top(0)

            def window(w, u, following, after):
                own.at(TOP + w * (TOP + FINISH))
                for i in range(NU):
                    if following:
                        for part in BESIDE[i]:
                            part_max(w + 1, part)
                        if i == NU - 2:
                            find_top(w + 1)
                    weigh(w, u, i)
                    if i == 3 and after:
                        mask(w + 2, u)
                finish(w, u)
            windows(v, window)


def relation_features(nc, k, weight, root, bias, name):
    with ExitStack() as ctx:
        sb = lambda n, s, d: ctx.enter_context(nc.sbuf_tensor(f"{name}_{n}", s, d))
        sem = lambda n: k.sem(f"{name}_{n}")
        wt = sb("wt", [D + 1, NREL + 1, D], F32)
        hs = [sb(f"hs{u}", [P, NREL, D], F32) for u in range(4)]
        ps = [ctx.enter_context(nc.psum_tensor(f"{name}_ps{u}", [P, CUT], F32)) for u in range(6)]
        rs = [ctx.enter_context(nc.psum_tensor(f"{name}_rs{u}", [P, CUT], F32)) for u in range(2)]
        loaded, blank, products, kept, rooted = map(sem, ("loaded", "blank", "products", "kept", "rooted"))
        stored = [sem(f"stored{u}") for u in range(4)]
        block = ctx.enter_context(nc.Block())

        @block.sync
        def _(sp):
            sp.dma_start(wt[0:D, 0:NREL, :], weight.rearrange("r d f -> d r f")).then_inc(loaded, 16)
            sp.dma_start(wt[0:D, NREL, :], root[:, :]).then_inc(loaded, 16)
            sp.dma_start(wt[D:D + 1, NREL, :], bias.rearrange("(a n) -> a n", a=1)).then_inc(loaded, 16)
            table = k.h.rearrange("(r w p) d -> w p r d", r=NREL, p=P)
            for w in range(W):
                sp.wait_ge(kept, w + 1)
                sp.dma_start(table[w], hs[w % 4][:, :, :]).then_inc(stored[w % 4], 16)
            for u in range(4):
                sp.wait_ge(stored[u], 16 * len(range(u, W, 4)))

        @block.vector
        def _(v):
            v.memset(wt[D:D + 1, 0:NREL, :], 0.0).then_inc(blank, 1)
            for w in range(W):
                v.wait_ge(rooted, w + 1)
                v.tensor_copy(k.z[:, w, :], rs[w % 2][:, 0:D]).then_inc(blank, 1)

        @block.tensor
        def _(pe):
            pe.wait_ge(loaded, 48)
            pe.wait_ge(blank, 1)
            for w in range(W):
                if w >= 6:
                    pe.wait_ge(kept, w - 5)
                if w >= 2:
                    pe.wait_ge(blank, w)
                at = k.xt[:, w * P:(w + 1) * P]
                pe.matmul(ps[w % 6][:, :], at, wt[:, 0:NREL, :].rearrange("p r d -> p (r d)"),
                          start=True, stop=True).then_inc(products, 1)
                pe.matmul(rs[w % 2][:, 0:D], at, wt[:, NREL, :], start=True, stop=True).then_inc(rooted, 1)

        @block.scalar
        def _(act):
            for w in range(W):
                act.wait_ge(products, w + 1)
                if w >= 4:
                    act.wait_ge(stored[w % 4], 16 * (w // 4))
                act.activation(hs[w % 4][:, :, :].rearrange("p r d -> p (r d)"), ps[w % 6][:, :],
                               ACT.Copy).then_inc(kept, 1)


def relation_sums(nc, k, name):
    with ExitStack() as ctx:
        sb = lambda n, s, d: ctx.enter_context(nc.sbuf_tensor(f"{name}_{n}", s, d))
        sem = lambda n: k.sem(f"{name}_{n}")
        now = [sb(f"now{j}", [P, 1], I32) for j in range(G)]
        got = [sb(f"got{j}", [P, D], F32) for j in range(G)]
        hot = [sb(f"hot{j}", [P, P], F32) for j in range(G)]
        typed = [sb(f"typed{j}", [P, NREL, D], F32) for j in range(G)]
        inv = sb("inv", [P, W, NREL], F32)
        mean = sb("mean", [P, NREL, D], F32)
        total = sb("total", [P, D], F32)
        ps = ctx.enter_context(nc.psum_tensor(f"{name}_ps", [P, CUT], F32))
        gat = [sem(f"gat{j}") for j in range(G)]
        passed = sem("passed")
        now_ok, spread, hots, multiplied, read, own_v = map(
            sem, ("now_ok", "spread", "hots", "multiplied", "read", "own"))
        block = ctx.enter_context(nc.Block())

        @block.gpsimd
        def _(pool):
            pool.sem_inc(now_ok, NT)
            with pool.Fori(0, W) as w:
                first, end, place = window_tiles(pool, k, w)
                with pool.Fori(first, end, G) as t0:
                    at = pool.snap(t0 + place)
                    for j in range(G):
                        pool.wait_ge(spread, at + j + 1)
                        pool.tensor_copy(now[j][:, :], k.msg_row[:, ds(t0 + j, 1)]).then_inc(now_ok, 1)
                        wait_alone(pool, now_ok, at + j + 1, passed)
                        pool.indirect_dma_start(
                            out=got[j][:, :], out_offset=None, in_=k.h[:, :],
                            in_offset=bass.IndirectOffsetOnAxis(ap=now[j][:, 0:1], axis=0)).then_inc(gat[j], 16)

        @block.vector
        def _(v):
            v.sem_inc(spread, NT + G)
            v.sem_inc(hots, NT)
            own = Own(v, own_v)
            own.do(v.tensor_scalar(inv[:, :, :], k.cnt8[:, :, :], 1.0, None, ALU.max))
            own.do(v.reciprocal(inv[:, :, :], inv[:, :, :]))
            begun = own.n
            gathered = v.alloc_register(f"{name}_gathered")
            v.reg_mov(gathered, 16)
            with v.Fori(0, W) as w:
                first, end, place = window_tiles(v, k, w)
                with v.Fori(first, end, G) as t0:
                    at = v.snap(t0 + place)
                    here = v.snap(gathered, min_val=16)
                    for j in range(G):
                        t = t0 + j
                        v.wait_ge(multiplied, at + j + 1)
                        v.tensor_scalar(hot[j][:, :], k.iota_p[:, :], k.wbase[:, ds(w, 1)],
                                        k.dst_t[:, ds(t, 1)], ALU.add, ALU.is_equal).then_inc(hots, 1)
                        v.wait_ge(gat[j], here)
                        v.tensor_tensor(typed[j][:, :, :], got[j][:, :].unsqueeze(1).broadcast_to([P, NREL, D]),
                                        k.type_hot[:, ds(t, 1), :].rearrange("p a r -> p (a r)")
                                        .unsqueeze(2).broadcast_to([P, NREL, D]), ALU.mult).then_inc(spread, 1)
                    v.reg_add(gathered, gathered, 16)
                v.wait_ge(multiplied, end + place + G)
                own.at(w * 3 + begun)
                own.do(v.tensor_tensor(mean[:, :, :], ps[:, :].rearrange("p (r d) -> p r d", r=NREL),
                                       inv[:, ds(w, 1), :].rearrange("p a r -> p (a r)")
                                       .unsqueeze(2).broadcast_to([P, NREL, D]), ALU.mult))
                v.sem_inc(read, 1)
                own.do(v.tensor_reduce(total[:, :], mean[:, :, :].rearrange("p r d -> p d r"), AX.X, ALU.add))
                z = k.z[:, ds(w, 1), :].rearrange("p a d -> p (a d)")
                own.do(v.tensor_tensor(z, z, total[:, :], ALU.add))

        @block.tensor
        def _(pe):
            pe.sem_inc(multiplied, NT + G)

            def tile(t, at, j, fresh):
                pe.wait_ge(hots, at + j + 1)
                pe.wait_ge(spread, at + j + 1 + G)
                pe.matmul(ps[:, :], hot[j][:, :], typed[j][:, :, :].rearrange("p r d -> p (r d)"),
                          start=fresh, stop=True, skip_group_check=True).then_inc(multiplied, 1)

            with pe.Fori(0, W) as w:
                first, end, place = window_tiles(pe, k, w)
                pe.wait_ge(read, w)
                at = pe.snap(first + place)
                for j in range(G):
                    tile(first + j, at, j, j == 0)
                with pe.Fori(first + G, end, G) as t0:
                    at2 = pe.snap(t0 + place)
                    for j in range(G):
                        tile(t0 + j, at2, j, False)


def store_nodes(nc, k, out):
    with ExitStack() as ctx:
        stored = k.sem("out_stored")
        block = ctx.enter_context(nc.Block())

        @block.sync
        def _(sp):
            sp.dma_start(out[0:(W - 1) * P, :].rearrange("(w p) d -> p w d", p=P),
                         k.x[:, 0:W - 1, :]).then_inc(stored, 16)
            sp.dma_start(out[(W - 1) * P:N, :], k.x[0:TAIL, W - 1, :]).then_inc(stored, 16)
            sp.wait_ge(stored, 32)


def build(nc, x, src, dst, edge_type_8, node_vec1, *rest, upto=99):
    weights, out = rest[:-1], rest[-1]
    with ExitStack() as ctx:
        k = allocate(nc, ctx)
        prepare(nc, k, x, src, dst, edge_type_8, node_vec1)
        count_edges(nc, k)
        if upto <= 2:
            return
        with ExitStack() as own:
            allocate_convolution(nc, own, k)
            for n, (a, b) in enumerate((weights[0:2], weights[2:4])):
                turn_nodes(nc, k, k.z if n else k.x, ACT.Relu, f"c{n}t")
                conv_features(nc, k, a, b, f"c{n}f")
                conv_sums(nc, k, n == 0, f"c{n}s")
                conv_result(nc, k, f"c{n}r")
            add_and_norm(nc, k, 2.0, "n0")
        if upto <= 3:
            return
        k.clear_semaphores()
        with ExitStack() as own:
            allocate_edges(nc, own, k)
            turn_nodes(nc, k, k.x, ACT.Copy, "et")
            edge_features(nc, k, weights[4], weights[5])
            edge_maxima(nc, k, weights[6], weights[7])
            add_and_norm(nc, k, 1.0, "n1")
        if upto <= 4:
            return
        k.clear_semaphores()
        with ExitStack() as own:
            allocate_attention(nc, own, k)
            for n in range(2):
                turn_nodes(nc, k, k.z if n else k.x, ACT.Copy, f"a{n}t")
                attention_features(nc, k, *weights[8 + 8 * n:16 + 8 * n], f"a{n}f")
                attention(nc, k, f"a{n}s")
                if upto <= 5:
                    return
            add_and_norm(nc, k, 1.0, "n2")
        if upto <= 6:
            return
        k.clear_semaphores()
        weight, root, bias = weights[24:27]
        for n in range(2):
            turn_nodes(nc, k, k.z if n else k.x, ACT.Copy, f"r{n}t")
            relation_features(nc, k, weight[n], root[n], bias[n], f"r{n}f")
            relation_sums(nc, k, f"r{n}s")
            if upto <= 7:
                return
        add_and_norm(nc, k, 1.0, "n3")
        store_nodes(nc, k, out)


UPTO = 99
_INS = ['x', 'src', 'dst', 'edge_type_8', 'node_vec1', 'L0_gnn_W1_out', 'L0_gnn_W1_back', 'L0_gnn_W2_out',
        'L0_gnn_W2_back', 'L1_gnn_W1', 'L1_gnn_b1', 'L1_gnn_W2', 'L1_gnn_b2', 'L2_gnn_l1_wq', 'L2_gnn_l1_bq',
        'L2_gnn_l1_wk', 'L2_gnn_l1_bk', 'L2_gnn_l1_wv', 'L2_gnn_l1_bv', 'L2_gnn_l1_ws', 'L2_gnn_l1_bs',
        'L2_gnn_l2_wq', 'L2_gnn_l2_bq', 'L2_gnn_l2_wk', 'L2_gnn_l2_bk', 'L2_gnn_l2_wv', 'L2_gnn_l2_bv',
        'L2_gnn_l2_ws', 'L2_gnn_l2_bs', 'L3_gnn_weight', 'L3_gnn_root', 'L3_gnn_bias']


def kernel(**inputs):
    import numpy as _np
    import concourse.bacc as _bacc
    from concourse import mybir as _mybir
    from concourse.bass_utils import run_bass_kernel_spmd as _run

    nc = _bacc.Bacc("TRN2", target_bir_lowering=False, num_devices=1)
    arrays, args = {}, []
    for name in _INS:
        a = _np.ascontiguousarray(inputs[name])
        arrays[f"in_{name}"] = a
        args.append(nc.dram_tensor(f"in_{name}", a.shape, _mybir.dt.from_np(a.dtype), kind="ExternalInput").ap())
    args.append(nc.dram_tensor("out_0", (N, D), _mybir.dt.float32, kind="ExternalOutput").ap())
    build(nc, *args, upto=UPTO)
    r = _run(nc, [arrays], core_ids=[0])
    return r.results[0]["out_0"]
```

```python
import concourse.bass as bass
from concourse import mybir
from concourse.alu_op_type import AluOpType as ALU
from contextlib import ExitStack, contextmanager
import itertools

F32 = mybir.dt.float32
I32 = mybir.dt.int32
I16 = mybir.dt.int16
F16 = mybir.dt.float16
BF16 = mybir.dt.bfloat16
ACT = mybir.ActivationFunctionType
AX = mybir.AxisListType
ds = bass.ds

P = 128
N = 3125
E = 103125
D = 64
NREL = 8
W = -(-N // P)
NP = W * P
TAIL = N - (W - 1) * P
T = -(-E // P)
CH = -(-T // P)
NT = CH * P
FULL_T = E // P
LAST_T = E - FULL_T * P
G = 4
NO_NODE = 4000.0
CUT = 512
SLICES = [(c, min(CUT, NP - c)) for c in range(0, NP, CUT)]
BW = 3
NB = -(-W // BW)
MAXR = -(-NP // 8)
MINR = 6
NARROW = 16.0
EPS = 1e-5
NEG = -1e30


_serial = itertools.count()


class Own:

    def __init__(self, eng, sem):
        self.eng, self.sem, self.base, self.n = eng, sem, 0, 0

    def at(self, base):
        self.base, self.n = base, 0

    def did(self, ins):
        ins.then_inc(self.sem, 1)
        self.n += 1

    def wait(self):
        self.eng.wait_ge(self.sem, self.base + self.n)

    def do(self, ins):
        self.did(ins)
        self.wait()


def wait_alone(eng, sem, value, passed):
    eng.wait_ge(sem, value)
    eng.sem_inc(passed, 1)


class Kept:

    def __init__(self, nc):
        self.nc, self.sems = nc, []

    def sem(self, name):
        self.sems.append(self.nc.alloc_semaphore(name))
        return self.sems[-1]

    def clear_semaphores(self):
        self.nc.all_engine_barrier()
        self.nc.clear_and_free_semaphores(self.sems)
        self.nc.all_engine_barrier()
        self.sems = []


def allocate(nc, ctx):
    k = Kept(nc)

    def sb(name, shape, dt):
        return ctx.enter_context(nc.sbuf_tensor(name, shape, dt))

    k.ident = sb("ident", [P, P], F32)
    k.identb = sb("identb", [P, P], BF16)
    k.iota_p = sb("iota_p", [P, P], F32)
    k.wbase = sb("wbase", [P, W], F32)
    k.src_t = sb("src_t", [P, NT], F32)
    k.dst_t = sb("dst_t", [P, NT], F32)
    k.msg_row = sb("msg_row", [P, NT], I32)
    k.type_hot = sb("type_hot", [P, NT, NREL], BF16)
    k.x = sb("x", [P, W, D], F32)
    k.vec = sb("vec", [P, W], F32)
    k.cnt8 = sb("cnt8", [P, W, NREL], F32)
    k.xt = sb("xt", [D + 1, NP], F32)
    k.z = sb("z", [P, W, D], F32)
    k.uniq_b = sb("uniq_b", [P, NB, W], F32)
    k.uniq = sb("uniq", [P, W], F32)
    k.tri = sb("tri", [W, W], F32)
    k.table = nc.dram_tensor("window_table", [W, 4], I32).ap()
    k.rounds = nc.dram_tensor("neighbour_rounds", [W, 4], I32).ap()
    k.table_row = sb("table_row", [1, W, 4], I32)
    k.rounds_row = sb("rounds_row", [1, W, 4], I32)
    k.ways = nc.dram_tensor("neighbour_ways", [1, 4], I32).ap()
    k.at = nc.dram_tensor("count_rows", [W, P, NP], BF16).ap()
    k.a = nc.dram_tensor("count_panels", [W, P, W, P], BF16).ap()
    k.q = nc.dram_tensor("edge_q", [NP, 2 * D], F32).ap()
    k.h = nc.dram_tensor("rel_h", [NREL * NP, D], F32).ap()
    return k


def allocate_convolution(nc, ctx, k):
    sb = lambda n, s, d: ctx.enter_context(nc.sbuf_tensor(n, s, d))
    k.y = sb("y", [P, W, 2, D], F32)
    k.agg = sb("agg", [P, W, 2, D], F32)
    k.parts = sb("parts", [P, W, 2, 3, D], BF16)


def allocate_edges(nc, ctx, k):
    sb = lambda n, s, d: ctx.enter_context(nc.sbuf_tensor(n, s, d))
    k.p = sb("p", [P, W, 2 * D], F32)


def allocate_attention(nc, ctx, k):
    sb = lambda n, s, d: ctx.enter_context(nc.sbuf_tensor(n, s, d))
    k.q_12 = sb("q_12", [P, 2, NP], BF16)
    k.q_13 = sb("q_13", [P, 2, NP], BF16)
    k.k_11 = sb("k_11", [P, 2, NP], BF16)
    k.k_22 = sb("k_22", [P, 2, NP], BF16)
    k.k_31 = sb("k_31", [P, 2, NP], BF16)
    k.va = sb("va", [P, W, 2, D + 1], F32)


def score_products(k):
    return (k.q_12, k.k_11), (k.q_12, k.k_22), (k.q_13, k.k_31)


def prepare(nc, k, x, src, dst, edge_type, node_vec1):
    with ExitStack() as ctx:
        sb = lambda n, s, d: ctx.enter_context(nc.sbuf_tensor(n, s, d))
        sem = lambda n: k.sem(n)
        raw = [sb(f"raw{j}", [P, CH, P], I32) for j in range(3)]
        rawf = [sb(f"rawf{j}", [P, CH, P], F32) for j in range(3)]
        idt = sb("idt", [W, NT], F32)
        t_min = sb("t_min", [P, CH], F32)
        t_max = sb("t_max", [P, CH], F32)
        hit = sb("hit", [W, NT], F32)
        hit2 = sb("hit2", [W, NT], F32)
        wlo = sb("wlo", [W, 1], F32)
        whi = sb("whi", [W, 1], F32)
        bound = sb("bound", [W, 4], F32)
        back = sb("back", [W, 1], F32)
        ni = sb("ni", [W, 1], I32)
        nf = sb("nf", [W, 1], F32)
        row = sb("row", [W, 4], I32)
        typ = sb("typ", [P, NT], F32)
        rowf = sb("rowf", [P, NT], F32)
        tp = [ctx.enter_context(nc.psum_tensor(f"tp{j}", [P, 2 * CUT], F32)) for j in range(3)]
        bc = ctx.enter_context(nc.psum_tensor("bc", [W, CUT], F32))
        blank, loaded, consts, floats, turned, kept = map(
            sem, ("blank", "loaded", "consts", "floats", "turned", "kept"))
        own_v, mins, spread, taken, nits, before, tabled, stored = map(
            sem, ("prep_own", "mins", "spread", "taken", "nits", "before", "tabled", "stored"))
        pads, own_p = sem("pads"), sem("prep_own_p")
        block = ctx.enter_context(nc.Block())
        head = (CH - 1) * P * P
        full = FULL_T - (CH - 1) * P
        arrays = (src, dst, edge_type)

        @block.sync
        def _(sp):
            sp.wait_ge(blank, 5)
            for j, a in enumerate(arrays):
                sp.dma_start(raw[j][:, 0:CH - 1, :],
                             a[0:head].rearrange("(c p j) -> p c j", p=P, j=P)).then_inc(loaded, 16)
                sp.dma_start(raw[j][0:full, CH - 1, :],
                             a[head:head + full * P].rearrange("(p j) -> p j", j=P)).then_inc(loaded, 16)
                sp.dma_start(raw[j][full:full + 1, CH - 1, 0:LAST_T],
                             a[FULL_T * P:E].rearrange("(p j) -> p j", p=1)).then_inc(loaded, 16)
            sp.dma_start(k.x[:, 0:W - 1, :],
                         x[0:(W - 1) * P, :].rearrange("(w p) d -> p w d", p=P)).then_inc(loaded, 16)
            sp.dma_start(k.x[0:TAIL, W - 1, :], x[(W - 1) * P:N, :]).then_inc(loaded, 16)
            sp.dma_start(k.vec[:, 0:W - 1],
                         node_vec1[0:(W - 1) * P, :].rearrange("(w p) a -> p (w a)", p=P),
                         allow_slow_non_contiguous=True).then_inc(loaded, 16)
            sp.dma_start(k.vec[0:TAIL, W - 1:W], node_vec1[(W - 1) * P:N, :]).then_inc(loaded, 16)
            sp.wait_ge(tabled, 1)
            sp.dma_start(k.table[:, :], row[:, :]).then_inc(stored, 16)
            sp.wait_ge(stored, 16)
            sp.dma_start(k.table_row[:, :, :], k.table.rearrange("(a w) c -> a w c", a=1)).then_inc(stored, 16)
            sp.wait_ge(stored, 32)

        @block.gpsimd
        def _(pool):
            own = Own(pool, own_p)
            pool.memset(raw[0][:, CH - 1, :], 0).then_inc(blank, 1)
            pool.memset(raw[1][:, CH - 1, :], int(NO_NODE)).then_inc(blank, 1)
            pool.memset(raw[2][:, CH - 1, :], 0).then_inc(blank, 1)
            pool.memset(k.x[:, W - 1, :], 0.0).then_inc(blank, 1)
            pool.memset(k.vec[:, W - 1:W], 0.0).then_inc(blank, 1)
            own.did(pool.memset(k.ident[:, :], 0.0))
            own.did(pool.memset(k.identb[:, :], 0.0))
            own.did(pool.memset(k.tri[:, :], 1.0))
            own.wait()
            for m in (k.ident, k.identb):
                pool.affine_select(out=m[:, :], in_=m[:, :], compare_op=ALU.not_equal, fill=1.0, base=0,
                                   pattern=[[-1, P]], channel_multiplier=1).then_inc(consts, 1)
            pool.affine_select(out=k.tri[:, :], in_=k.tri[:, :], compare_op=ALU.is_gt, fill=0.0, base=0,
                               pattern=[[1, W]], channel_multiplier=-1).then_inc(consts, 1)
            pool.iota(k.iota_p[:, :], pattern=[[1, P]], base=0, channel_multiplier=0,
                      allow_small_or_imprecise_dtypes=True).then_inc(consts, 1)
            pool.iota(k.wbase[:, :], pattern=[[P, W]], base=0, channel_multiplier=0,
                      allow_small_or_imprecise_dtypes=True).then_inc(consts, 1)
            pool.iota(wlo[:, :], pattern=[[0, 1]], base=0, channel_multiplier=P,
                      allow_small_or_imprecise_dtypes=True).then_inc(consts, 1)
            pool.iota(whi[:, :], pattern=[[0, 1]], base=P - 1, channel_multiplier=P,
                      allow_small_or_imprecise_dtypes=True).then_inc(consts, 1)
            pool.iota(idt[:, :], pattern=[[1, NT]], base=0, channel_multiplier=0,
                      allow_small_or_imprecise_dtypes=True).then_inc(consts, 1)

        @block.vector
        def _(v):
            own = Own(v, own_v)
            v.wait_ge(loaded, 16 * 13)
            for j in range(3):
                v.tensor_copy(rawf[j][:, :, :], raw[j][:, :, :]).then_inc(floats, 1)
            v.wait_ge(floats, 2)
            v.tensor_reduce(t_min[:, :], rawf[1][:, :, :], AX.X, ALU.min).then_inc(mins, 1)
            v.tensor_reduce(t_max[:, :], rawf[1][:, :, :], AX.X, ALU.max).then_inc(mins, 1)
            for j, out in enumerate((k.src_t, k.dst_t, typ)):
                v.wait_ge(turned, j + 1)
                v.tensor_copy(out[:, :], tp[j][:, 0:NT]).then_inc(kept, 1)
            v.wait_ge(kept, 3)
            own.do(v.scalar_tensor_tensor(rowf[:, :], typ[:, :], float(NP), k.src_t[:, :], ALU.mult, ALU.add))
            own.did(v.tensor_copy(k.msg_row[:, :], rowf[:, :]))
            for r in range(NREL):
                own.did(v.tensor_scalar(k.type_hot[:, :, r], typ[:, :], float(r), None, ALU.is_equal))
            v.wait_ge(consts, 8)
            for c in range(2):
                cols = slice(c * CUT, min((c + 1) * CUT, NT))
                wd = cols.stop - cols.start
                v.wait_ge(spread, 1 + c)
                own.do(v.tensor_scalar(hit[:, cols], bc[:, 0:wd], whi[:, 0:1], None, ALU.is_le))
                v.sem_inc(taken, 1)
            for c in range(2):
                cols = slice(c * CUT, min((c + 1) * CUT, NT))
                wd = cols.stop - cols.start
                v.wait_ge(spread, 3 + c)
                own.do(v.tensor_scalar(hit2[:, cols], bc[:, 0:wd], wlo[:, 0:1], None, ALU.is_ge))
                v.sem_inc(taken, 1)
            own.do(v.tensor_tensor(hit[:, :], hit[:, :], hit2[:, :], ALU.mult))
            own.do(v.scalar_tensor_tensor(hit2[:, :], idt[:, :], 1.0, hit[:, :], ALU.add, ALU.mult))
            own.did(v.tensor_reduce(bound[:, 1:2], hit2[:, :], AX.X, ALU.max))
            own.do(v.scalar_tensor_tensor(hit[:, :], idt[:, :], -float(NT), hit[:, :], ALU.add, ALU.mult))
            own.do(v.tensor_reduce(bound[:, 0:1], hit[:, :], AX.X, ALU.min))
            own.do(v.tensor_scalar(bound[:, 0:1], bound[:, 0:1], float(NT), None, ALU.add))
            own.do(v.tensor_tensor(bound[:, 0:1], bound[:, 0:1], bound[:, 1:2], ALU.min))
            own.do(v.tensor_tensor(bound[:, 2:3], bound[:, 1:2], bound[:, 0:1], ALU.subtract))
            own.do(v.tensor_scalar(bound[:, 2:3], bound[:, 2:3], float(G - 1), float(3 * G - 1), ALU.add, ALU.max))
            own.do(v.tensor_copy(ni[:, :], bound[:, 2:3]))
            own.do(v.tensor_scalar(ni[:, :], ni[:, :], G.bit_length() - 1, None, ALU.arith_shift_right))
            own.do(v.tensor_copy(nf[:, :], ni[:, :]))
            v.sem_inc(nits, 1)
            own.did(v.tensor_copy(row[:, 0:1], bound[:, 0:1]))
            own.did(v.memset(row[:, 3:4], 0))
            own.do(v.tensor_scalar(back[:, :], bound[:, 0:1], -float(NT), None, ALU.add))
            own.did(v.scalar_tensor_tensor(row[:, 1:2], nf[:, :], float(G), bound[:, 0:1], ALU.mult, ALU.add))
            v.wait_ge(before, 1)
            own.do(v.scalar_tensor_tensor(row[:, 2:3], bc[:, 0:1], float(G), back[:, :],
                                          ALU.mult, ALU.subtract))
            v.sem_inc(tabled, 1)

        @block.tensor
        def _(pe):
            pe.wait_ge(consts, 1)
            for j in range(3):
                pe.wait_ge(floats, j + 1)
                for c in range(CH):
                    last = pe.transpose(tp[j][:, c * P:(c + 1) * P], rawf[j][:, c, :], k.ident[:, :])
                last.then_inc(turned, 1)
            pe.wait_ge(mins, 2)
            n = 0
            for t in (t_min, t_max):
                for cs in (range(0, 4), range(4, CH)):
                    if n:
                        pe.wait_ge(taken, n)
                    for c in cs:
                        o = (c - cs.start) * P
                        last = pe.matmul(bc[:, o:o + P], t[:, c:c + 1].broadcast_to([P, W]), k.ident[:, :],
                                         start=True, stop=True)
                    last.then_inc(spread, 1)
                    n += 1
            pe.wait_ge(nits, 1)
            pe.wait_ge(consts, 8)
            pe.matmul(bc[:, 0:1], k.tri[:, :], nf[:, 0:1], start=True, stop=True).then_inc(before, 1)


def load_row(eng, row, bounds):
    regs = [eng.alloc_register(f"row_{next(_serial)}") for _ in bounds]
    eng.load(regs, row)
    out = []
    for reg, (lo, hi) in zip(regs, bounds):
        kept = eng.alloc_register(f"row_{next(_serial)}")
        eng.reg_alu(kept, reg, lo, ALU.max)
        out.append(eng.snap(kept, min_val=lo, max_val=hi))
    return out


def window_tiles(eng, k, w):
    return load_row(eng, k.table_row[:, ds(w, 1), 0:3].rearrange("a w c -> a (w c)"),
                    ((0, T), (2 * G, T + 2 * G), (NT - T, NT + W * (T + 2 * G))))


def count_edges(nc, k):
    with ExitStack() as ctx:
        sb = lambda n, s, d: ctx.enter_context(nc.sbuf_tensor(n, s, d))
        sem = lambda n: k.sem(n)
        iota_s = sb("iota_s", [P, NP], F16)
        srcm = sb("srcm", [P, NT], F32)
        hot_s = sb("hot_s", [P, G, NP], BF16)
        hot_d = sb("hot_d", [P, G, P], BF16)
        rows = sb("rows", [P, 2, NP], BF16)
        table_in, passed_act = sem("cnt_table_in"), sem("cnt_passed_act")
        scratch = sb("scratch", [P, 1], F32)
        ps = ctx.enter_context(nc.psum_tensor("ps_count", [P, 8 * CUT], F32))
        passed = sem("passed")
        iota_ok, own_v, hots, used, copied, stored = map(
            sem, ("iota_ok", "cnt_own", "hots", "used", "copied", "cnt_stored"))
        block = ctx.enter_context(nc.Block())
        half = NP // 2


        @block.gpsimd
        def _(pool):
            pool.iota(iota_s[:, :], pattern=[[1, NP]], base=-half, channel_multiplier=0,
                      allow_small_or_imprecise_dtypes=True).then_inc(iota_ok, 1)

        @block.vector
        def _(v):
            own = Own(v, own_v)
            own.did(v.tensor_scalar(srcm[:, :], k.src_t[:, :], -float(half), None, ALU.add))
            own.wait()
            v.sem_inc(iota_ok, 1)
            v.sem_inc(hots, 2 * NT)
            v.wait_ge(iota_ok, 2)
            with v.Fori(0, W) as w:
                first, end, place = window_tiles(v, k, w)
                with v.Fori(first, end, G) as t0:
                    for j in range(G):
                        v.wait_ge(used, t0 + place + (j + 1))
                        t = t0 + j
                        v.tensor_scalar(hot_d[:, j, :], k.iota_p[:, :], k.wbase[:, ds(w, 1)],
                                        k.dst_t[:, ds(t, 1)], ALU.add, ALU.is_equal).then_inc(hots, 1)
                        v.tensor_scalar(hot_s[:, j, :], iota_s[:, :], srcm[:, ds(t, 1)], None,
                                        ALU.is_equal).then_inc(hots, 1)

        @block.tensor
        def _(pe):
            pe.sem_inc(used, NT + G)
            pe.wait_ge(iota_ok, 2)

            def tile(t, j, w, seq):
                fresh = w is not None
                pe.wait_ge(hots, seq)
                for n, (c, wd) in enumerate(SLICES):
                    if fresh:
                        pe.wait_ge(copied, w * len(SLICES) + n + 1)
                    pe.matmul(ps[:, c:c + wd], hot_d[:, j, :], hot_s[:, j, c:c + wd], start=fresh,
                              stop=True, skip_group_check=True)
                return pe.matmul(ps[:, NP:NP + NREL], hot_d[:, j, :], k.type_hot[:, ds(t, 1), :], start=False,
                                 stop=True, skip_group_check=True)

            with pe.Fori(0, W) as w:
                first, end, place = window_tiles(pe, k, w)
                for j in range(G):
                    last = tile(first + j, j, None if j else w, (first + place + (j + 1)) * 2)
                    last.then_inc(used, 1)
                with pe.Fori(first + G, end, G) as t0:
                    for j in range(G):
                        tile(t0 + j, j, None, (t0 + place + (j + 1)) * 2).then_inc(used, 1)

        @block.scalar
        def _(act):
            act.sem_inc(copied, len(SLICES))
            with act.Fori(0, W) as w:
                first, end, place = window_tiles(act, k, w)
                act.activation(scratch[:, :], k.ident[:, 0:1], ACT.Copy).then_inc(table_in, 1)
                wait_alone(act, table_in, w + 1, passed_act)
                act.wait_ge(used, end + place + G)
                act.wait_ge(stored, w * 16)
                for n, (c, wd) in enumerate(SLICES):
                    if n == len(SLICES) - 1:
                        act.activation(k.cnt8[:, ds(w, 1), :], ps[:, NP:NP + NREL], ACT.Copy)
                    act.activation(rows[:, ds(w % 2, 1), c:c + wd], ps[:, c:c + wd], ACT.Copy).then_inc(copied, 1)

        @block.sync
        def _(sp):
            sp.sem_inc(stored, 16)
            with sp.Fori(0, W) as w:
                sp.wait_ge(copied, (w + 2) * len(SLICES))
                sp.dma_start(k.at[ds(w, 1), :, :].rearrange("w p n -> p (w n)"),
                             rows[:, ds(w % 2, 1), :].rearrange("p a n -> p (a n)")).then_inc(stored, 16)
                wait_alone(sp, stored, w * 16 + 32, passed)


def turn_nodes(nc, k, source, func, name):
    with ExitStack() as ctx:
        sem = lambda n: k.sem(n)
        ps = ctx.enter_context(nc.psum_tensor(f"{name}_ps", [D, 7 * CUT], F32))
        turned, copied = sem(f"{name}_turned"), sem(f"{name}_copied")
        block = ctx.enter_context(nc.Block())

        @block.tensor
        def _(pe):
            for s, (c, wd) in enumerate(SLICES):
                for j in range(wd // P):
                    w = c // P + j
                    last = pe.transpose(ps[:, w * P:(w + 1) * P], source[:, w, :], k.ident[:, :])
                last.then_inc(turned, 1)

        @block.scalar
        def _(act):
            for s, (c, wd) in enumerate(SLICES):
                act.wait_ge(turned, s + 1)
                act.activation(k.xt[0:D, c:c + wd], ps[:, c:c + wd], func).then_inc(copied, 1)

        @block.vector
        def _(v):
            v.memset(k.xt[D:D + 1, :], 1.0)


def conv_features(nc, k, w_out, w_back, name):
    with ExitStack() as ctx:
        sb = lambda n, s, d: ctx.enter_context(nc.sbuf_tensor(f"{name}_{n}", s, d))
        sem = lambda n: k.sem(f"{name}_{n}")
        wt = sb("wt", [D, 2 * D], F32)
        stats = sb("stats", [D, len(SLICES), 6], F32)
        mv = sb("mv", [D, 2], F32)
        eps = sb("eps", [D, 1], F32)
        std = sb("std", [D, 1], F32)
        scale = sb("scale", [D, 2], F32)
        rest = sb("rest", [P, W * 2 * D], F32)
        ps = ctx.enter_context(nc.psum_tensor(f"{name}_ps", [P, 7 * CUT], F32))
        loaded, own_v, var_ok, std_ok, normed, products, copied = map(
            sem, ("loaded", "own", "var_ok", "std_ok", "normed", "products", "copied"))
        block = ctx.enter_context(nc.Block())

        @block.sync
        def _(sp):
            sp.dma_start(wt[:, 0:D], w_out[:, :]).then_inc(loaded, 16)
            sp.dma_start(wt[:, D:2 * D], w_back[:, :]).then_inc(loaded, 16)

        @block.vector
        def _(v):
            own = Own(v, own_v)
            for s, (c, wd) in enumerate(SLICES):
                own.did(v.bn_stats(stats[:, s, :], k.xt[0:D, c:min(c + wd, N)]))
            own.did(v.memset(eps[:, :], EPS))
            own.wait()
            own.do(v.bn_aggr(mv[:, :], stats[:, :, :].rearrange("p a b -> p (a b)")))
            v.sem_inc(var_ok, 1)
            v.wait_ge(std_ok, 1)
            own.do(v.reciprocal(scale[:, 0:1], std[:, :]))
            own.do(v.scalar_tensor_tensor(scale[:, 1:2], mv[:, 0:1], -1.0, scale[:, 0:1], ALU.mult, ALU.mult))
            v.tensor_scalar(k.xt[0:D, :], k.xt[0:D, :], scale[:, 0:1], scale[:, 1:2],
                            ALU.mult, ALU.add).then_inc(normed, 1)
            v.wait_ge(copied, len(SLICES))
            y = k.y[:, :, :, :].rearrange("p w c d -> p w (c d)")
            left = y
            r = rest[:, :].rearrange("p (w d) -> p w d", w=W)
            for part in range(3):
                for c in range(2):
                    own.did(v.tensor_copy(k.parts[:, :, c, part, :], left[:, :, c * D:(c + 1) * D]))
                own.wait()
                if part < 2:
                    for c in range(2):
                        own.did(v.tensor_tensor(r[:, :, c * D:(c + 1) * D], left[:, :, c * D:(c + 1) * D],
                                                k.parts[:, :, c, part, :], ALU.subtract))
                    own.wait()
                    left = r

        @block.scalar
        def _(act):
            act.wait_ge(var_ok, 1)
            act.activation(std[:, :], mv[:, 1:2], ACT.Sqrt, bias=eps[:, 0:1]).then_inc(std_ok, 1)
            for s, (c, wd) in enumerate(SLICES):
                act.wait_ge(products, s + 1)
                act.activation(k.y[:, c // P:(c + wd) // P, :, :].rearrange("p w c d -> p (w c d)"),
                               ps[:, c:c + wd], ACT.Copy).then_inc(copied, 1)

        @block.tensor
        def _(pe):
            pe.wait_ge(loaded, 32)
            pe.wait_ge(normed, 1)
            for s, (c, wd) in enumerate(SLICES):
                for j in range(wd // P):
                    o = c + j * P
                    last = pe.matmul(ps[:, o:o + P], k.xt[0:D, o:o + P], wt[:, :], start=True, stop=True)
                last.then_inc(products, 1)


def conv_sums(nc, k, first, name):
    with ExitStack() as ctx:
        sb = lambda n, s, d: ctx.enter_context(nc.sbuf_tensor(f"{name}_{n}", s, d))
        sem = lambda n: k.sem(f"{name}_{n}")
        rows = [sb(f"rows{u}", [P, NP], BF16) for u in range(2)]
        panel = [sb(f"panel{u}", [P, W, P], BF16) for u in range(2)]
        edge = sb("edge", [P, W, P], BF16)
        seen = sb("seen", [P, W], F32)
        zero = sb("zero", [P, CUT], BF16)
        by_src = ctx.enter_context(nc.psum_tensor(f"{name}_src", [P, 4 * CUT], F32))
        by_dst = [ctx.enter_context(nc.psum_tensor(f"{name}_dst{u}", [P, CUT], F32)) for u in range(2)]
        tps = [ctx.enter_context(nc.psum_tensor(f"{name}_t{u}", [P, 2 * CUT], BF16)) for u in range(2)]
        blank = sem("blank")
        rows_in = [sem(f"rows_in{u}") for u in range(2)]
        panel_in = [sem(f"panel_in{u}") for u in range(2)]
        panel_out = [sem(f"panel_out{u}") for u in range(2)]
        turned, copied, own_v, summed, read, panel_free = map(
            sem, ("turned", "copied", "own", "summed", "read", "panel_free"))
        block = ctx.enter_context(nc.Block())
        GRP = [(b, min(8, W - b)) for b in range(0, W, 8)]
        NG = len(GRP)

        def windows(eng, body):
            with eng.Fori(0, W - 1, 2) as w:
                body(w, 0)
                body(w + 1, 1)
            body(W - 1, 0)

        @block.sync
        def _(sp):
            def load(w, u):
                sp.wait_ge(summed, w + 1)
                sp.dma_start(rows[u][:, :], k.at[ds(w, 1), :, :].rearrange("w p n -> p (w n)")
                             ).then_inc(rows_in[u], 16)
                if not first:
                    sp.dma_start(panel[u][:, :, :], k.a[ds(w, 1), :, :, :].rearrange("w p k d -> p (w k) d")
                                 ).then_inc(panel_in[u], 16)
            windows(sp, load)

        @block.tensor
        def _(pe):
            pe.sem_inc(summed, 2)
            pe.wait_ge(blank, 1)
            for b in range(4):
                pe.matmul(by_src[:, b * CUT:(b + 1) * CUT], zero[:, 0:P], zero[:, :], start=True, stop=True,
                          skip_group_check=True)

            def window(w, u):
                pe.wait_ge(rows_in[u], (w - u) * 8 + 16)

                def turn(g):
                    b, n = GRP[g]
                    pe.wait_ge(copied, w * NG + g + 1)
                    for j in range(n):
                        last = pe.transpose(tps[g % 2][:, j * P:(j + 1) * P],
                                            rows[u][:, (b + j) * P:(b + j + 1) * P], k.identb[:, :])
                    last.then_inc(turned, 1)

                def back(blocks):
                    for b in blocks:
                        for part in range(3):
                            last = pe.matmul(by_src[:, b * D:(b + 1) * D], rows[u][:, b * P:(b + 1) * P],
                                             k.parts[:, ds(w, 1), 1, part, :], start=False, stop=True,
                                             skip_group_check=True)
                    return last

                cuts = [0, 7, 14, 20, W]
                for g in range(NG):
                    if first:
                        turn(g)
                    back(range(cuts[g], cuts[g + 1]))
                if first:
                    pe.wait_ge(copied, (w + 1) * NG + 2)
                else:
                    pe.wait_ge(panel_in[u], (w - u) * 8 + 16)
                pe.wait_ge(read, w + 1)
                for b in range(W):
                    last = pe.matmul(by_dst[u][:, 0:3 * D], panel[u][:, b, :],
                                     k.parts[:, b, 0, :, :].rearrange("p a d -> p (a d)"),
                                     start=(b == 0), stop=(b == W - 1))
                last.then_inc(summed, 1)
            windows(pe, window)

        @block.scalar
        def _(act):
            if not first:
                return
            act.sem_inc(copied, 2)
            for u in range(2):
                act.sem_inc(panel_out[u], 16)

            def window(w, u):
                act.wait_ge(panel_out[u], (w - u) * 8 + 16)
                act.wait_ge(summed, w + 1)
                act.wait_ge(panel_free, w + 1)
                for g, (b, n) in enumerate(GRP):
                    act.wait_ge(turned, w * NG + g + 1)
                    act.activation(panel[u][:, b:b + n, :].rearrange("p a d -> p (a d)"),
                                   tps[g % 2][:, 0:n * P], ACT.Copy).then_inc(copied, 1)
                act.wait_ge(copied, (w + 1) * NG + 2)
                act.dma_start(k.a[ds(w, 1), :, :, :].rearrange("w p k d -> p (w k) d"),
                              panel[u][:, :, :]).then_inc(panel_out[u], 16)
            windows(act, window)
            act.wait_ge(panel_out[0], 16 * (W // 2 + 2))
            act.wait_ge(panel_out[1], 16 * (W // 2 + 1))

        @block.vector
        def _(v):
            own = Own(v, own_v)
            if first:
                own.did(v.memset(k.uniq_b[:, :, :], 0.0))
            own.did(v.memset(zero[:, :], 0.0))
            own.wait()
            v.sem_inc(blank, 1)
            v.sem_inc(read, 2)
            v.sem_inc(panel_free, 2)
            begun = own.n
            steps = 4 if first else 1

            def window(w, u):
                own.at(w * steps + begun)
                if first:
                    v.wait_ge(copied, (w + 1) * NG + 2)
                    own.did(v.tensor_scalar(edge[:, :, :], panel[u][:, :, :], 1.0, None, ALU.min))
                    own.wait()
                    v.sem_inc(panel_free, 1)
                    own.do(v.tensor_reduce(seen[:, :], edge[:, :, :], AX.X, ALU.add))
                    block_ = k.uniq_b[:, ds(w // BW, 1), :].rearrange("p b w -> p (b w)")
                    own.do(v.tensor_tensor(block_, block_, seen[:, :], ALU.add))
                v.wait_ge(summed, w + 3)
                own.do(v.tensor_reduce(k.agg[:, ds(w, 1), 0, :],
                                       by_dst[u][:, 0:3 * D].rearrange("p (a d) -> p d a", a=3), AX.X, ALU.add))
                v.sem_inc(read, 1)
            windows(v, window)
            v.wait_ge(summed, W + 2)
            v.tensor_copy(k.agg[:, :, 1, :], by_src[:, 0:W * D].rearrange("p (w d) -> p w d", w=W)).then_inc(read, 1)


def conv_result(nc, k, name):
    with ExitStack() as ctx:
        sb = lambda n, s, d: ctx.enter_context(nc.sbuf_tensor(f"{name}_{n}", s, d))
        sem = lambda n: k.sem(f"{name}_{n}")
        deg = sb("deg", [P, W], F32)
        root = sb("root", [P, W], F32)
        norm = sb("norm", [P, W], F32)
        own_v, deg_ok, root_ok = map(sem, ("own", "deg_ok", "root_ok"))
        block = ctx.enter_context(nc.Block())

        @block.vector
        def _(v):
            own = Own(v, own_v)
            own.do(v.tensor_reduce(deg[:, :], k.cnt8[:, :, :], AX.X, ALU.add))
            own.do(v.tensor_scalar(deg[:, :], deg[:, :], 1.0, None, ALU.max))
            v.sem_inc(deg_ok, 1)
            own.do(v.tensor_tensor(k.agg[:, :, :, :], k.agg[:, :, :, :], k.y[:, :, :, :], ALU.add))
            v.wait_ge(root_ok, 1)
            own.do(v.reciprocal(norm[:, :], root[:, :]))
            for c, by in enumerate((norm, k.vec)):
                own.did(v.tensor_tensor(k.agg[:, :, c, :], k.agg[:, :, c, :],
                                        by[:, :].unsqueeze(2).broadcast_to([P, W, D]), ALU.mult))
            own.wait()
            own.do(v.tensor_tensor(k.z[:, :, :], k.agg[:, :, 0, :], k.agg[:, :, 1, :], ALU.add))

        @block.scalar
        def _(act):
            act.wait_ge(deg_ok, 1)
            act.activation(root[:, :], deg[:, :], ACT.Sqrt).then_inc(root_ok, 1)


def add_and_norm(nc, k, scale, name):
    with ExitStack() as ctx:
        sb = lambda n, s, d: ctx.enter_context(nc.sbuf_tensor(f"{name}_{n}", s, d))
        sem = lambda n: k.sem(f"{name}_{n}")
        mean = sb("mean", [P, W], F32)
        var = sb("var", [P, W], F32)
        sq = sb("sq", [P, W, D], F32)
        eps = sb("eps", [P, 1], F32)
        own_v, var_ok, std_ok = map(sem, ("own", "var_ok", "std_ok"))
        block = ctx.enter_context(nc.Block())
        wide = lambda t: t[:, :].unsqueeze(2).broadcast_to([P, W, D])

        @block.vector
        def _(v):
            own = Own(v, own_v)
            own.did(v.memset(eps[:, :], EPS))
            own.do(v.scalar_tensor_tensor(k.x[:, :, :], k.x[:, :, :], float(scale), k.z[:, :, :],
                                          ALU.mult, ALU.add))
            own.do(v.tensor_reduce(mean[:, :], k.x[:, :, :], AX.X, ALU.add))
            own.do(v.tensor_scalar(mean[:, :], mean[:, :], 1.0 / D, None, ALU.mult))
            own.do(v.tensor_tensor(k.x[:, :, :], k.x[:, :, :], wide(mean), ALU.subtract))
            own.do(v.tensor_tensor(sq[:, :, :], k.x[:, :, :], k.x[:, :, :], ALU.mult))
            own.do(v.tensor_reduce(var[:, :], sq[:, :, :], AX.X, ALU.add))
            v.sem_inc(var_ok, 1)
            v.wait_ge(std_ok, 1)
            own.do(v.reciprocal(var[:, :], var[:, :]))
            own.do(v.tensor_tensor(k.x[:, :, :], k.x[:, :, :], wide(var), ALU.mult))

        @block.scalar
        def _(act):
            act.wait_ge(var_ok, 1)
            act.activation(var[:, :], var[:, :], ACT.Sqrt, bias=eps[:, 0:1], scale=1.0 / D).then_inc(std_ok, 1)


def edge_features(nc, k, w1, b1):
    with ExitStack() as ctx:
        sb = lambda n, s, d: ctx.enter_context(nc.sbuf_tensor(f"ef_{n}", s, d))
        sem = lambda n: k.sem(f"ef_{n}")
        wt = sb("wt", [D + 1, 2, 2 * D], F32)
        qs = sb("qs", [P, W, 2 * D], F32)
        most = sb("most", [P, 1], F32)
        top = sb("top", [1, 1], F32)
        way = sb("way", [1, 4], I32)
        need = sb("need", [W, 1], F32)
        whole = sb("whole", [W, 1], I32)
        rounds = sb("rounds", [W, 1], F32)
        count = sb("count", [W, 1], F32)
        row = sb("row", [W, 4], I32)
        ps = [ctx.enter_context(nc.psum_tensor(f"ef_ps{u}", [P, CUT], F32)) for u in range(4)]
        pt = [ctx.enter_context(nc.psum_tensor(f"ef_pt{u}", [W, CUT], F32)) for u in range(3)]
        loaded, own_v, wt_ok, most_ok, most_t, products, kept, rounds_ok, before, row_ok, stored = map(
            sem, ("loaded", "own", "wt_ok", "most_ok", "most_t", "products", "kept", "rounds_ok", "before",
                  "row_ok", "stored"))
        block = ctx.enter_context(nc.Block())
        H = 2 * D
        PAIRS = [(w, min(2, W - w)) for w in range(0, W, 2)]

        @block.sync
        def _(sp):
            sp.dma_start(wt[0:D, 0, :], w1[0:D, :]).then_inc(loaded, 16)
            sp.dma_start(wt[0:D, 1, :], w1[D:2 * D, :]).then_inc(loaded, 16)
            sp.dma_start(wt[D:D + 1, 0, :], b1.rearrange("(a n) -> a n", a=1)).then_inc(loaded, 16)
            sp.wait_ge(row_ok, 1)
            sp.dma_start(k.rounds[:, :], row[:, :]).then_inc(stored, 16)
            sp.wait_ge(stored, 16)
            sp.dma_start(k.rounds_row[:, :, :], k.rounds.rearrange("(a w) c -> a w c", a=1)).then_inc(stored, 16)
            sp.dma_start(k.ways[:, :], way[:, :]).then_inc(stored, 16)
            sp.wait_ge(kept, len(PAIRS))
            sp.dma_start(k.q.rearrange("(w p) h -> p w h", p=P), qs[:, :, :]).then_inc(stored, 16)
            sp.wait_ge(stored, 64)

        @block.vector
        def _(v):
            own = Own(v, own_v)
            own.did(v.memset(wt[D:D + 1, 1, :], 0.0))
            own.did(v.memset(row[:, 2:4], 0))
            own.did(v.memset(way[:, 2:4], 0))
            own.did(v.tensor_reduce(k.uniq[:, :], k.uniq_b[:, :, :].rearrange("p b w -> p w b"), AX.X, ALU.add))
            own.do(v.tensor_reduce(most[:, :], k.uniq_b[:, :, :].rearrange("p b w -> p (b w)"), AX.X, ALU.max))
            v.sem_inc(most_ok, 1)
            v.wait_ge(loaded, 48)
            own.do(v.tensor_tensor(wt[0:D, 0, :], wt[0:D, 0, :], wt[0:D, 1, :], ALU.subtract))
            v.sem_inc(wt_ok, 1)
            v.wait_ge(most_t, 1)
            own.do(v.tensor_reduce(need[:, :], pt[0][:, 0:P], AX.X, ALU.max))
            own.do(v.tensor_scalar(need[:, :], need[:, :], 7.0, float(8 * MINR), ALU.add, ALU.max))
            own.do(v.tensor_copy(whole[:, :], need[:, :]))
            own.do(v.tensor_scalar(whole[:, :], whole[:, :], 3, None, ALU.arith_shift_right))
            own.do(v.tensor_copy(rounds[:, :], whole[:, :]))
            v.sem_inc(rounds_ok, 1)
            own.do(v.tensor_reduce(top[:, :], pt[1][0:1, 0:P], AX.X, ALU.max))
            own.did(v.tensor_scalar(way[:, 0:1], top[:, :], NARROW, None, ALU.is_le))
            own.did(v.tensor_scalar(way[:, 1:2], top[:, :], NARROW, None, ALU.is_gt))
            v.wait_ge(before, 1)
            own.did(v.tensor_copy(row[:, 1:2], pt[2][:, 0:1]))
            own.do(v.tensor_tensor(count[:, :], pt[2][:, 0:1], rounds[:, :], ALU.add))
            own.do(v.tensor_copy(whole[:, :], count[:, :]))
            own.do(v.tensor_scalar(whole[:, :], whole[:, :], 1, None, ALU.arith_shift_right))
            own.do(v.tensor_copy(need[:, :], whole[:, :]))
            own.do(v.scalar_tensor_tensor(count[:, :], need[:, :], -2.0, count[:, :], ALU.mult, ALU.add))
            own.do(v.tensor_tensor(count[:, :], count[:, :], k.ident[0:W, W - 1:W], ALU.mult))
            own.do(v.tensor_tensor(row[:, 0:1], rounds[:, :], count[:, :], ALU.add))
            v.sem_inc(row_ok, 1)

        @block.tensor
        def _(pe):
            pe.wait_ge(most_ok, 1)
            pe.transpose(pt[0][:, 0:P], k.uniq[:, :], k.ident[:, :])
            pe.transpose(pt[1][0:1, 0:P], most[:, :], k.ident[:, :]).then_inc(most_t, 1)
            pe.wait_ge(rounds_ok, 1)
            pe.matmul(pt[2][:, 0:1], k.tri[:, :], rounds[:, :], start=True, stop=True).then_inc(before, 1)
            pe.wait_ge(wt_ok, 1)
            for n, (w, m) in enumerate(PAIRS):
                if n >= 4:
                    pe.wait_ge(kept, n - 3)
                for j in range(m):
                    last = pe.matmul(ps[n % 4][:, j * 2 * H:(j + 1) * 2 * H],
                                     k.xt[:, (w + j) * P:(w + j + 1) * P],
                                     wt[:, :, :].rearrange("p a h -> p (a h)"), start=True, stop=True)
                last.then_inc(products, 1)

        @block.scalar
        def _(act):
            for n, (w, m) in enumerate(PAIRS):
                act.wait_ge(products, n + 1)
                both = ps[n % 4][:, 0:m * 2 * H].rearrange("p (j a h) -> p j a h", j=m, a=2)
                act.activation(k.p[:, w:w + m, :], both[:, :, 0, :], ACT.Copy)
                act.activation(qs[:, w:w + m, :], both[:, :, 1, :], ACT.Copy).then_inc(kept, 1)


def edge_maxima(nc, k, w2, b2, narrow):
    with ExitStack() as ctx:
        name = "en" if narrow else "ew"
        sb = lambda n, s, d: ctx.enter_context(nc.sbuf_tensor(f"{name}_{n}", s, d))
        sem = lambda n: k.sem(f"{name}_{n}")
        H = 2 * D
        F = 4
        SLOTS = 4
        RING = 2 * MAXR
        BLOCKS = [(c, min(BW * P, NP - c)) for c in range(0, NP, BW * P)]
        THIRD = -(-NB // 3)
        CW = 16 * NB if narrow else NP
        place = sb("place", [P, NP], I16)
        raw = sb("raw", [P, 2, NP], BF16)
        left = sb("left", [P, NP], I16)
        cand = sb("cand", [P, CW], F32) if narrow else left
        work = sb("work", [P, CW], F32 if narrow else I16)
        top = sb("top", [P, 8], F32)
        first = sb("first", [P, W], F32)
        none = sb("none", [P, 8], F32)
        idx = sb("idx", [P, RING, 8], I32)
        now = [sb(f"now{u}", [P, F], I32) for u in range(SLOTS)]
        got = sb("got", [P, SLOTS, F, H], F32)
        hid = [sb(f"hid{u}", [P, F * P], F32) for u in range(2)]
        w2s = sb("w2s", [P, D], F32)
        b2s = sb("b2s", [P, D], F32)
        best = sb("best", [P, D], F32)
        red = sb("red", [P, 2, D], F32)
        has = sb("has", [P, W], F32)
        tps = [ctx.enter_context(nc.psum_tensor(f"{name}_t{u}", [P, F * P], F32)) for u in range(2)]
        ops = [ctx.enter_context(nc.psum_tensor(f"{name}_o{u}", [P, CUT], F32)) for u in range(2)]
        consts, found, raw_free, own_v, own_x, own_y, arrived, added, taken, now_ok, lined = map(
            sem, ("consts", "found", "raw_free", "own", "own_x", "own_y", "arrived", "added", "taken",
                  "now_ok", "lined"))
        gat = [sem(f"gat{u}") for u in range(SLOTS)]
        raw_in = sem("raw_in")
        outs = [sem(f"outs{u}") for u in range(2)]
        read = [sem(f"read{u}") for u in range(2)]
        passed = [sem(f"passed{e}") for e in range(4)]
        block = ctx.enter_context(nc.Block())

        def once(eng):
            at = 0 if narrow else 1
            return eng.If(eng.value_load(k.ways[0:1, at:at + 1], min_val=0, max_val=1) > 0)

        def window_rounds(eng, w):
            return load_row(eng, k.rounds_row[:, ds(w, 1), 0:2].rearrange("a w c -> a (w c)"), ((MINR, MAXR + 1), (0, W * (MAXR + 1))))

        def all_rounds(eng):
            rounds, before = window_rounds(eng, W - 1)
            return rounds + before

        @block.sync
        def _(sp):
            with once(sp):
                sp.dma_start(w2s[:, :], w2[:, :]).then_inc(consts, 16)
                sp.dma_start(b2s[:, :], b2.rearrange("(a n) -> a n", a=1).broadcast_to([P, D])
                             ).then_inc(consts, 16)
                with sp.Fori(0, W) as w:
                    sp.wait_ge(raw_free, w + 1)
                    sp.dma_start(raw[:, ds(w % 2, 1), :].rearrange("p u (a d) -> p (u a) d", d=P),
                                 k.a[:, :, ds(w, 1), :].rearrange("a p k d -> p a (k d)")).then_inc(raw_in, 16)
                    wait_alone(sp, raw_in, w * 16 + 16, passed[3])

        @block.gpsimd
        def _(pool):
            with once(pool):
                pool.iota(place[:, :], pattern=[[-1, NP]], base=NP, channel_multiplier=0,
                          allow_small_or_imprecise_dtypes=True).then_inc(consts, 1)
                pool.sem_inc(taken, SLOTS)
                numbers = idx[:, :, :].rearrange("p (n u) e -> p n u e", u=2)
                with pool.Fori(0, all_rounds(pool), 2) as g:

                    def lay(i):
                        if i % 2 == 0:
                            wait_alone(pool, found, g + i // 2 + 1, passed[0])
                        wait_alone(pool, taken, g * 2 + i + 1, passed[0])
                        o = i % 2 * F
                        pool.tensor_copy(now[i][:, :], numbers[:, ds(g // 2 % (RING // 2), 1), i // 2, o:o + F]
                                         .rearrange("p a e -> p (a e)")).then_inc(now_ok, 1)
                    lay(0)
                    for i in range(SLOTS):
                        if i + 1 < SLOTS:
                            lay(i + 1)
                        wait_alone(pool, now_ok, g * 2 + i + 1, passed[0])
                        for j in range(F):
                            pool.indirect_dma_start(
                                out=got[:, i, j, :], out_offset=None, in_=k.q[:, :],
                                in_offset=bass.IndirectOffsetOnAxis(ap=now[i][:, j:j + 1], axis=0)
                            ).then_inc(gat[i], 16)

        @block.vector
        def _(v):
            with once(v):
                for u in range(2):
                    v.sem_inc(read[u], 1)
                v.sem_inc(raw_free, 2)
                v.sem_inc(own_v, 8)
                own, x, y = Own(v, own_v), Own(v, own_x), Own(v, own_y)
                own.at(8)
                own.did(v.memset(first[:, :], 1.0))
                own.did(v.tensor_scalar(has[:, :], k.uniq[:, :], 0.0, None, ALU.is_gt))
                wait_alone(v, own_v, own.base + own.n, passed[1])
                v.wait_ge(consts, 33)
                begun = own.base + own.n

                def search(w, piece):
                    part, third = piece // 3, piece % 3
                    blocks = range(third * THIRD, min(NB, (third + 1) * THIRD))
                    y.at(w * (3 + 3 * NB))
                    y.n = 3 + (part - 1) * NB + blocks.start if part else third
                    if part == 0:
                        cols = slice(blocks.start * BW * P, min(NP, blocks.stop * BW * P))
                        v.wait_ge(raw_in, (w + 1) * 16)
                        y.did(v.scalar_tensor_tensor(left[:, cols],
                                                     raw[:, ds(w % 2, 1), cols].rearrange("p a c -> p (a c)"), 0.0,
                                                     place[:, cols], ALU.is_gt, ALU.mult))
                        wait_alone(v, own_y, y.base + y.n, passed[1])
                        if third == 2:
                            v.sem_inc(raw_free, 1)
                            if not narrow:
                                v.sem_inc(own_y, 3 * NB)
                        return
                    if not narrow:
                        return
                    v.sem_inc(passed[1], 1)
                    for b in blocks:
                        c, wd = BLOCKS[b]
                        row = left[:, c:c + wd]
                        if part == 2:
                            eighth = cand[:, b * 8 + 7:b * 8 + 8]
                            y.did(v.scalar_tensor_tensor(row, row, eighth, row, ALU.is_lt, ALU.mult))
                        else:
                            o = (part // 2 * NB + b) * 8
                            y.did(v.max(cand[:, o:o + 8], row))
                    wait_alone(v, own_y, y.base + y.n, passed[1])
                PIECES = 12

                def take(w, g):
                    x.at(g * 6 + w)
                    x.did(v.tensor_copy(work[:, :], cand[:, :]))
                    wait_alone(v, own_x, x.base + x.n, passed[1])

                def find(w, g):
                    x.at(g * 6 + w + 1)
                    these = work[:, :]
                    v.sem_inc(passed[1], 1)
                    one = first[:, ds(w, 1)]
                    x.do(v.max(top[:, :], these))
                    x.did(v.scalar_tensor_tensor(these, these, top[:, 7:8], these, ALU.is_lt, ALU.mult))
                    x.did(v.tensor_tensor(one, one, top[:, 0:1], ALU.max))
                    x.do(v.tensor_scalar(none[:, :], top[:, :], 0.0, None, ALU.is_equal))
                    x.do(v.scalar_tensor_tensor(none[:, :], none[:, :], one, top[:, :], ALU.mult, ALU.add))
                    x.do(v.tensor_scalar(idx[:, ds(g % RING, 1), :].rearrange("p a e -> p (a e)"), none[:, :],
                                         -1.0, float(NP), ALU.mult, ALU.add))
                    v.sem_inc(found, 1)

                def add(w, g, half):
                    v.wait_ge(arrived, g * 2 + half + 1)
                    rows = got[:, ds(g % 2 * 2 + half, 1), :, :].rearrange("p a k h -> p (a k) h")
                    v.tensor_tensor(rows, rows, k.p[:, ds(w, 1), :].broadcast_to([P, F, H]),
                                    ALU.add).then_inc(added, 1)

                def reduce(w, g, half):
                    own.at(g * 4 + w * 3 + (begun + 1 - 4))
                    own.n = half * 2
                    v.wait_ge(outs[half], g + 1)
                    own.do(v.tensor_reduce(red[:, half, :], ops[half][:, 0:F * D].rearrange("p (k d) -> p d k", k=F),
                                           AX.X, ALU.max))
                    v.sem_inc(read[half], 1)
                    own.do(v.tensor_tensor(best[:, :], best[:, :], red[:, half, :], ALU.max))

                def open_(w, g):
                    own.at(g * 4 + w * 3 + begun)
                    own.did(v.memset(best[:, :], -3.0e38))
                    wait_alone(v, own_v, own.base + own.n, passed[1])

                def close(w, g):
                    own.at(g * 4 + w * 3 + (begun + 1))
                    own.do(v.tensor_tensor(best[:, :], best[:, :], b2s[:, :], ALU.add))
                    own.did(v.tensor_scalar(k.z[:, ds(w, 1), :].rearrange("p a d -> p (a d)"), best[:, :],
                                            has[:, ds(w, 1)], None, ALU.mult))
                    wait_alone(v, own_v, own.base + own.n, passed[1])

                @contextmanager
                def loop(a, b):
                    with v.If(b > a):
                        with v.Fori(a, b) as r:
                            yield r

                def window(w, before, following, after):
                    rounds, start = window_rounds(v, w)
                    if following:
                        next_rounds, next_start = window_rounds(v, w + 1)

                    def round_(r, find_too, last_of_before):
                        g = v.snap(start + r)
                        if find_too and isinstance(r, int) and r == 0:
                            take(w + 1, next_start)
                        if find_too:
                            find(w + 1, v.snap(next_start + r))
                        for half in range(2):
                            add(w, g, half)
                            if last_of_before is None:
                                reduce(w, g, half)
                            elif last_of_before is not False:
                                reduce(last_of_before, g, half)
                            if after and isinstance(r, int):
                                search(w + 2, 2 * r + half)
                        if last_of_before is not None:
                            if last_of_before is not False:
                                close(last_of_before, g)
                            open_(w, g)
                        v.sem_inc(passed[1], 1)
                    for r in range(MINR):
                        round_(r, following, (False if before is None else before) if r == 0 else None)
                    if following:
                        fewer = v.alloc_register(f"fewer_{next(_serial)}")
                        v.reg_alu(fewer, rounds, next_rounds, ALU.min)
                        both = v.snap(fewer, min_val=MINR, max_val=MAXR + 1)
                        with loop(MINR, both) as r:
                            round_(r, True, None)
                        with loop(both, rounds) as r:
                            round_(r, False, None)
                        with loop(both, next_rounds) as r:
                            find(w + 1, v.snap(next_start + r))
                    else:
                        with loop(MINR, rounds) as r:
                            round_(r, False, None)

                for piece in range(PIECES):
                    search(0, piece)
                take(0, 0)
                rounds, _ = window_rounds(v, 0)
                with v.Fori(0, rounds) as r:
                    find(0, r)
                for piece in range(PIECES):
                    search(1, piece)
                window(0, None, True, True)
                with v.Fori(1, W - 2) as w:
                    window(w, w - 1, True, True)
                window(W - 2, W - 3, True, False)
                window(W - 1, W - 2, False, False)
                total = v.snap(all_rounds(v))
                for half in range(2):
                    reduce(W - 1, total, half)
                close(W - 1, total)

        @block.tensor
        def _(pe):
            with once(pe):
                pe.sem_inc(outs[0], 1)
                pe.sem_inc(outs[1], 1)
                pe.wait_ge(consts, 33)
                with pe.Fori(0, all_rounds(pe), 2) as g:

                    def turn(i):
                        pe.wait_ge(added, g * 2 + i + 1)
                        pe.wait_ge(lined, g * 2 + i + 1)
                        for j in range(F):
                            last = pe.transpose(tps[i % 2][:, j * P:(j + 1) * P], got[:, i, j, :], k.ident[:, :])
                        last.then_inc(taken, 1)

                    def multiply(i):
                        pe.wait_ge(lined, g * 2 + i + 3)
                        pe.wait_ge(read[i % 2], g + i // 2 + 1)
                        for j in range(F):
                            last = pe.matmul(ops[i % 2][:, j * D:(j + 1) * D], hid[i % 2][:, j * P:(j + 1) * P],
                                             w2s[:, :], start=True, stop=True, skip_group_check=True)
                        last.then_inc(outs[i % 2], 1)
                    turn(0)
                    turn(1)
                    multiply(0)
                    turn(2)
                    multiply(1)
                    turn(3)
                    multiply(2)
                    multiply(3)

        @block.scalar
        def _(act):
            with once(act):
                act.sem_inc(lined, 2)
                gathered = act.alloc_register(f"{name}_gathered")
                act.reg_mov(gathered, 16 * F)
                with act.Fori(0, all_rounds(act), 2) as g:
                    here = act.snap(gathered, min_val=16 * F)

                    def arrive(i):
                        act.wait_ge(gat[i], here)
                        act.sem_inc(arrived, 1)

                    def line(i):
                        act.wait_ge(taken, g * 2 + i + 1 + SLOTS)
                        act.wait_ge(outs[i % 2], g + i // 2 + 1)
                        act.activation(hid[i % 2][:, :], tps[i % 2][:, :], ACT.Relu).then_inc(lined, 1)
                    arrive(0)
                    arrive(1)
                    line(0)
                    arrive(2)
                    line(1)
                    arrive(3)
                    line(2)
                    line(3)
                    act.reg_add(gathered, gathered, 16 * F)


def attention_features(nc, k, wq, bq, wk, bk, wv, bv, ws, bs, name):
    with ExitStack() as ctx:
        sb = lambda n, s, d: ctx.enter_context(nc.sbuf_tensor(f"{name}_{n}", s, d))
        sem = lambda n: k.sem(f"{name}_{n}")
        H = 2 * D
        wqk = sb("wqk", [D + 1, 2, 2, 2, D], F32)
        wvs = sb("wvs", [D + 1, H + D], F32)
        rest = [sb(f"rest{u}", [P, CUT], F32) for u in range(2)]
        ps = [ctx.enter_context(nc.psum_tensor(f"{name}_ps{u}", [P, CUT], F32)) for u in range(8)]
        loaded, products, copied, first, second, less, split = map(
            sem, ("loaded", "products", "copied", "first", "second", "less", "split"))
        block = ctx.enter_context(nc.Block())
        row = lambda b: b.rearrange("(a n) -> a n", a=1)
        heads = lambda m: m.rearrange("p (h d) -> p h d", h=2)
        QK = [(t, h, c, wd) for t in range(2) for h in range(2) for c, wd in SLICES]
        VS = [(w, min(2, W - w)) for w in range(0, W, 2)]
        KV = H + D
        NQK = len(QK)

        def free(eng, n):
            if n >= 8:
                if n - 8 < NQK:
                    eng.wait_ge(less, n - 7)
                else:
                    eng.wait_ge(copied, n - 8 - NQK + 1)

        @block.sync
        def _(sp):
            for u in range(2):
                for t, (m, b) in enumerate(((wq, bq), (wk, bk))):
                    sp.dma_start(wqk[0:D, t, :, u, :], heads(m[:, :])).then_inc(loaded, 16)
                    sp.dma_start(wqk[D:D + 1, t, :, u, :], heads(row(b))).then_inc(loaded, 16)
            for dst, src in ((wvs[0:D, 0:H], wv[:, :]), (wvs[D:D + 1, 0:H], row(bv)),
                             (wvs[0:D, H:KV], ws[:, :]), (wvs[D:D + 1, H:KV], row(bs))):
                sp.dma_start(dst, src).then_inc(loaded, 16)

        @block.tensor
        def _(pe):
            pe.wait_ge(loaded, 16 * 12)
            n = 0
            for t, h, c, wd in QK:
                free(pe, n)
                pe.matmul(ps[n % 8][:, 0:wd], wqk[:, t, h, :, :].rearrange("p u d -> p (u d)"), k.xt[:, c:c + wd],
                          start=True, stop=True).then_inc(products, 1)
                n += 1
            for w, m in VS:
                free(pe, n)
                for j in range(m):
                    last = pe.matmul(ps[n % 8][:, j * KV:(j + 1) * KV], k.xt[:, (w + j) * P:(w + j + 1) * P],
                                     wvs[:, :], start=True, stop=True)
                last.then_inc(products, 1)
                n += 1

        @block.scalar
        def _(act):
            def second_part(n):
                t, h, c, wd = QK[n]
                act.wait_ge(less, n + 1)
                lo = 0 if t else D
                out = k.k_22 if t else k.q_12
                act.activation(out[lo:P, h, c:c + wd], rest[n % 2][lo:P, 0:wd], ACT.Copy).then_inc(second, 1)

            for n, (t, h, c, wd) in enumerate(QK):
                act.wait_ge(products, n + 1)
                act.activation((k.k_11 if t else k.q_12)[:, h, c:c + wd], ps[n % 8][:, 0:wd], ACT.Copy,
                               scale=1.0 if t else D ** -0.5).then_inc(first, 1)
                if n >= 1:
                    second_part(n - 1)
            second_part(NQK - 1)
            for i, (w, m) in enumerate(VS):
                n = NQK + i
                act.wait_ge(products, n + 1)
                both = ps[n % 8][:, 0:m * KV].rearrange("p (j c) -> p j c", j=m)
                for h in range(2):
                    act.activation(k.va[:, w:w + m, h, 0:D], both[:, :, h * D:(h + 1) * D], ACT.Copy)
                act.activation(k.z[:, w:w + m, :], both[:, :, H:KV], ACT.Copy).then_inc(copied, 1)

        @block.vector
        def _(v):
            v.memset(k.va[:, :, :, D:D + 1], 1.0)

            def remainder(n):
                t, h, c, wd = QK[n]
                v.wait_ge(first, n + 1)
                if n >= 2:
                    v.wait_ge(split, n - 1)
                v.scalar_tensor_tensor(rest[n % 2][:, 0:wd], ps[n % 8][:, 0:wd], 1.0 if t else D ** -0.5,
                                       (k.k_11 if t else k.q_12)[:, h, c:c + wd],
                                       ALU.mult, ALU.subtract).then_inc(less, 1)

            def third_part(n):
                t, h, c, wd = QK[n]
                v.wait_ge(second, n + 1)
                own, other = (slice(0, D), slice(D, P)) if t else (slice(D, P), slice(0, D))
                third, one = (k.k_31, k.k_11) if t else (k.q_13, k.q_12)
                two = k.k_22 if t else k.q_12
                v.tensor_copy(third[other, h, c:c + wd], one[other, h, c:c + wd])
                v.tensor_tensor(third[own, h, c:c + wd], rest[n % 2][own, 0:wd], two[own, h, c:c + wd],
                                ALU.subtract).then_inc(split, 1)

            for n in range(NQK):
                remainder(n)
                if n >= 1:
                    third_part(n - 1)
            third_part(NQK - 1)


def attention(nc, k, name):
    with ExitStack() as ctx:
        sb = lambda n, s, d: ctx.enter_context(nc.sbuf_tensor(f"{name}_{n}", s, d))
        sem = lambda n: k.sem(f"{name}_{n}")
        rows = sb("rows", [P, NP], BF16)
        no_row = [sb(f"no_row{u}", [P, NP], BF16) for u in range(2)]
        panel = [sb(f"panel{u}", [P, W * P], BF16) for u in range(2)]
        ones = sb("ones", [3, P], BF16)
        parts = sb("parts", [P, 3, 2], BF16)
        rest = sb("rest", [P, 2], F32)
        mrow = [sb(f"mrow{u}", [3, 2, P], BF16) for u in range(2)]
        seen = [sb(f"seen{u}", [P, CUT], F32) for u in range(2)]
        most = sb("most", [P, 2, len(SLICES)], F32)
        top = sb("top", [P, 2], F32)
        some = sb("some", [P, 2], F32)
        GRP = [(b, min(4, W - b)) for b in range(0, W, 4)]
        ex = [sb(f"ex{u}", [P, 4 * P], F32) for u in range(2)]
        exc = [sb(f"exc{u}", [P, 4 * P], F32) for u in range(2)]
        den = sb("den", [P, 2], F32)
        sps = [ctx.enter_context(nc.psum_tensor(f"{name}_s{u}", [P, CUT], F32)) for u in range(2)]
        tps = [ctx.enter_context(nc.psum_tensor(f"{name}_t{u}", [P, CUT], F32)) for u in range(2)]
        mps = ctx.enter_context(nc.psum_tensor(f"{name}_m", [P, CUT], F32))
        ops = [ctx.enter_context(nc.psum_tensor(f"{name}_o{u}", [P, CUT], F32)) for u in range(2)]
        rows_in, own_v, masked, scored, veiled, maxed, top_ok, top_t, m_ok = map(
            sem, ("rows_in", "own", "masked", "scored", "veiled", "maxed", "top_ok", "top_t", "m_ok"))
        panel_in = [sem(f"panel_in{u}") for u in range(2)]
        shifted, expd, weighed, summed, done = map(sem, ("shifted", "expd", "weighed", "summed", "done"))
        block = ctx.enter_context(nc.Block())
        PART = [(h, c, wd) for h in range(2) for c, wd in SLICES]
        UNIT = [(h, b, n) for h in range(2) for b, n in GRP]
        NPT, NU = len(PART), len(UNIT)
        BESIDE = [[i for i in range(NPT) if i * (NU - 2) // NPT == g] for g in range(NU)]

        def windows(eng, body):
            with eng.Fori(0, W - 3, 2) as w:
                body(w, 0, True, True)
                body(w + 1, 1, True, True)
            body(W - 3, 0, True, True)
            body(W - 2, 1, True, False)
            body(W - 1, 0, False, False)

        @block.sync
        def _(sp):
            def load_rows(w):
                sp.dma_start(rows[:, :], k.at[ds(w, 1), :, :].rearrange("w p n -> p (w n)")).then_inc(rows_in, 16)

            def load_panel(w, u):
                sp.dma_start(panel[u][:, :], k.a[ds(w, 1), :, :, :].rearrange("w p k d -> p (w k d)")
                             ).then_inc(panel_in[u], 16)

            load_rows(0)
            load_panel(0, 0)
            load_panel(1, 1)
            sp.wait_ge(masked, 1)
            load_rows(1)

            def load(w, u, following, after):
                if after:
                    sp.wait_ge(masked, w + 2)
                    load_rows(w + 2)
                    sp.wait_ge(done, w + 3)
                    load_panel(w + 2, u)
            windows(sp, load)

        @block.scalar
        def _(act):
            def maxima(w, u):
                act.wait_ge(top_t, w + 1)
                act.activation(mrow[u][:, :, :], mps[0:3, 0:2 * P].rearrange("p (h d) -> p h d", h=2),
                               ACT.Copy).then_inc(m_ok, 1)

            maxima(0, 0)

            def window(w, u, following, after):
                for i, (h, b, n) in enumerate(UNIT):
                    act.wait_ge(shifted, w * NU + i + 1)
                    act.wait_ge(weighed, w * NU + i + 1)
                    act.activation(ex[i % 2][:, 0:n * P], tps[i % 2][:, 0:n * P], ACT.Exp).then_inc(expd, 1)
                    if i == NU - 2 and following:
                        maxima(w + 1, 1 - u)
            windows(act, window)

        @block.tensor
        def _(pe):
            def score(w, u, i):
                h, c, wd = PART[i]
                pe.wait_ge(veiled, w * NPT + i + 1)
                for n, (q, key) in enumerate(score_products(k)):
                    last = pe.matmul(sps[i % 2][:, 0:wd], q[:, h, ds(w * P, P)], key[:, h, c:c + wd],
                                     start=(n == 0), stop=(n == 2))
                last.then_inc(scored, 1)

            def turn_top(w):
                pe.wait_ge(top_ok, w + 1)
                for h in range(2):
                    last = pe.matmul(mps[0:3, h * P:(h + 1) * P], parts[:, :, h], k.identb[:, :],
                                     start=(h == 0), stop=True, skip_group_check=True)
                last.then_inc(top_t, 1)

            def shift(w, u, i):
                h, b, n = UNIT[i]
                if i == 0:
                    pe.wait_ge(m_ok, w + 1)
                pe.wait_ge(expd, w * NU + i + 1)
                pe.matmul(tps[i % 2][:, 0:n * P], ones[:, :], mrow[u][:, h, :].unsqueeze(1).broadcast_to([3, n, P]),
                          start=True, stop=True, skip_group_check=True)
                for j in range(n):
                    for q, key in score_products(k):
                        last = pe.matmul(tps[i % 2][:, j * P:(j + 1) * P], key[:, h, (b + j) * P:(b + j + 1) * P],
                                         q[:, h, ds(w * P, P)], start=False, stop=True, skip_group_check=True)
                last.then_inc(shifted, 1)

            def sum_up(w, u, i):
                h, b, n = UNIT[i]
                pe.wait_ge(weighed, w * NU + i + 3)
                if i == 0:
                    pe.wait_ge(done, w + 1)
                for j in range(n):
                    last = pe.matmul(ops[u][:, h * 2 * D:h * 2 * D + D + 1], exc[i % 2][:, j * P:(j + 1) * P],
                                     k.va[:, b + j, h, :], start=(i == 0 and j == 0),
                                     stop=True, skip_group_check=True)
                last.then_inc(summed, 1)

            for i in range(NPT):
                score(0, 0, i)
            turn_top(0)

            def window(w, u, following, after):
                for i in range(NU):
                    if following:
                        for part in BESIDE[i]:
                            score(w + 1, 1 - u, part)
                    shift(w, u, i)
                    if i >= 2:
                        sum_up(w, u, i - 2)
                    if i == NU - 2 and following:
                        turn_top(w + 1)
                sum_up(w, u, NU - 2)
                sum_up(w, u, NU - 1)
            windows(pe, window)

        @block.vector
        def _(v):
            for s in (done, expd, weighed, summed, veiled, maxed):
                v.sem_inc(s, 2)
            own = Own(v, own_v)

            def mask(w, u):
                v.wait_ge(rows_in, (w + 1) * 16)
                v.tensor_scalar(no_row[u][:, :], rows[:, :], 0.0, NEG, ALU.is_equal, ALU.mult).then_inc(masked, 1)

            def veil(w, u, i):
                h, c, wd = PART[i]
                if i == 0:
                    v.wait_ge(masked, w + 1)
                v.wait_ge(maxed, w * NPT + i + 1)
                v.wait_ge(scored, w * NPT + i + 1)
                v.tensor_tensor(seen[i % 2][:, 0:wd], sps[i % 2][:, 0:wd], no_row[u][:, c:c + wd],
                                ALU.add).then_inc(veiled, 1)

            def part_max(w, i):
                h, c, wd = PART[i]
                v.wait_ge(veiled, w * NPT + i + 3)
                v.tensor_reduce(most[:, h, i % len(SLICES):i % len(SLICES) + 1], seen[i % 2][:, 0:wd],
                                AX.X, ALU.max).then_inc(maxed, 1)

            def find_top(w):
                v.wait_ge(maxed, (w + 1) * NPT + 2)
                own.do(v.tensor_reduce(top[:, :], most[:, :, :], AX.X, ALU.max))
                own.do(v.tensor_scalar(some[:, :], top[:, :], NEG / 2, None, ALU.is_gt))
                own.do(v.scalar_tensor_tensor(top[:, :], top[:, :], -1.0, some[:, :], ALU.mult, ALU.mult))
                own.do(v.tensor_copy(parts[:, 0, :], top[:, :]))
                own.do(v.tensor_tensor(rest[:, :], top[:, :], parts[:, 0, :], ALU.subtract))
                own.do(v.tensor_copy(parts[:, 1, :], rest[:, :]))
                own.do(v.tensor_tensor(parts[:, 2, :], rest[:, :], parts[:, 1, :], ALU.subtract))
                v.sem_inc(top_ok, 1)
            TOP = 7

            def weigh(w, u, i):
                h, b, n = UNIT[i]
                if i == 0:
                    v.wait_ge(panel_in[u], (w - u) * 8 + 16)
                v.wait_ge(expd, w * NU + i + 3)
                v.wait_ge(summed, w * NU + i + 1)
                v.scalar_tensor_tensor(exc[i % 2][:, 0:n * P], ex[i % 2][:, 0:n * P], 1.0,
                                       panel[u][:, b * P:(b + n) * P], ALU.min, ALU.mult).then_inc(weighed, 1)

            def finish(w, u):
                v.wait_ge(summed, (w + 1) * NU + 2)
                own.do(v.tensor_scalar(den[:, :], ops[u][:, 0:4 * D].rearrange("p (h c) -> p h c", h=2)[:, :, D],
                                       1e-16, 2.0, ALU.add, ALU.mult))
                own.do(v.reciprocal(den[:, :], den[:, :]))
                for h in range(2):
                    z = k.z[:, ds(w, 1), :].rearrange("p a d -> p (a d)")
                    own.do(v.scalar_tensor_tensor(z, ops[u][:, h * 2 * D:h * 2 * D + D], den[:, h:h + 1], z,
                                                  ALU.mult, ALU.add))
                v.sem_inc(done, 1)
            FINISH = 4

            v.memset(ones[:, :], 1.0)
            mask(0, 0)
            mask(1, 1)
            for i in range(NPT):
                veil(0, 0, i)
                if i >= 1:
                    part_max(0, i - 1)
            part_max(0, NPT - 1)
            find_top(0)

            def window(w, u, following, after):
                own.at(TOP + w * (TOP + FINISH))
                for i in range(NU):
                    beside = BESIDE[i] if following else []
                    for part in beside:
                        veil(w + 1, 1 - u, part)
                    if following and i == NU - 2:
                        find_top(w + 1)
                    weigh(w, u, i)
                    for part in beside:
                        part_max(w + 1, part)
                    if i == 3 and after:
                        mask(w + 2, u)
                finish(w, u)
            windows(v, window)


def relation_features(nc, k, weight, root, bias, name):
    with ExitStack() as ctx:
        sb = lambda n, s, d: ctx.enter_context(nc.sbuf_tensor(f"{name}_{n}", s, d))
        sem = lambda n: k.sem(f"{name}_{n}")
        wt = sb("wt", [D + 1, NREL + 1, D], F32)
        hs = [sb(f"hs{u}", [P, NREL, D], F32) for u in range(4)]
        ps = [ctx.enter_context(nc.psum_tensor(f"{name}_ps{u}", [P, CUT], F32)) for u in range(6)]
        rs = [ctx.enter_context(nc.psum_tensor(f"{name}_rs{u}", [P, CUT], F32)) for u in range(2)]
        loaded, blank, products, kept, rooted = map(sem, ("loaded", "blank", "products", "kept", "rooted"))
        stored = [sem(f"stored{u}") for u in range(4)]
        block = ctx.enter_context(nc.Block())

        @block.sync
        def _(sp):
            sp.dma_start(wt[0:D, 0:NREL, :], weight.rearrange("r d f -> d r f")).then_inc(loaded, 16)
            sp.dma_start(wt[0:D, NREL, :], root[:, :]).then_inc(loaded, 16)
            sp.dma_start(wt[D:D + 1, NREL, :], bias.rearrange("(a n) -> a n", a=1)).then_inc(loaded, 16)
            table = k.h.rearrange("(r w p) d -> w p r d", r=NREL, p=P)
            for w in range(W):
                sp.wait_ge(kept, w + 1)
                sp.dma_start(table[w], hs[w % 4][:, :, :]).then_inc(stored[w % 4], 16)
            for u in range(4):
                sp.wait_ge(stored[u], 16 * len(range(u, W, 4)))

        @block.vector
        def _(v):
            v.memset(wt[D:D + 1, 0:NREL, :], 0.0).then_inc(blank, 1)
            for w in range(W):
                v.wait_ge(rooted, w + 1)
                v.tensor_copy(k.z[:, w, :], rs[w % 2][:, 0:D]).then_inc(blank, 1)

        @block.tensor
        def _(pe):
            pe.wait_ge(loaded, 48)
            pe.wait_ge(blank, 1)
            for w in range(W):
                if w >= 6:
                    pe.wait_ge(kept, w - 5)
                if w >= 2:
                    pe.wait_ge(blank, w)
                at = k.xt[:, w * P:(w + 1) * P]
                pe.matmul(ps[w % 6][:, :], at, wt[:, 0:NREL, :].rearrange("p r d -> p (r d)"),
                          start=True, stop=True).then_inc(products, 1)
                pe.matmul(rs[w % 2][:, 0:D], at, wt[:, NREL, :], start=True, stop=True).then_inc(rooted, 1)

        @block.scalar
        def _(act):
            for w in range(W):
                act.wait_ge(products, w + 1)
                if w >= 4:
                    act.wait_ge(stored[w % 4], 16 * (w // 4))
                act.activation(hs[w % 4][:, :, :].rearrange("p r d -> p (r d)"), ps[w % 6][:, :],
                               ACT.Copy).then_inc(kept, 1)


def relation_sums(nc, k, name):
    with ExitStack() as ctx:
        sb = lambda n, s, d: ctx.enter_context(nc.sbuf_tensor(f"{name}_{n}", s, d))
        sem = lambda n: k.sem(f"{name}_{n}")
        SLOTS = 2 * G
        now = sb("now", [P, SLOTS], I32)
        got = sb("got", [P, SLOTS, D], F32)
        here = sb("here", [P, P], F32)
        hot = sb("hot", [P, G, P], F32)
        typed = [sb(f"typed{j}", [P, NREL, D], F32) for j in range(G)]
        inv = sb("inv", [P, W, NREL], F32)
        mean = sb("mean", [P, NREL, D], F32)
        total = sb("total", [P, D], F32)
        ps = ctx.enter_context(nc.psum_tensor(f"{name}_ps", [P, 2, CUT], F32))
        gat = [sem(f"gat{j}") for j in range(SLOTS)]
        passed = [sem(f"passed{e}") for e in range(3)]
        now_ok, arrived, spread, multiplied, read, own_v = map(
            sem, ("now_ok", "arrived", "spread", "multiplied", "read", "own"))
        block = ctx.enter_context(nc.Block())

        def last_place(eng):
            _, end, place = window_tiles(eng, k, W - 1)
            return end + place

        @block.scalar
        def _(act):
            act.sem_inc(now_ok, NT)
            with act.Fori(0, W) as w:
                first, end, place = window_tiles(act, k, w)
                with act.Fori(first, end, G) as t0:
                    at = act.snap(t0 + place)
                    half = act.snap(at // G % 2)
                    for j in range(G):
                        act.wait_ge(arrived, at + j + 1)
                        act.activation(now[:, ds(half * G + j, 1)], k.msg_row[:, ds(t0 + j, 1)],
                                       ACT.Copy).then_inc(now_ok, 1)
            wait_alone(act, arrived, last_place(act) + SLOTS, passed[1])
            act.sem_inc(now_ok, SLOTS)

        @block.gpsimd
        def _(pool):
            with pool.Fori(NT, last_place(pool), SLOTS) as n:
                for j in range(SLOTS):
                    wait_alone(pool, spread, n + j + 1, passed[0])
                    wait_alone(pool, now_ok, n + j + 1, passed[0])
                    pool.indirect_dma_start(
                        out=got[:, j, :], out_offset=None, in_=k.h[:, :],
                        in_offset=bass.IndirectOffsetOnAxis(ap=now[:, j:j + 1], axis=0)).then_inc(gat[j], 16)

        @block.sync
        def _(sp):
            sp.sem_inc(arrived, NT + SLOTS)
            gathered = sp.alloc_register(f"{name}_gathered")
            sp.reg_mov(gathered, 16)
            with sp.Fori(NT, last_place(sp), SLOTS) as n:
                here_ = sp.snap(gathered, min_val=16)
                for j in range(SLOTS):
                    sp.wait_ge(gat[j], here_)
                    sp.sem_inc(arrived, 1)
                sp.reg_add(gathered, gathered, 16)

        @block.vector
        def _(v):
            v.sem_inc(spread, NT + SLOTS)
            own = Own(v, own_v)
            own.do(v.tensor_scalar(inv[:, :, :], k.cnt8[:, :, :], 1.0, None, ALU.max))
            own.do(v.reciprocal(inv[:, :, :], inv[:, :, :]))
            begun = own.n

            def tiles(t0, place):
                at = v.snap(t0 + place)
                half = v.snap(at // G % 2)
                for j in range(G):
                    if j % 2 == 0:
                        v.wait_ge(multiplied, at + j + 2)
                        v.tensor_tensor(hot[:, j:j + 2, :], here[:, :].unsqueeze(1).broadcast_to([P, 2, P]),
                                        k.dst_t[:, ds(t0 + j, 2)].unsqueeze(2).broadcast_to([P, 2, P]),
                                        ALU.is_equal)
                    v.wait_ge(arrived, at + j + 1 + SLOTS)
                    v.tensor_tensor(typed[j][:, :, :],
                                    got[:, ds(half * G + j, 1), :].broadcast_to([P, NREL, D]),
                                    k.type_hot[:, ds(t0 + j, 1), :].rearrange("p a r -> p (a r)")
                                    .unsqueeze(2).broadcast_to([P, NREL, D]), ALU.mult).then_inc(spread, 1)

            def finish(w, end_place, opened):
                v.wait_ge(multiplied, end_place + G)
                own.at(w * 4 + (begun + 1 + opened))
                own.do(v.tensor_tensor(mean[:, :, :],
                                       ps[:, ds(w % 2, 1), :].rearrange("p a (r d) -> p (a r) d", r=NREL),
                                       inv[:, ds(w, 1), :].rearrange("p a r -> p (a r)")
                                       .unsqueeze(2).broadcast_to([P, NREL, D]), ALU.mult))
                v.sem_inc(read, 1)
                own.do(v.tensor_reduce(total[:, :], mean[:, :, :].rearrange("p r d -> p d r"), AX.X, ALU.add))
                z = k.z[:, ds(w, 1), :].rearrange("p a d -> p (a d)")
                own.did(v.tensor_tensor(z, z, total[:, :], ALU.add))
                wait_alone(v, own_v, own.base + own.n, passed[2])

            def window(w, finish_before):
                first, end, place = window_tiles(v, k, w)
                if finish_before:
                    v.wait_ge(spread, first + place + SLOTS)
                own.at(w * 4 + (begun if not finish_before else begun - 3))
                own.did(v.tensor_scalar(here[:, :], k.iota_p[:, :], k.wbase[:, ds(w, 1)], None, ALU.add))
                wait_alone(v, own_v, own.base + own.n, passed[2])
                tiles(first, place)
                if finish_before:
                    finish(w - 1, first + place, 1)
                with v.Fori(first + G, end, G) as t0:
                    tiles(t0, place)
                return end + place

            window(0, False)
            with v.Fori(1, W - 1) as w:
                window(w, True)
            complete = window(W - 1, True)
            finish(W - 1, complete, 0)

        @block.tensor
        def _(pe):
            pe.sem_inc(multiplied, NT + G)
            pe.sem_inc(read, 2)

            def tiles(w, at, fresh):
                for j in range(G):
                    pe.wait_ge(spread, at + j + 1 + SLOTS)
                    pe.matmul(ps[:, ds(w % 2, 1), :].rearrange("p a c -> p (a c)"), hot[:, j, :],
                              typed[j][:, :, :].rearrange("p r d -> p (r d)"),
                              start=fresh and j == 0, stop=True, skip_group_check=True).then_inc(multiplied, 1)

            with pe.Fori(0, W) as w:
                first, end, place = window_tiles(pe, k, w)
                pe.wait_ge(read, w + 1)
                tiles(w, pe.snap(first + place), True)
                with pe.Fori(first + G, end, G) as t0:
                    tiles(w, pe.snap(t0 + place), False)


def store_nodes(nc, k, out):
    with ExitStack() as ctx:
        stored = k.sem("out_stored")
        block = ctx.enter_context(nc.Block())

        @block.sync
        def _(sp):
            sp.dma_start(out[0:(W - 1) * P, :].rearrange("(w p) d -> p w d", p=P),
                         k.x[:, 0:W - 1, :]).then_inc(stored, 16)
            sp.dma_start(out[(W - 1) * P:N, :], k.x[0:TAIL, W - 1, :]).then_inc(stored, 16)
            sp.wait_ge(stored, 32)


def build(nc, x, src, dst, edge_type_8, node_vec1, *rest):
    weights, out = rest[:-1], rest[-1]
    with ExitStack() as ctx:
        k = allocate(nc, ctx)
        prepare(nc, k, x, src, dst, edge_type_8, node_vec1)
        count_edges(nc, k)
        with ExitStack() as own:
            allocate_convolution(nc, own, k)
            for n, (a, b) in enumerate((weights[0:2], weights[2:4])):
                turn_nodes(nc, k, k.z if n else k.x, ACT.Relu, f"c{n}t")
                conv_features(nc, k, a, b, f"c{n}f")
                conv_sums(nc, k, n == 0, f"c{n}s")
                conv_result(nc, k, f"c{n}r")
            add_and_norm(nc, k, 2.0, "n0")
        k.clear_semaphores()
        with ExitStack() as own:
            allocate_edges(nc, own, k)
            turn_nodes(nc, k, k.x, ACT.Copy, "et")
            edge_features(nc, k, weights[4], weights[5])
            for narrow in (True, False):
                edge_maxima(nc, k, weights[6], weights[7], narrow)
            add_and_norm(nc, k, 1.0, "n1")
        k.clear_semaphores()
        with ExitStack() as own:
            allocate_attention(nc, own, k)
            for n in range(2):
                turn_nodes(nc, k, k.z if n else k.x, ACT.Copy, f"a{n}t")
                attention_features(nc, k, *weights[8 + 8 * n:16 + 8 * n], f"a{n}f")
                attention(nc, k, f"a{n}s")
            add_and_norm(nc, k, 1.0, "n2")
        k.clear_semaphores()
        weight, root, bias = weights[24:27]
        for n in range(2):
            turn_nodes(nc, k, k.z if n else k.x, ACT.Copy, f"r{n}t")
            relation_features(nc, k, weight[n], root[n], bias[n], f"r{n}f")
            relation_sums(nc, k, f"r{n}s")
        add_and_norm(nc, k, 1.0, "n3")
        store_nodes(nc, k, out)


_INS = ['x', 'src', 'dst', 'edge_type_8', 'node_vec1', 'L0_gnn_W1_out', 'L0_gnn_W1_back', 'L0_gnn_W2_out',
        'L0_gnn_W2_back', 'L1_gnn_W1', 'L1_gnn_b1', 'L1_gnn_W2', 'L1_gnn_b2', 'L2_gnn_l1_wq', 'L2_gnn_l1_bq',
        'L2_gnn_l1_wk', 'L2_gnn_l1_bk', 'L2_gnn_l1_wv', 'L2_gnn_l1_bv', 'L2_gnn_l1_ws', 'L2_gnn_l1_bs',
        'L2_gnn_l2_wq', 'L2_gnn_l2_bq', 'L2_gnn_l2_wk', 'L2_gnn_l2_bk', 'L2_gnn_l2_wv', 'L2_gnn_l2_bv',
        'L2_gnn_l2_ws', 'L2_gnn_l2_bs', 'L3_gnn_weight', 'L3_gnn_root', 'L3_gnn_bias']


def kernel(**inputs):
    import numpy as _np
    import concourse.bacc as _bacc
    from concourse import mybir as _mybir
    from concourse.bass_utils import run_bass_kernel_spmd as _run

    nc = _bacc.Bacc("TRN2", target_bir_lowering=False, num_devices=1)
    arrays, args = {}, []
    for name in _INS:
        a = _np.ascontiguousarray(inputs[name])
        arrays[f"in_{name}"] = a
        args.append(nc.dram_tensor(f"in_{name}", a.shape, _mybir.dt.from_np(a.dtype), kind="ExternalInput").ap())
    args.append(nc.dram_tensor("out_0", (N, D), _mybir.dt.float32, kind="ExternalOutput").ap())
    build(nc, *args)
    r = _run(nc, [arrays], core_ids=[0])
    return r.results[0]["out_0"]
```
